# Optimizing a Trainium2 kernel written in Bass

```python
import numpy as np
import jax
import jax.numpy as jnp

def _softmax(x, axis=-1):
    return jax.nn.softmax(x, axis=axis)

def _gelu(x):
    return jax.nn.gelu(x, approximate=True)

def _silu(x):
    return jax.nn.silu(x)

def _sigmoid(x):
    return jax.nn.sigmoid(x)

def _layernorm(x, axis=-1, eps=1e-05):
    m = jnp.mean(x, axis=axis, keepdims=True)
    v = jnp.var(x, axis=axis, keepdims=True)
    return (x - m) / jnp.sqrt(v + eps)

def _scatter_add(tgt, idx, src, axis=0):
    return tgt.at[idx].add(src)

def _segment_sum(src, seg, n):
    return jax.ops.segment_sum(src, seg, n)
kernel_name = 'mk_gnn_preln_d2_gnn_r32_18f3a8'

def setup_inputs(seed: int=0):
    np.random.seed(seed)
    _w = jnp.asarray

    def _rec_inputs():
        import jax
        import jax.numpy as jnp
        _gk = jax.random.key(seed)
        x = -0.000202 + 1 * jax.random.normal(jax.random.fold_in(_gk, 1), (3125, 128), jnp.float32)
        _s = jax.random.randint(jax.random.fold_in(_gk, 2), (50000,), 0, 3125, jnp.int32)
        _d = jax.random.randint(jax.random.fold_in(_gk, 3), (50000,), 0, 3125, jnp.int32)
        _loop = jnp.arange(3125, dtype=jnp.int32)
        src = jnp.concatenate([_s, _d, _loop])
        dst = jnp.concatenate([_d, _s, _loop])
        _o = jnp.argsort(dst, stable=True)
        src = src[_o]
        dst = dst[_o]
        edge_attr_32 = 0.000196303 + 1.00016 * jax.random.normal(jax.random.fold_in(_gk, 11), (103125, 32), jnp.float32)
        edge_weight = jax.random.uniform(jax.random.fold_in(_gk, 13), (103125,), jnp.float32, 0.0, 5)
        return (x, src, dst, edge_attr_32, edge_weight)
    x, src, dst, edge_attr_32, edge_weight = _rec_inputs()

    def _L0_gnn_setup():
        import jax, jax.numpy as jnp
        import numpy as np
        N_NODES = 50000
        N_EDGES = 46875
        FEAT = 128
        CUTOFF = 5.0
        key = jax.random.key(seed)
        k_x, k_ei, k_el, k_w = jax.random.split(key, 4)
        x = jax.random.normal(k_x, (N_NODES, FEAT), dtype=jnp.float32)
        edge_index = jax.random.randint(k_ei, (2, N_EDGES), 0, N_NODES, dtype=jnp.int64)
        edge_len = jax.random.uniform(k_el, (N_EDGES,), dtype=jnp.float32) * CUTOFF
        W_mix = jax.random.normal(k_w, (FEAT, FEAT), dtype=jnp.float32) / np.sqrt(FEAT)
        log_scale = jnp.asarray(np.log(6.0), dtype=jnp.float32)
        filter_w = jnp.asarray(0.7, dtype=jnp.float32)
        filter_b = jnp.asarray(0.1, dtype=jnp.float32)
        return {'x': x, 'edge_index': edge_index, 'edge_len': edge_len, 'W_mix': W_mix, 'log_scale': log_scale, 'filter_w': filter_w, 'filter_b': filter_b}
    _L0_gnn_all = _L0_gnn_setup()
    _L0_gnn_in = {k: v for k, v in _L0_gnn_all.items() if k in ('W_mix', 'log_scale', 'filter_w', 'filter_b')}
    del _L0_gnn_all

    def _L1_gnn_setup():
        import jax, jax.numpy as jnp
        import numpy as np
        N, E = (50000, 25000)
        D_IN, HID, H, C, E_DIM = (128, 128, 4, 32, 32)
        key = jax.random.key(seed)
        ks = jax.random.split(key, 16)

        def lin(k, fan_in, fan_out):
            return jax.random.normal(k, (fan_in, fan_out), jnp.float32) / np.sqrt(fan_in)
        return {'x': jax.random.normal(ks[0], (N, D_IN), jnp.float32), 'edge_index': jax.random.randint(ks[1], (2, E), 0, N, jnp.int32), 'edge_attr': jax.random.normal(ks[2], (E, E_DIM), jnp.float32), 'Wq': lin(ks[3], D_IN, HID), 'bq': jnp.zeros((HID,), jnp.float32), 'Wk': lin(ks[4], D_IN, HID), 'bk': jnp.zeros((HID,), jnp.float32), 'Wv': lin(ks[5], D_IN, HID), 'bv': jnp.zeros((HID,), jnp.float32), 'We': lin(ks[6], E_DIM, HID), 'Wskip': lin(ks[7], D_IN, HID), 'bskip': jnp.zeros((HID,), jnp.float32), 'W1': lin(ks[8], HID, HID), 'b1': jnp.zeros((HID,), jnp.float32), 'W2': lin(ks[9], HID, HID), 'b2': jnp.zeros((HID,), jnp.float32)}
    _L1_gnn_all = _L1_gnn_setup()
    _L1_gnn_in = {k: v for k, v in _L1_gnn_all.items() if k in ('Wq', 'bq', 'Wk', 'bk', 'Wv', 'bv', 'We', 'Wskip', 'bskip', 'W1', 'b1', 'W2', 'b2')}
    del _L1_gnn_all
    return {'x': x, 'src': src, 'dst': dst, 'edge_attr_32': edge_attr_32, 'edge_weight': edge_weight, 'L0_gnn_W_mix': _L0_gnn_in['W_mix'], 'L0_gnn_log_scale': _L0_gnn_in['log_scale'], 'L0_gnn_filter_w': _L0_gnn_in['filter_w'], 'L0_gnn_filter_b': _L0_gnn_in['filter_b'], 'L1_gnn_Wq': _L1_gnn_in['Wq'], 'L1_gnn_bq': _L1_gnn_in['bq'], 'L1_gnn_Wk': _L1_gnn_in['Wk'], 'L1_gnn_bk': _L1_gnn_in['bk'], 'L1_gnn_Wv': _L1_gnn_in['Wv'], 'L1_gnn_bv': _L1_gnn_in['bv'], 'L1_gnn_We': _L1_gnn_in['We'], 'L1_gnn_Wskip': _L1_gnn_in['Wskip'], 'L1_gnn_bskip': _L1_gnn_in['bskip'], 'L1_gnn_W1': _L1_gnn_in['W1'], 'L1_gnn_b1': _L1_gnn_in['b1'], 'L1_gnn_W2': _L1_gnn_in['W2'], 'L1_gnn_b2': _L1_gnn_in['b2']}

def reference(x, src, dst, edge_attr_32, edge_weight, L0_gnn_W_mix, L0_gnn_log_scale, L0_gnn_filter_w, L0_gnn_filter_b, L1_gnn_Wq, L1_gnn_bq, L1_gnn_Wk, L1_gnn_bk, L1_gnn_Wv, L1_gnn_bv, L1_gnn_We, L1_gnn_Wskip, L1_gnn_bskip, L1_gnn_W1, L1_gnn_b1, L1_gnn_W2, L1_gnn_b2):
    import jax
    import jax.numpy as jnp

    def _L0_gnn_ref(x, edge_index, edge_len, W_mix, log_scale, filter_w, filter_b):
        import jax, jax.numpy as jnp
        import numpy as np
        N_NODES = 50000
        N_EDGES = 46875
        FEAT = 128
        CUTOFF = 5.0
        sender = edge_index[0]
        receiver = edge_index[1]
        n_nodes = x.shape[0]
        scale = jnp.exp(log_scale).astype(edge_len.dtype)
        decay = jnp.exp(-jnp.maximum(edge_len / (scale + 1e-06), 0.0) ** 2)
        gate = jax.nn.sigmoid(edge_len * filter_w + filter_b)
        weights = jnp.nan_to_num(decay * gate, nan=0.0, posinf=0.0, neginf=0.0)
        messages = weights[:, None].astype(x.dtype) * x[sender]
        agg = jax.ops.segment_sum(messages, receiver, num_segments=n_nodes)
        degree = jax.ops.segment_sum(jnp.ones_like(edge_len), receiver, num_segments=n_nodes)
        agg = agg / jnp.maximum(degree, 1.0)[:, None].astype(x.dtype)
        return x + agg @ W_mix

    def _L1_gnn_ref(x, edge_index, edge_attr, Wq, bq, Wk, bk, Wv, bv, We, Wskip, bskip, W1, b1, W2, b2):
        import jax, jax.numpy as jnp
        import numpy as np
        N, E = (50000, 25000)
        D_IN, HID, H, C, E_DIM = (128, 128, 4, 32, 32)
        src, dst = (edge_index[0], edge_index[1])
        n = x.shape[0]
        q = (x @ Wq + bq).reshape(n, H, C)
        k = (x @ Wk + bk).reshape(n, H, C)
        v = (x @ Wv + bv).reshape(n, H, C)
        e = (edge_attr @ We).reshape(-1, H, C)
        kj = k[src] + e
        vj = v[src] + e
        alpha = jnp.einsum('ehc,ehc->eh', q[dst], kj) / np.sqrt(C)
        amax = jax.ops.segment_max(alpha, dst, num_segments=n)
        amax = jnp.where(jnp.isfinite(amax), amax, 0.0)
        ex = jnp.exp(alpha - amax[dst])
        denom = jax.ops.segment_sum(ex, dst, num_segments=n)
        alpha = ex / (denom[dst] + 1e-16)
        agg = jax.ops.segment_sum(vj * alpha[:, :, None], dst, num_segments=n)
        out = agg.reshape(n, HID) + (x @ Wskip + bskip)
        h = jax.nn.gelu(out @ W1 + b1, approximate=True)
        h = jax.nn.gelu(h @ W2 + b2, approximate=True)
        return out + h
    edge_index = jnp.stack([src, dst])
    h = jnp.maximum(_layernorm(x, axis=-1), 0.0)
    x = x + _L0_gnn_ref(h, edge_index, edge_weight, L0_gnn_W_mix, L0_gnn_log_scale, L0_gnn_filter_w, L0_gnn_filter_b)
    h = jnp.maximum(_layernorm(x, axis=-1), 0.0)
    x = x + _L1_gnn_ref(h, edge_index, edge_attr_32, L1_gnn_Wq, L1_gnn_bq, L1_gnn_Wk, L1_gnn_bk, L1_gnn_Wv, L1_gnn_bv, L1_gnn_We, L1_gnn_Wskip, L1_gnn_bskip, L1_gnn_W1, L1_gnn_b1, L1_gnn_W2, L1_gnn_b2)
    return x

_drawn_inputs = setup_inputs


def setup_inputs(seed=0):
    import zlib

    import numpy as np

    out = dict(_drawn_inputs(seed))
    spreads = {'L1_gnn_bq': (0.0, 0.407),
     'L1_gnn_bk': (0.0, 0.8),
     'L1_gnn_bv': (0.0, 0.1),
     'L1_gnn_bskip': (0.0, 0.1),
     'L1_gnn_b1': (0.0, 0.369),
     'L1_gnn_b2': (0.0, 0.1)}
    factors = {'edge_weight': 8.0}
    for name, (base, spread) in spreads.items():
        noise = np.random.default_rng([zlib.crc32(name.encode()), seed]).standard_normal(out[name].shape)
        drawn = base * np.exp(spread * noise) if base else spread * noise
        out[name] = jnp.asarray(drawn.astype(out[name].dtype))
    for name, factor in factors.items():
        out[name] = (out[name] * factor).astype(out[name].dtype)
    return out
```

```python
import concourse.bass as bass
from concourse import mybir
from contextlib import ExitStack

P = 128
F = 128
H = 4
C = F // H
A = 32
G = 8
HALF = G // 2
BANK = 512
U = BANK // F
BIG = 1.0e30
FLT_MAX = 3.4028234e38
LN_EPS = 1e-5


def gnn_kernel(nc, x, src, dst, edge_attr, edge_weight, w_mix, log_scale, filter_w, filter_b,
               wq, bq, wk, bk, wv, bv, we, wskip, bskip, w1, b1, w2, b2, out):
    f32, bf16, i32 = mybir.dt.float32, mybir.dt.bfloat16, mybir.dt.int32
    ALU, ACT, AX = mybir.AluOpType, mybir.ActivationFunctionType, mybir.AxisListType

    N, E = x.shape[0], src.shape[0]
    NB = -(-N // P)
    NU = -(-NB // U)
    NBP = NU * U
    T = -(-E // P)
    TAIL = E - (T - 1) * P
    V = -(-(T + NB - 1) // 32) * 32
    VC = -(-V // P)
    NG = V // G
    PD = max(p for p in range(1, P + 1) if E % p == 0)
    DD = E // PD
    LINE = V * P // P
    CHUNK = 32
    NCH = V // CHUNK
    STATS = NB * P
    assert NU <= 7 and STATS + NB * H <= NU * BANK and NB <= 32 and N < 1 << 24

    edges_d = nc.dram_tensor("edges_d", (T, 3 * P), i32).ap()
    h_d = nc.dram_tensor("h_d", (NBP * P, F), f32).ap()
    kv_d = nc.dram_tensor("kv_d", (NBP * P, 2 * F), f32).ap()
    attr_d = nc.dram_tensor("attr_d", (T * A, P), f32).ap()
    v_d = nc.dram_tensor("v_d", (NG, P, G, F), f32).ap()
    key_d = nc.dram_tensor("key_d", (VC * P, P), f32).ap()
    line_d = nc.dram_tensor("line_d", (H, V * P), f32).ap()
    exp_d = nc.dram_tensor("exp_d", (H, V * P), f32).ap()
    visit_d = nc.dram_tensor("visit_d", (2, VC * P), i32).ap()

    ctx = ExitStack()
    with ctx:
        ctx.enter_context(nc.allow_non_contiguous_dma(reason="a few hundred single words"))

        def sb(name, shape, dt=f32):
            return ctx.enter_context(nc.sbuf_tensor(name, shape, dt))

        def sem(name):
            return ctx.enter_context(nc.semaphore(name))

        def sems(name, n):
            return [sem(f"{name}{k}") for k in range(n)]

        ident = sb("ident", [P, P])
        identb = sb("identb", [P, P], bf16)
        iota = sb("iota", [P, P])
        ones = sb("ones", [P, P])
        zeros = sb("zeros", [P, BANK], bf16)
        w_kvqs = sb("w_kvqs", [P, 4 * F])
        b_kvqs = sb("b_kvqs", [1, 4 * F])
        w_mix_s = sb("w_mix_s", [P, F])
        w1_s = sb("w1_s", [P, F])
        w2_s = sb("w2_s", [P, F])
        b1_s = sb("b1_s", [P, 1])
        b2_s = sb("b2_s", [1, F])
        we_s = sb("we_s", [A, F])
        gate = sb("gate", [P, 8])
        xs = sb("xs", [P, NBP, F])
        hs = sb("hs", [P, NBP, F])
        qs = sb("qs", [P, NBP, 3, F], bf16)
        slot_e = sb("slot_e", [P, VC * P])
        src_e = sb("src_e", [P, VC * P], i32)
        wgt_e = sb("wgt_e", [P, VC * P])
        visit_row = sb("visit_row", [1, 2, VC * P], i32)
        score = sb("score", [P, V, H])
        stat = sb("stat", [P, 4, NBP])
        degree = sb("degree", [P, NB])
        esum = sb("esum", [P, NB, H])

        ARENA = 15400
        arena = sb("arena", [P, ARENA])
        used = [0]

        def carve(words, dt=f32, fresh=False):
            if fresh:
                used[0] = 0
            view = arena[:, used[0]:used[0] + words]
            used[0] += words
            assert used[0] <= ARENA, used[0]
            return view if dt is f32 else view.bitcast(dt)

        edge_rows = carve(VC * 3 * P, fresh=True).rearrange("p (c n) -> p c n", c=VC)
        edge_int = edge_rows.bitcast(i32)
        dst_all = carve(DD, i32)
        below = carve(DD)
        rel = carve(VC * P).rearrange("p (c e) -> p c e", c=VC)
        fits = carve(VC * P).rearrange("p (c e) -> p c e", c=VC)
        key = carve(VC * P).rearrange("p (c e) -> p c e", c=VC)
        srcf = carve(VC * P).rearrange("p (c e) -> p c e", c=VC)
        past = carve(VC * (NB - 1)).rearrange("p (c b) -> p c b", c=VC)
        small = carve(24 * 32).rearrange("p (k b) -> p k b", b=32)
        small_i = small.bitcast(i32)
        vis = carve(8 * VC).rearrange("p (k c) -> p k c", k=8)
        vis_i = vis.bitcast(i32)
        pad_row = carve(3 * P, i32)
        centred = carve(NBP * F).rearrange("p (b f) -> p b f", b=NBP)
        squares = qs[:, :, :, :].rearrange("p b t f -> p (b t f)").bitcast(f32)[:, 0:NBP * F].rearrange("p (b f) -> p b f", b=NBP)
        decay, sig, ok = (score[:, :, :].rearrange("p v h -> p (v h)")[:, n * V:(n + 1) * V] for n in range(3))
        src_ring = carve(2 * G, i32, fresh=True).rearrange("p (k s) -> p k s", k=2)
        wgt_ring = carve(2 * G).rearrange("p (k s) -> p k s", k=2)
        h_src = carve(2 * G * F).rearrange("p (k s f) -> p k s f", k=2, s=G)
        h_wgt = carve(2 * G * F).rearrange("p (k s f) -> p k s f", k=2, s=G)
        hot0 = carve(2 * G * P).rearrange("p (k s n) -> p k s n", k=2, s=G)
        attr_in = carve(2 * 2 * P).rearrange("p (k q n) -> p k q n", k=2, q=2)
        attr_t = carve(2 * G * P).rearrange("p (k n) -> p k n", k=2)[0:A]
        rest_in = carve(16 * A).rearrange("p (t c) -> p t c", t=16)
        rest_t = carve(16 * P)[0:A]
        mean_in = carve(NBP * F, fresh=True).rearrange("p (b f) -> p b f", b=NBP)
        side = carve(2 * BANK).rearrange("p (k n) -> p k n", k=2)
        c_u = carve(2 * BANK).rearrange("p (k n) -> p k n", k=2)
        sq_u = carve(2 * BANK).rearrange("p (k n) -> p k n", k=2)
        h2_u = carve(2 * BANK).rearrange("p (k n) -> p k n", k=2)
        h2t_u = carve(2 * BANK).rearrange("p (k n) -> p k n", k=2)
        kv_u = carve(2 * U * 2 * F).rearrange("p (k c f) -> p k c f", k=2, c=U)
        q_f = carve(2 * 3 * F).rearrange("p (k t f) -> p k t f", k=2, t=3)
        src_ring1 = carve(2 * G, i32, fresh=True).rearrange("p (k s) -> p k s", k=2)
        kv_src = carve(2 * G * 2 * F).rearrange("p (k s t f) -> p k s t f", k=2, s=G, t=2)
        kv_edge = carve(2 * G * 2 * F).rearrange("p (k s t f) -> p k s t f", k=2, s=G, t=2)
        prod = carve(2 * HALF * F).rearrange("p (j n) -> p j n", j=2)
        hot_b = carve(2 * G * P // 2, bf16).rearrange("p (k s n) -> p k s n", k=2, s=G)
        hot_t = carve(2 * G * P // 2, bf16).rearrange("p (k s n) -> p k s n", k=2, s=G)
        attr_g = carve(2 * G * P).rearrange("p (k s e) -> p k s e", k=2, s=G)[0:A]
        line_rows = carve(NCH * P, fresh=True).rearrange("p (c e) -> p c e", c=NCH)
        line = carve(H * LINE).rearrange("p (h n) -> p h n", h=H)
        peak = carve(H * LINE).rearrange("p (h n) -> p h n", h=H)
        keys = carve(LINE + 2)
        apart = carve(LINE + 1)
        lead = carve(LINE)
        trail = carve(LINE)
        ends = carve(6 * P).rearrange("p (k n) -> p k n", k=6)
        ends_t = carve(8 * (P + 1)).rearrange("p (k n) -> p k n", k=8)
        v_ring = carve(4 * G * F, fresh=True).rearrange("p (k s f) -> p k s f", k=4, s=G)
        msg = carve(4 * G * F).rearrange("p (k s f) -> p k s f", k=4, s=G)
        hot1 = carve(4 * G * P).rearrange("p (k s n) -> p k s n", k=4, s=G)
        slot_ring = carve(4 * HALF).rearrange("p (k s) -> p k s", k=4)
        exp_ring = carve(4 * G * H).rearrange("p (k s h) -> p k s h", k=4, s=G)
        o_u = carve(NBP * F, fresh=True).rearrange("p (b f) -> p b f", b=NBP)
        ot_u = carve(2 * BANK).rearrange("p (k n) -> p k n", k=2)
        ht_u = carve(2 * BANK).rearrange("p (k n) -> p k n", k=2)
        g_u = carve(2 * BANK).rearrange("p (k n) -> p k n", k=2)
        r_u = carve(NB * H).rearrange("p (b h) -> p b h", h=H)

        acc = ctx.enter_context(nc.psum_tensor("acc", [P, 7 * BANK], f32))
        aside = ctx.enter_context(nc.psum_tensor("aside", [P, BANK], f32))

        def bank(b):
            return aside[:, :] if b == 7 else acc[:, b * BANK:(b + 1) * BANK]

        s_const = sem("s_const")
        s_pad = sem("s_pad")
        s_dst = sem("s_dst")
        s_x = sem("s_x")
        s_wload = sem("s_wload")
        s_gate = sem("s_gate")
        s_edges = sem("s_edges")
        s_cnt = sem("s_cnt")
        s_bound = sem("s_bound")
        s_vis = sem("s_vis")
        s_visd = sem("s_visd")
        s_visr = sem("s_visr")
        s_rows = sem("s_rows")
        s_key = sem("s_key")
        s_keyd = sem("s_keyd")
        s_tr = sem("s_tr")
        s_trc = sem("s_trc")
        s_dve = sem("s_dve")
        s_act = sem("s_act")
        s_mean = sem("s_mean")
        s_sq = sem("s_sq")
        s_var = sem("s_var")
        s_std = sem("s_std")
        s_h = sem("s_h")
        s_hd = sem("s_hd")
        s_dec = sem("s_dec")
        s_decv = sem("s_decv")
        s_wgt = sem("s_wgt")
        s_zero = sem("s_zero")
        s_src0 = sems("s_src0_", 2)
        s_wr0 = sems("s_wr0_", 2)
        s_hot0 = sems("s_hot0_", 2)
        s_gath0 = sems("s_gath0_", 2)
        s_msg0 = sems("s_msg0_", 2)
        s_acc0 = sems("s_acc0_", 2)
        s_hop_pool = sem("s_hop_pool")
        s_hop_act = sem("s_hop_act")
        s_hop_sp = sem("s_hop_sp")
        s_hop_dve = sem("s_hop_dve")
        s_hop_pe = sem("s_hop_pe")
        s_ain = sems("s_ain", 2)
        s_atr = sem("s_atr")
        s_atc = sem("s_atc")
        s_aout = sems("s_aout", 2)
        s_rin = sem("s_rin")
        s_rest = sem("s_rest")
        s_mix_in = sem("s_mix_in")
        s_n0pe = sem("s_n0pe")
        s_n0act = sem("s_n0act")
        s_n0dve = sem("s_n0dve")
        s_kvd = sems("s_kvd", 2)
        s_src1 = sems("s_src1_", 2)
        s_gath1 = sems("s_gath1_", 2)
        s_attr1 = sems("s_attr1_", 2)
        s_hot1 = sems("s_hot1_", 2)
        s_hott = sems("s_hott", 2)
        s_hotc = sems("s_hotc", 2)
        s_edge = sems("s_edge", 2)
        s_kve = sems("s_kve", 2)
        s_q = sems("s_q", 2)
        s_prod = sems("s_prod", 2)
        s_score = sems("s_score", 2)
        s_vout = sems("s_vout", 2)
        s_lt = sem("s_lt")
        s_lc = sem("s_lc")
        s_lined = sem("s_lined")
        s_line = sem("s_line")
        s_keys = sem("s_keys")
        s_ends = sem("s_ends")
        s_endt = sem("s_endt")
        s_diff = sem("s_diff")
        s_exp = sem("s_exp")
        s_expd = sem("s_expd")
        s_expr = sem("s_expr")
        s_et = sem("s_et")
        s_ec = sem("s_ec")
        s_v = sems("s_v", 4)
        s_expc = sems("s_expc", 4)
        s_msg1 = sems("s_msg1_", 4)
        s_hotp = sems("s_hotp", 4)
        s_acc1 = sems("s_acc1_", 4)
        s_n1pe = sem("s_n1pe")
        s_n1act = sem("s_n1act")
        s_n1dve = sem("s_n1dve")
        s_out = sem("s_out")

        WEIGHTS = 14
        FULL = T - 1
        QIT = (T - 1) // 16
        REST = T - 16 * QIT
        assert QIT <= NG // 2
        RESTC = -(-REST // 4)

        def numbered(steps):
            return {s: n + 1 for n, s in enumerate(steps)}

        def ahead(first, rest):
            for u in range(-1, NU):
                if u + 1 < NU:
                    yield from ((f, u + 1) for f in first)
                if u >= 0:
                    yield from ((f, u) for f in rest)

        pe0 = numbered(ahead(["mean_t", "mix"], ["h2_t"] + [f"proj{c}" for c in range(U)]))
        act0 = numbered(ahead(["side", "std"], ["h2_side"] + [f"{f}{c}" for c in range(U) for f in ("kv", "q", "skip")]))
        dve0 = numbered([("degree", 0), ("one", 0), ("rdeg", 0)] + [("mean", u) for u in range(NU)] + [("xh", 0)] + list(ahead(
            ["x1", "sum", "mu", "centre", "square", "sum2", "var", "relu", "rstd", "h2"],
            [f"{f}{c}" for c in range(U) for f in ("part0", "left1", "part1", "left2", "part2")])))
        pe1 = numbered(ahead(["o_t"], ["w1", "w2"]))
        act1 = numbered(ahead(["ot"], ["gelu1", "gelu2"]))
        dve1 = numbered([("esum", 0), ("resum", 0)] + [(f, u) for u in range(NU) for f in ("pad", "o", "skip")]
                        + [(f, u) for u in range(NU) for f in ("xo", "y")])
        LAST = len

        def table_done(eng):
            for k in range(2):
                eng.wait_ge(s_kvd[k], 16 * ((NU + 1 - k) // 2))

        def load_blocks(pe, first):
            blocks = []
            for m in (0, 4):
                blocks += nc.values_load_multi_w_load_instructions(
                    visit_row[0:1, 0, bass.ds(first + m, 4)], engines=[mybir.EngineType.PE], min_val=0, max_val=NB - 1)[1]
            return blocks

        block = ctx.enter_context(nc.Block())


        @block.sync
        def _(sp):
            sp.dma_start(dst_all[0:PD, :], dst.rearrange("(p n) -> p n", p=PD)).then_inc(s_dst, 16)
            nfull = N // P
            sp.wait_ge(s_pad, 2)
            sp.dma_start(xs[:, 0:nfull, :], x[0:nfull * P, :].rearrange("(b p) f -> p b f", p=P)).then_inc(s_x, 16)
            if N % P:
                sp.dma_start(xs[0:N % P, nfull, :], x[nfull * P:N, :]).then_inc(s_x, 16)
            else:
                sp.sem_inc(s_x, 16)
            for n, a in enumerate((src, dst, edge_weight.bitcast(i32))):
                cols = slice(n * P, n * P + P)
                sp.dma_start(edges_d[0:FULL, cols], a[0:FULL * P].rearrange("(t e) -> t e", e=P)).then_inc(s_edges, 16)
                sp.dma_start(edges_d[FULL:T, n * P:n * P + TAIL], a[FULL * P:E].rearrange("(t e) -> t e", t=1)).then_inc(s_edges, 16)
                if TAIL < P:
                    sp.dma_start(edges_d[FULL:T, n * P + TAIL:n * P + P], pad_row[0:1, n * P + TAIL:n * P + P]).then_inc(s_edges, 16)
                else:
                    sp.sem_inc(s_edges, 16)
            sp.wait_ge(s_vis, 1)
            for n in range(2):
                sp.dma_start(visit_d[n, :].rearrange("(c p) -> p c", p=P), vis_i[:, 6 + n, :]).then_inc(s_visd, 16)
            sp.wait_ge(s_visd, 32)
            sp.dma_start(visit_row[:, :, :], visit_d.rearrange("(a k) n -> a k n", a=1)).then_inc(s_visr, 16)
            sp.wait_ge(s_h, 1)
            sp.dma_start(h_d.rearrange("(b p) f -> p b f", p=P), hs[:, :, :]).then_inc(s_hd, 16)
            sp.wait_ge(s_key, 1)
            sp.dma_start(key_d.rearrange("(c p) e -> p c e", p=P), key).then_inc(s_keyd, 16)
            sp.wait_ge(s_keyd, 16)

            sp.wait_ge(s_trc, 3 * -(-VC // U))
            sp.wait_ge(s_rows, 16 * VC)
            sp.wait_ge(s_wgt, 1)
            sp.wait_ge(s_hd, 16)
            sp.wait_ge(s_visr, 16)
            attr_q = edge_attr.rearrange("e c -> (e c)")[0:16 * QIT * P * A].rearrange("(i k q p n) -> i k q p n", i=QIT, k=2, q=2, p=P)
            attr_o = attr_d[0:16 * QIT * A, :].rearrange("(g t c) e -> g c t e", t=G, c=A)
            with sp.Fori(0, QIT) as i:
                for k in range(2):
                    sp.wait_ge(s_atr, 2 * i + k)
                    sp.sem_inc(s_hop_sp, 1)
                    sp.dma_start(attr_in[:, k, :, :], attr_q[bass.ds(i, 1), k].rearrange("i q p n -> p (i q) n")).then_inc(s_ain[k], 16)
                for k in range(2):
                    sp.wait_ge(s_atc, 2 * i + k + 1)
                    sp.sem_inc(s_hop_sp, 1)
                    sp.dma_start(attr_o[bass.ds(2 * i + k, 1)].rearrange("g c t e -> c (g t) e"),
                                 attr_t[:, k, :].rearrange("c (t e) -> c t e", t=G)).then_inc(s_aout[k], 16)
            sp.wait_ge(s_rin, 1)
            nrest = REST - 1
            if nrest:
                sp.dma_start(rest_in[:, 0:nrest, :], edge_attr[16 * QIT * P:FULL * P, :].rearrange("(t e) c -> e t c", e=P)).then_inc(s_rin, 16)
            else:
                sp.sem_inc(s_rin, 16)
            sp.dma_start(rest_in[0:TAIL, nrest, :], edge_attr[FULL * P:E, :]).then_inc(s_rin, 16)
            sp.wait_ge(s_rest, 2 * RESTC)
            sp.dma_start(attr_d[16 * QIT * A:T * A, :].rearrange("(t c) e -> c t e", c=A),
                         rest_t[:, 0:REST * P].rearrange("c (t e) -> c t e", t=REST)).then_inc(s_aout[0], 16)

            for u in range(NU):
                sp.wait_ge(s_n0act, act0[f"skip{U - 1}", u])
                sp.dma_start(kv_d[u * U * P:(u + 1) * U * P, :].rearrange("(c p) f -> p c f", p=P), kv_u[:, u % 2, :, :]).then_inc(s_kvd[u % 2], 16)
            table_done(sp)
            sp.wait_ge(s_aout[0], 16 * (QIT + 1))
            sp.wait_ge(s_aout[1], 16 * QIT)
            sp.wait_ge(s_n0dve, LAST(dve0))
            sp.wait_ge(s_n0act, LAST(act0))

            attr_rows = attr_d.rearrange("(t c) e -> c t e", c=A)
            with sp.Fori(0, NG // 2) as i:
                for k in range(2):
                    sp.wait_ge(s_score[k], i)
                    sp.sem_inc(s_hop_sp, 1)
                    tiles = []
                    for m in (0, 4):
                        tiles += nc.values_load_multi_w_load_instructions(
                            visit_row[0:1, 1, bass.ds(16 * i + G * k + m, 4)], engines=[mybir.EngineType.SP], min_val=0, max_val=T - 1)[1]
                    for m, t in enumerate(tiles):
                        sp.dma_start(attr_g[:, k, m, :], attr_rows[:, bass.ds(t, 1), :].rearrange("c t e -> c (t e)")).then_inc(s_attr1[k], 16)
                for k in range(2):
                    sp.wait_ge(s_kve[1], 2 * i + k + 1)
                    sp.sem_inc(s_hop_sp, 1)
                    sp.dma_start(v_d[bass.ds(2 * i + k, 1)].rearrange("g p s f -> p (g s) f"), kv_edge[:, k, :, 1, :]).then_inc(s_vout[k], 16)

            for h in range(H):
                sp.wait_ge(s_lc, -(-NCH // U))
                sp.dma_start(line_d[h, :].rearrange("(c v e) -> v c e", v=CHUNK, e=P),
                             line_rows[h::H, :, :]).then_inc(s_lined, 16)
            flat = key_d.rearrange("v e -> (v e)")[0:V * P]
            sp.wait_ge(s_pad, 3)
            sp.dma_start(keys[:, 1:LINE + 1], flat.rearrange("(p n) -> p n", p=P)).then_inc(s_keys, 16)
            sp.dma_start(keys[1:P, 0:1], flat[LINE - 1:LINE - 1 + (P - 1) * LINE].rearrange("(p n) -> p n", n=LINE)[:, 0:1]).then_inc(s_keys, 16)
            sp.dma_start(keys[0:P - 1, LINE + 1:LINE + 2], flat[LINE:V * P].rearrange("(p n) -> p n", n=LINE)[:, 0:1]).then_inc(s_keys, 16)
            sp.wait_ge(s_lined, 16 * H)
            for h in range(H):
                sp.dma_start(line[:, h, :], line_d[h, :].rearrange("(p n) -> p n", p=P)).then_inc(s_line, 16)
            for h in range(H):
                sp.wait_ge(s_exp, h + 1)
                sp.dma_start(exp_d[h, :].rearrange("(p n) -> p n", p=P), line[:, h, :]).then_inc(s_expd, 16)
            for h in range(H):
                sp.wait_ge(s_expd, 16 * H)
                sp.dma_start(line_rows[h::H, :, :],
                             exp_d[h, :].rearrange("(c v e) -> v c e", v=CHUNK, e=P)).then_inc(s_expr, 16)

            sp.wait_ge(s_vout[0], 16 * (NG // 2))
            sp.wait_ge(s_vout[1], 16 * (NG // 2))
            sp.wait_ge(s_et, NCH)
            with sp.Fori(0, NG // 4) as i:
                for k in range(4):
                    sp.wait_ge(s_msg1[k], i)
                    sp.sem_inc(s_hop_sp, 1)
                    sp.dma_start(v_ring[:, k, :, :], v_d[bass.ds(4 * i + k, 1)].rearrange("g p s f -> p (g s) f")).then_inc(s_v[k], 16)

            for u in range(NU):
                sp.wait_ge(s_n1dve, dve1["y", u])
                b0, b1_ = u * U, min((u + 1) * U, N // P)
                if b1_ > b0:
                    sp.dma_start(out[b0 * P:b1_ * P, :].rearrange("(b p) f -> p b f", p=P), xs[:, b0:b1_, :]).then_inc(s_out, 16)
                else:
                    sp.sem_inc(s_out, 16)
            if N % P:
                sp.dma_start(out[(N // P) * P:N, :], xs[0:N % P, N // P, :]).then_inc(s_out, 16)
                sp.wait_ge(s_out, 16 * (NU + 1))
            else:
                sp.wait_ge(s_out, 16 * NU)

        @block.gpsimd
        def _(pool):
            pool.memset(xs[:, N // P:NBP, :], 0.0).then_inc(s_pad, 1)
            pool.memset(pad_row[:, :], 0).then_inc(s_const, 1)
            pool.wait_ge(s_const, 1)
            pool.memset(pad_row[:, P:2 * P], -1).then_inc(s_pad, 1)
            pool.memset(ones[:, :], 1.0).then_inc(s_const, 1)
            pool.memset(ident[:, :], 0.0).then_inc(s_const, 1)
            pool.memset(identb[:, :], 0.0).then_inc(s_const, 1)
            pool.wait_ge(s_const, 4)
            for m in (ident, identb):
                pool.affine_select(out=m[:, :], in_=m[:, :], compare_op=ALU.not_equal, fill=1.0, base=0,
                                   pattern=[[-1, P]], channel_multiplier=1).then_inc(s_const, 1)
            pool.iota(iota[:, :], pattern=[[1, P]], base=0, channel_multiplier=0,
                      allow_small_or_imprecise_dtypes=True).then_inc(s_const, 1)
            pool.iota(vis[:, 0, :], pattern=[[P, VC]], base=0, channel_multiplier=1,
                      allow_small_or_imprecise_dtypes=True).then_inc(s_const, 1)
            pool.memset(zeros[:, :], 0.0).then_inc(s_const, 1)
            for n, w in enumerate((wk, wv, wq, wskip)):
                pool.dma_start(w_kvqs[:, n * F:(n + 1) * F], w).then_inc(s_wload, 16)
            for n, b in enumerate((bk, bv, bq, bskip)):
                pool.dma_start(b_kvqs[0:1, n * F:(n + 1) * F], b.rearrange("(a n) -> a n", a=1)).then_inc(s_wload, 16)
            for s, w in ((w_mix_s, w_mix), (w1_s, w1), (w2_s, w2), (we_s, we)):
                pool.dma_start(s[:, :], w).then_inc(s_wload, 16)
            pool.dma_start(b1_s[:, :], b1.rearrange("(n a) -> n a", a=1)).then_inc(s_wload, 16)
            pool.dma_start(b2_s[:, :], b2.rearrange("(a n) -> a n", a=1)).then_inc(s_wload, 16)
            pool.wait_ge(s_vis, 1)
            pool.wait_ge(s_edges, 16 * 9)
            for c in range(VC):
                pool.indirect_dma_start(out=edge_int[:, c, :], out_offset=None, in_=edges_d,
                                        in_offset=bass.IndirectOffsetOnAxis(ap=vis_i[:, 7, c:c + 1], axis=0)).then_inc(s_rows, 16)
            pool.wait_ge(s_hd, 16)
            pool.wait_ge(s_trc, 3 * -(-VC // U))
            pool.wait_ge(s_keyd, 16)
            with pool.Fori(0, NG // 2) as i:
                for k in range(2):
                    pool.wait_ge(s_src0[k], i + 1)
                    pool.wait_ge(s_msg0[k], i)
                    pool.sem_inc(s_hop_pool, 1)
                    for m in range(G):
                        pool.indirect_dma_start(out=h_src[:, k, m, :], out_offset=None, in_=h_d,
                                                in_offset=bass.IndirectOffsetOnAxis(ap=src_ring[:, k, m:m + 1], axis=0)).then_inc(s_gath0[k], 16)
            table_done(pool)
            pool.wait_ge(s_n0dve, LAST(dve0))
            pool.wait_ge(s_n0act, LAST(act0))
            with pool.Fori(0, NG // 2) as i:
                for k in range(2):
                    pool.wait_ge(s_src1[k], i + 1)
                    pool.wait_ge(s_score[k], i)
                    pool.sem_inc(s_hop_pool, 1)
                    for m in range(G):
                        pool.indirect_dma_start(out=kv_src[:, k, m, :, :].rearrange("p t f -> p (t f)"), out_offset=None, in_=kv_d,
                                                in_offset=bass.IndirectOffsetOnAxis(ap=src_ring1[:, k, m:m + 1], axis=0)).then_inc(s_gath1[k], 16)
            pool.wait_ge(s_score[0], NG // 2)
            pool.wait_ge(s_score[1], NG // 2)
            pool.wait_ge(s_vout[0], 16 * (NG // 2))
            pool.wait_ge(s_vout[1], 16 * (NG // 2))
            pool.memset(keys[:, :], -2.0).then_inc(s_pad, 1)
            pool.wait_ge(s_et, NCH)
            with pool.Fori(0, NG // 4) as i:
                for k in range(4):
                    pool.wait_ge(s_expc[k], i + 1)
                    pool.sem_inc(s_hop_pool, 1)
                    for m in range(HALF):
                        ins = pool.tensor_scalar(hot1[:, k, HALF + m, :], iota[:, :], slot_ring[:, k, m:m + 1], None, ALU.is_equal)
                    ins.then_inc(s_hotp[k], 1)

        @block.vector
        def _(dve):
            order = [0]

            def step(ins):
                order[0] += 1
                ins.then_inc(s_dve, 1)
                dve.wait_ge(s_dve, order[0])

            V_ = nc.vector
            start, cnt = small[:, 0, :], small[:, 1, :]
            step(V_.memset(small[:, :, :], 0.0))
            dve.wait_ge(s_dst, 16)
            for b in range(1, NB):
                step(V_.tensor_scalar(below[0:PD, :], dst_all[0:PD, :], float(P * b), 0.0, ALU.is_lt, ALU.add,
                                      accum_out=cnt[0:PD, b:b + 1]))
            V_.memset(cnt[0:PD, NB:NB + 1], float(DD)).then_inc(s_cnt, 1)
            dve.wait_ge(s_x, 32)
            mean, var, rstd = stat[:, 0, :], stat[:, 1, :], stat[:, 2, :]

            def wide(a, n=F):
                return a.unsqueeze(2).to_broadcast([P, a.shape[1], n])

            step(V_.tensor_reduce(mean, xs[:, :, :], AX.X, ALU.add))
            step(V_.tensor_scalar(mean, mean, 1.0 / F, None, ALU.mult))
            V_.tensor_tensor(centred, xs[:, :, :], wide(mean), ALU.subtract).then_inc(s_mean, 1)
            dve.wait_ge(s_bound, 1)
            B = slice(0, NB)
            step(V_.tensor_copy(start[:, 0:NB + 1], bank(7)[:, 0:NB + 1]))
            end = start[:, 1:NB + 1]
            s_int, e_int, ft, cl, full, cntv, last, first, gap, dif = (small[:, n, B] for n in range(2, 12))
            si_i, ei_i = small_i[:, 12, B], small_i[:, 13, B]
            step(V_.tensor_copy(si_i, start[:, B]))
            step(V_.tensor_scalar(e_int, end, float(P - 1), None, ALU.add))
            step(V_.tensor_copy(ei_i, e_int))
            step(V_.tensor_scalar(small_i[:, 14, B], si_i, 7, None, ALU.arith_shift_right))
            step(V_.tensor_scalar(small_i[:, 15, B], ei_i, 7, None, ALU.arith_shift_right))
            step(V_.tensor_copy(ft, small_i[:, 14, B]))
            step(V_.tensor_copy(cl, small_i[:, 15, B]))
            step(V_.tensor_tensor(full, end, start[:, B], ALU.is_gt))
            step(V_.tensor_tensor(cntv, cl, ft, ALU.subtract))
            step(V_.tensor_tensor(cntv, cntv, full, ALU.mult))
            step(V_.tensor_tensor_scan(last, ones[:, B], cntv, 0.0, ALU.mult, ALU.add))
            step(V_.tensor_tensor(first, last, cntv, ALU.subtract))
            step(V_.tensor_tensor(gap, ft, first, ALU.subtract))
            dve.wait_ge(s_const, 9)
            visit, blk, tile, live, base, tmp = (vis[:, n, :] for n in range(6))
            if NB > 1:
                step(V_.tensor_tensor(dif[:, 1:NB], gap[:, 1:NB], gap[:, 0:NB - 1], ALU.subtract))
                step(V_.tensor_tensor(past, wide(visit, NB - 1), first[:, 1:NB].unsqueeze(1).to_broadcast([P, VC, NB - 1]), ALU.is_ge))
                step(V_.tensor_reduce(blk, past, AX.X, ALU.add))
                step(V_.tensor_tensor(past, past, dif[:, 1:NB].unsqueeze(1).to_broadcast([P, VC, NB - 1]), ALU.mult))
                step(V_.tensor_reduce(tile, past, AX.X, ALU.add))
            else:
                step(V_.memset(vis[:, 1:3, :], 0.0))
            step(V_.tensor_tensor(tile, tile, visit, ALU.add))
            step(V_.tensor_scalar(tile, tile, float(T - 1), 0.0, ALU.min, ALU.max))
            step(V_.tensor_scalar(live, visit, last[:, NB - 1:NB], None, ALU.is_ge))
            step(V_.tensor_scalar(tmp, live, float(1 << 22), None, ALU.mult))
            step(V_.tensor_scalar(base, blk, float(P), None, ALU.mult))
            step(V_.tensor_tensor(base, base, tmp, ALU.add))
            step(V_.tensor_copy(vis_i[:, 6, :], blk))
            V_.tensor_copy(vis_i[:, 7, :], tile).then_inc(s_vis, 1)
            dve.wait_ge(s_sq, 1)
            step(V_.tensor_reduce(var, squares, AX.X, ALU.add))
            V_.tensor_scalar(var, var, 1.0 / F, LN_EPS, ALU.mult, ALU.add).then_inc(s_var, 1)
            dve.wait_ge(s_std, 1)
            step(V_.reciprocal(rstd, stat[:, 3, :]))
            step(V_.tensor_scalar(hs[:, :, :], centred, 0.0, None, ALU.max))
            V_.tensor_tensor(hs[:, :, :], hs[:, :, :], wide(rstd), ALU.mult).then_inc(s_h, 1)
            dve.wait_ge(s_rows, 16 * VC)
            step(V_.tensor_tensor(rel, edge_int[:, :, P:2 * P], wide(base, P), ALU.subtract))
            step(V_.tensor_scalar(fits, rel, 0.0, None, ALU.is_ge))
            step(V_.scalar_tensor_tensor(fits, rel, float(P), fits, ALU.is_lt, ALU.mult))
            step(V_.scalar_tensor_tensor(key, edge_int[:, :, P:2 * P], 1.0, fits, ALU.add, ALU.mult))
            step(V_.tensor_scalar(key, key, 1.0, None, ALU.subtract))
            V_.tensor_copy(srcf, edge_int[:, :, 0:P]).then_inc(s_key, 1)
            dve.wait_ge(s_dec, 1)
            g = gate
            step(V_.tensor_scalar(g[:, 4:5], g[:, 3:4], 1e-6, None, ALU.add))
            step(V_.reciprocal(g[:, 5:6], g[:, 4:5]))
            dve.wait_ge(s_trc, 3 * -(-VC // U))
            wv_ = wgt_e[:, 0:V]
            step(V_.tensor_scalar(decay, wv_, g[:, 5:6], 0.0, ALU.mult, ALU.max))
            step(V_.tensor_tensor(decay, decay, decay, ALU.mult))
            step(V_.tensor_scalar(sig, wv_, g[:, 1:2], g[:, 2:3], ALU.mult, ALU.add))
            V_.memset(ok, 0.0).then_inc(s_decv, 1)
            dve.wait_ge(s_dec, 2)
            step(V_.tensor_scalar(sig, sig, 1.0, None, ALU.add))
            step(V_.reciprocal(sig, sig))
            step(V_.tensor_tensor(decay, decay, sig, ALU.mult))
            step(V_.tensor_scalar(ok, decay, FLT_MAX, None, ALU.is_le))
            step(V_.tensor_scalar(sig, decay, -FLT_MAX, None, ALU.is_ge))
            step(V_.tensor_tensor(ok, ok, sig, ALU.mult))
            step(V_.memset(wv_, 0.0))
            V_.copy_predicated(wv_, ok.bitcast(i32), decay).then_inc(s_wgt, 1)
            dve.wait_ge(s_wgt, 1)

            dve.wait_ge(s_keyd, 16)
            dve.wait_ge(s_hd, 16)
            dve.wait_ge(s_visr, 16)
            V_.memset(rest_in, 0.0).then_inc(s_rin, 1)
            with dve.Fori(0, NG // 2) as i:
                for k in range(2):
                    at = bass.ds(16 * i + G * k, G)
                    dve.wait_ge(s_gath0[k], 16 * G * i)
                    V_.tensor_copy(src_ring[:, k, :], src_e[:, at]).then_inc(s_src0[k], 1)
                    dve.wait_ge(s_msg0[k], i)
                    V_.tensor_copy(wgt_ring[:, k, :], wgt_e[:, at]).then_inc(s_wr0[k], 1)
                    dve.wait_ge(s_acc0[k], i)
                    V_.tensor_tensor(hot0[:, k, :, :], iota[:, :].unsqueeze(1).to_broadcast([P, G, P]),
                                     slot_e[:, at].unsqueeze(2).to_broadcast([P, G, P]), ALU.is_equal).then_inc(s_hot0[k], 1)

            at0 = [0]

            def tick(name, u, ins, chained=True):
                at0[0] += 1
                assert dve0[name, u] == at0[0]
                ins.then_inc(s_n0dve, 1)
                if chained:
                    dve.wait_ge(s_n0dve, at0[0])

            for k in range(2):
                dve.wait_ge(s_acc0[k], NG // 2)
            dve.wait_ge(s_rest, 2 * RESTC)
            dve.wait_ge(s_aout[0], 16 * (QIT + 1))
            dve.wait_ge(s_aout[1], 16 * QIT)
            tick("degree", 0, V_.tensor_scalar(degree[:, :], acc[:, STATS:STATS + NB], 1.0, None, ALU.max))
            tick("one", 0, V_.memset(stat[:, 0, :], 1.0))
            tick("rdeg", 0, V_.reciprocal(stat[:, 0, 0:NB], degree[:, :]))
            for u in range(NU):
                tick("mean", u, V_.tensor_tensor(mean_in[:, u * U:(u + 1) * U, :], bank(u).rearrange("p (b f) -> p b f", b=U),
                                                 wide(stat[:, 0, u * U:(u + 1) * U]), ALU.mult), chained=False)
            tick("xh", 0, V_.tensor_tensor(xs[:, :, :], xs[:, :, :], hs[:, :, :], ALU.add))

            def second_norm(u):
                sl, k = slice(u * U, (u + 1) * U), u % 2
                c3, q3, h3 = (a[:, k, :].rearrange("p (b f) -> p b f", b=U) for a in (c_u, sq_u, h2_u))
                m4, v4, d4, r4 = (stat[:, n, sl] for n in range(4))
                dve.wait_ge(s_n0pe, pe0["mix", u])
                tick("x1", u, V_.tensor_tensor(xs[:, sl, :], bank(u).rearrange("p (b f) -> p b f", b=U), xs[:, sl, :], ALU.add))
                tick("sum", u, V_.tensor_reduce(m4, xs[:, sl, :], AX.X, ALU.add))
                tick("mu", u, V_.tensor_scalar(m4, m4, 1.0 / F, None, ALU.mult))
                tick("centre", u, V_.tensor_tensor(c3, xs[:, sl, :], wide(m4), ALU.subtract))
                tick("square", u, V_.tensor_tensor(q3, c3, c3, ALU.mult))
                tick("sum2", u, V_.tensor_reduce(v4, q3, AX.X, ALU.add))
                tick("var", u, V_.tensor_scalar(v4, v4, 1.0 / F, LN_EPS, ALU.mult, ALU.add))
                tick("relu", u, V_.tensor_scalar(c3, c3, 0.0, None, ALU.max))
                dve.wait_ge(s_n0act, act0["std", u])
                tick("rstd", u, V_.reciprocal(r4, d4))
                if u >= 2:
                    dve.wait_ge(s_n0pe, pe0["h2_t", u - 2])
                tick("h2", u, V_.tensor_tensor(h3, c3, wide(r4), ALU.mult), chained=False)

            second_norm(0)
            for u in range(NU):
                if u + 1 < NU:
                    second_norm(u + 1)
                for c in range(U):
                    b = u * U + c
                    dve.wait_ge(s_n0act, act0[f"q{c}", u])
                    qf = q_f[:, c % 2, :, :]
                    tick(f"part0{c}", u, V_.tensor_copy(qs[:, b, 0, :], qf[:, 0, :]))
                    tick(f"left1{c}", u, V_.tensor_tensor(qf[:, 1, :], qf[:, 0, :], qs[:, b, 0, :], ALU.subtract))
                    tick(f"part1{c}", u, V_.tensor_copy(qs[:, b, 1, :], qf[:, 1, :]))
                    tick(f"left2{c}", u, V_.tensor_tensor(qf[:, 2, :], qf[:, 1, :], qs[:, b, 1, :], ALU.subtract))
                    tick(f"part2{c}", u, V_.tensor_copy(qs[:, b, 2, :], qf[:, 2, :]))

            table_done(dve)
            dve.wait_ge(s_n0act, LAST(act0))
            with dve.Fori(0, NG // 2) as i:
                for k in range(2):
                    g_ = 2 * i + k
                    dve.wait_ge(s_gath1[k], 16 * G * i)
                    V_.tensor_copy(src_ring1[:, k, :], src_e[:, bass.ds(16 * i + G * k, G)]).then_inc(s_src1[k], 1)
                    V_.tensor_tensor(hot_b[:, k, :, :], iota[:, :].unsqueeze(1).to_broadcast([P, G, P]),
                                     slot_e[:, bass.ds(16 * i + G * k, G)].unsqueeze(2).to_broadcast([P, G, P]),
                                     ALU.is_equal).then_inc(s_hot1[k], 1)
                    dve.wait_ge(s_vout[k], 16 * i)
                    dve.wait_ge(s_gath1[k], 16 * G * i + 16 * G)
                    for j in range(2):
                        part = slice(HALF * j, HALF * (j + 1))
                        dve.wait_ge(s_edge[j], g_ + 1)
                        V_.tensor_tensor(kv_edge[:, k, part, :, :], kv_src[:, k, part, :, :],
                                         bank(4 + j).rearrange("p (s f) -> p s f", s=HALF).unsqueeze(2).to_broadcast([P, HALF, 2, F]),
                                         ALU.add).then_inc(s_kve[j], 1)
                        dve.wait_ge(s_kve[j], g_ + 1)
                        dve.wait_ge(s_q[j], g_ + 1)
                        V_.tensor_tensor(prod[:, j, :].rearrange("p (s f) -> p s f", s=HALF), kv_edge[:, k, part, 0, :],
                                         bank(2 + j).rearrange("p (s f) -> p s f", s=HALF), ALU.mult).then_inc(s_prod[j], 1)
                        dve.wait_ge(s_prod[j], g_ + 1)
                        red = V_.tensor_reduce(score[:, bass.ds(16 * i + G * k + HALF * j, HALF), :],
                                               prod[:, j, :].rearrange("p (s h c) -> p s h c", s=HALF, h=H), AX.X, ALU.add)
                    red.then_inc(s_score[k], 1)

            dve.wait_ge(s_keys, 48)
            step(V_.tensor_tensor(apart, keys[:, 0:LINE + 1], keys[:, 1:LINE + 2], ALU.is_equal))
            step(V_.tensor_scalar(apart, apart, BIG, BIG, ALU.mult, ALU.subtract))
            step(V_.tensor_tensor_scan(lead, apart[:, 0:LINE], apart[:, 0:LINE], 0.0, ALU.min, ALU.min))
            step(V_.tensor_tensor_scan(trail[:, ::-1], apart[:, LINE:0:-1], apart[:, LINE:0:-1], 0.0, ALU.min, ALU.min))
            for h in range(H):
                dve.wait_ge(s_line, 16 * H)
                step(V_.tensor_tensor_scan(peak[:, h, :], apart[:, 0:LINE], line[:, h, :], -BIG, ALU.add, ALU.max))
                step(V_.tensor_tensor_scan(peak[:, h, ::-1], apart[:, LINE:0:-1], peak[:, h, ::-1], -BIG, ALU.add, ALU.max))
                step(V_.tensor_copy(ends[:, 0, h:h + 1], peak[:, h, LINE - 1:LINE]))
                step(V_.tensor_copy(ends[:, 1, h:h + 1], peak[:, h, 0:1]))
                step(V_.tensor_copy(ends[:, 2, h:h + 1], lead[:, LINE - 1:LINE]))
                step(V_.tensor_copy(ends[:, 3, h:h + 1], trail[:, 0:1]))
            step(V_.memset(ends_t[0:H, :, :], -BIG))
            V_.memset(ends[:, 4, :], 0.0).then_inc(s_ends, 1)
            dve.wait_ge(s_endt, 1)
            for n in range(4):
                step(V_.tensor_copy(ends_t[0:H, n, 0:P], bank(7)[0:H, n * P:(n + 1) * P]))
            step(V_.tensor_tensor_scan(ends_t[0:H, 4, 1:P + 1], ends_t[0:H, 2, 0:P], ends_t[0:H, 0, 0:P], -BIG, ALU.add, ALU.max))
            step(V_.tensor_tensor_scan(ends_t[0:H, 5, P - 1::-1], ends_t[0:H, 3, P - 1::-1], ends_t[0:H, 1, P - 1::-1], -BIG, ALU.add, ALU.max))
            V_.memset(ends[:, 5, :], 0.0).then_inc(s_ends, 1)
            dve.wait_ge(s_endt, 2)
            step(V_.tensor_copy(ends[:, 4, 0:2 * H], bank(7)[:, 0:2 * H]))
            for h in range(H):
                step(V_.scalar_tensor_tensor(peak[:, h, :], lead, ends[:, 4, h:h + 1], peak[:, h, :], ALU.add, ALU.max))
                step(V_.scalar_tensor_tensor(peak[:, h, :], trail, ends[:, 4, H + h:H + h + 1], peak[:, h, :], ALU.add, ALU.max))
                V_.tensor_tensor(line[:, h, :], line[:, h, :], peak[:, h, :], ALU.subtract).then_inc(s_diff, 1)

            dve.wait_ge(s_et, NCH)
            with dve.Fori(0, NG // 4) as i:
                for k in range(4):
                    dve.wait_ge(s_acc1[k], i)
                    V_.tensor_tensor(hot1[:, k, 0:HALF, :], iota[:, :].unsqueeze(1).to_broadcast([P, HALF, P]),
                                     slot_e[:, bass.ds(32 * i + G * k, HALF)].unsqueeze(2).to_broadcast([P, HALF, P]), ALU.is_equal)
                    dve.wait_ge(s_v[k], 16 * i + 16)
                    dve.wait_ge(s_expc[k], i + 1)
                    V_.tensor_tensor(msg[:, k, :, :].rearrange("p s (h c) -> p (s h) c", h=H),
                                     v_ring[:, k, :, :].rearrange("p s (h c) -> p (s h) c", h=H),
                                     exp_ring[:, k, :, :].rearrange("p s h -> p (s h)").unsqueeze(2).to_broadcast([P, G * H, C]),
                                     ALU.mult).then_inc(s_msg1[k], 1)

            at1 = [0]

            def tock(name, u, ins, chained=True):
                at1[0] += 1
                assert dve1[name, u] == at1[0]
                ins.then_inc(s_n1dve, 1)
                if chained:
                    dve.wait_ge(s_n1dve, at1[0])

            for k in range(4):
                dve.wait_ge(s_acc1[k], NG // 4)
            tock("esum", 0, V_.tensor_scalar(esum[:, :, :], acc[:, STATS:STATS + NB * H].rearrange("p (b h) -> p b h", h=H), 1e-16, None, ALU.add))
            tock("resum", 0, V_.reciprocal(r_u, esum[:, :, :]))
            for u in range(NU):
                b0, b1_ = u * U, min((u + 1) * U, NB)
                n = b1_ - b0
                tock("pad", u, V_.memset(o_u[:, (b1_ if n < U else b0):(u + 1) * U, :], 0.0))
                tock("o", u, V_.tensor_tensor(o_u[:, b0:b1_, :].rearrange("p b (h c) -> p (b h) c", h=H),
                                              bank(u)[:, 0:n * F].rearrange("p (k c) -> p k c", c=C),
                                              r_u[:, b0:b1_, :].rearrange("p b h -> p (b h)").unsqueeze(2).to_broadcast([P, n * H, C]), ALU.mult))
                tock("skip", u, V_.tensor_tensor(o_u[:, u * U:(u + 1) * U, :], o_u[:, u * U:(u + 1) * U, :], hs[:, u * U:(u + 1) * U, :], ALU.add))
            for u in range(NU):
                sl, k = slice(u * U, (u + 1) * U), u % 2
                tock("xo", u, V_.tensor_tensor(xs[:, sl, :], xs[:, sl, :], o_u[:, sl, :], ALU.add))
                dve.wait_ge(s_n1act, act1["gelu2", u])
                tock("y", u, V_.tensor_tensor(xs[:, sl, :], xs[:, sl, :], g_u[:, k, :].rearrange("p (b f) -> p b f", b=U), ALU.add), chained=False)

        @block.scalar
        def _(act):
            S_ = nc.scalar
            for n, a in enumerate((log_scale, filter_w, filter_b)):
                act.dma_start(gate[:, n:n + 1], a.rearrange("(a n) -> a n", a=1).to_broadcast([P, 1])).then_inc(s_gate, 16)
            act.wait_ge(s_gate, 48)
            S_.activation(gate[:, 3:4], gate[:, 0:1], ACT.Exp).then_inc(s_dec, 1)
            act.wait_ge(s_mean, 1)
            S_.activation(squares, centred, ACT.Square).then_inc(s_sq, 1)
            act.wait_ge(s_var, 1)
            S_.activation(stat[:, 3, :], stat[:, 1, :], ACT.Sqrt).then_inc(s_std, 1)
            n = 0
            for dest in (slot_e, src_e, wgt_e):
                for c in range(0, VC, U):
                    w = min(U, VC - c) * P
                    act.wait_ge(s_tr, n + 1)
                    S_.activation(dest[:, c * P:c * P + w], bank(n % 7)[:, 0:w], ACT.Copy).then_inc(s_trc, 1)
                    n += 1
            act.wait_ge(s_decv, 1)
            S_.activation(decay, decay, ACT.Exp, scale=-1.0).then_inc(s_act, 1)
            S_.activation(sig, sig, ACT.Exp, scale=-1.0).then_inc(s_dec, 1)
            act.wait_ge(s_act, 1)

            act.wait_ge(s_keyd, 16)

            def messages(i, k):
                act.wait_ge(s_gath0[k], 16 * G * i + 16 * G)
                act.wait_ge(s_wr0[k], i + 1)
                act.wait_ge(s_acc0[k], i)
                act.sem_inc(s_hop_act, 1)
                for m in range(G):
                    ins = S_.activation(h_wgt[:, k, m, :], h_src[:, k, m, :], ACT.Copy, scale=wgt_ring[:, k, m:m + 1])
                ins.then_inc(s_msg0[k], 1)

            with act.Fori(0, QIT) as i:
                for k in range(2):
                    messages(i, k)
                    act.wait_ge(s_atr, 2 * i + k + 1)
                    act.wait_ge(s_aout[k], 16 * i)
                    act.sem_inc(s_hop_act, 1)
                    for j in range(4):
                        ins = S_.activation(attr_t[:, k, :].rearrange("c (t r j) -> c t r j", t=G, j=4)[:, :, :, j],
                                            aside[32 * j:32 * j + A, 0:2 * P].rearrange("c (t r) -> c t r", t=G), ACT.Copy)
                    ins.then_inc(s_atc, 1)
            for i in range(QIT, NG // 2):
                for k in range(2):
                    messages(i, k)
            for n in range(RESTC):
                w = min(4, REST - 4 * n) * P
                act.wait_ge(s_rest, 2 * n + 1)
                S_.activation(rest_t[:, 4 * n * P:4 * n * P + w], aside[0:A, 0:w], ACT.Copy).then_inc(s_rest, 1)

            act.wait_ge(s_n0dve, dve0["xh", 0])
            at0 = [0]

            def tick(name, u, ins):
                at0[0] += 1
                assert act0[name, u] == at0[0]
                ins.then_inc(s_n0act, 1)

            def side_std(u):
                act.wait_ge(s_n0pe, pe0["mean_t", u])
                tick("side", u, S_.activation(side[:, u % 2, :], bank(u), ACT.Copy))
                act.wait_ge(s_n0dve, dve0["var", u])
                tick("std", u, S_.activation(stat[:, 2, u * U:(u + 1) * U], stat[:, 1, u * U:(u + 1) * U], ACT.Sqrt))

            side_std(0)
            for u in range(NU):
                k = u % 2
                if u + 1 < NU:
                    side_std(u + 1)
                act.wait_ge(s_n0pe, pe0["h2_t", u])
                tick("h2_side", u, S_.activation(h2t_u[:, k, :], bank(u), ACT.Copy))
                if u >= 2:
                    act.wait_ge(s_kvd[k], 16 * (u // 2))
                for c in range(U):
                    b = u * U + c
                    dest = bank(7) if c % 2 == 0 else bank(u)
                    act.wait_ge(s_n0pe, pe0[f"proj{c}", u])
                    tick(f"kv{c}", u, S_.activation(kv_u[:, k, c, :], dest[:, 0:2 * F], ACT.Copy))
                    if b >= 2:
                        act.wait_ge(s_n0dve, dve0[f"part2{(b - 2) % U}", (b - 2) // U])
                    tick(f"q{c}", u, S_.activation(q_f[:, c % 2, 0, :], dest[:, 2 * F:3 * F], ACT.Copy))
                    tick(f"skip{c}", u, S_.activation(hs[:, b, :], dest[:, 3 * F:4 * F], ACT.Copy))

            act.wait_ge(s_n0act, LAST(act0))
            table_done(act)
            with act.Fori(0, NG // 2) as i:
                for k in range(2):
                    for j in range(2):
                        act.wait_ge(s_hott[j], 2 * i + k + 1)
                        act.sem_inc(s_hop_act, 1)
                        S_.activation(hot_t[:, k, HALF * j:HALF * (j + 1), :],
                                      bank(j).bitcast(bf16)[:, 0:HALF * P].rearrange("p (s e) -> p s e", s=HALF), ACT.Copy).then_inc(s_hotc[j], 1)

            for k in range(2):
                act.wait_ge(s_score[k], NG // 2)
                act.wait_ge(s_vout[k], 16 * (NG // 2))
            for n in range(0, NCH, U):
                w = min(U, NCH - n)
                act.wait_ge(s_lt, min(n + U, NCH))
                S_.activation(line_rows[:, n:n + w, :], bank(n // U)[:, 0:w * P].rearrange("p (c e) -> p c e", c=w), ACT.Copy).then_inc(s_lc, 1)
            for h in range(H):
                act.wait_ge(s_diff, h + 1)
                S_.activation(line[:, h, :], line[:, h, :], ACT.Exp, scale=float(C) ** -0.5).then_inc(s_exp, 1)
            for n in range(NCH):
                act.wait_ge(s_et, n + 1)
                S_.activation(score[:, CHUNK * n:CHUNK * (n + 1), :].rearrange("p v h -> p (v h)"), bank(n % 7)[:, 0:P], ACT.Copy).then_inc(s_ec, 1)

            act.wait_ge(s_ec, NCH)
            with act.Fori(0, NG // 4) as i:
                for k in range(4):
                    act.wait_ge(s_acc1[k], i)
                    act.sem_inc(s_hop_act, 1)
                    S_.activation(slot_ring[:, k, :], slot_e[:, bass.ds(32 * i + G * k + HALF, HALF)], ACT.Copy)
                    S_.activation(exp_ring[:, k, :, :], score[:, bass.ds(32 * i + G * k, G), :], ACT.Copy).then_inc(s_expc[k], 1)

            at1 = [0]

            def tock(name, u, ins):
                at1[0] += 1
                assert act1[name, u] == at1[0]
                ins.then_inc(s_n1act, 1)

            def o_side(u):
                act.wait_ge(s_n1pe, pe1["o_t", u])
                tock("ot", u, S_.activation(ot_u[:, u % 2, :], bank(u), ACT.Copy))

            o_side(0)
            for u in range(NU):
                k = u % 2
                if u + 1 < NU:
                    o_side(u + 1)
                act.wait_ge(s_n1pe, pe1["w1", u])
                tock("gelu1", u, S_.activation(ht_u[:, k, :], bank(u), ACT.Gelu_apprx_tanh, bias=b1_s[:, 0:1]))
                act.wait_ge(s_n1pe, pe1["w2", u])
                if u >= 2:
                    act.wait_ge(s_n1dve, dve1["y", u - 2])
                tock("gelu2", u, S_.activation(g_u[:, k, :], bank(u), ACT.Gelu_apprx_tanh))

        @block.tensor
        def _(pe):
            T_ = nc.tensor
            pe.wait_ge(s_const, 9)
            pe.wait_ge(s_cnt, 1)
            T_.matmul(bank(7)[:, 0:NB + 1], ones[0:PD, :], small[0:PD, 1, 0:NB + 1], start=True, stop=True).then_inc(s_bound, 1)
            pe.wait_ge(s_key, 1)
            n = 0
            for rows in (rel, srcf, edge_rows[:, :, 2 * P:3 * P]):
                for c in range(0, VC, U):
                    w = min(U, VC - c)
                    if n >= 7:
                        pe.wait_ge(s_trc, n - 6)
                    for m in range(w):
                        ins = T_.transpose(bank(n % 7)[:, m * P:(m + 1) * P], rows[:, c + m, :], ident[:, :])
                    ins.then_inc(s_tr, 1)
                    n += 1
            pe.wait_ge(s_trc, n)

            def open_blocks():
                for u in range(NU):
                    ins = T_.matmul(bank(u), zeros[:, 0:P], zeros[:, :], start=True, stop=True)
                ins.then_inc(s_zero, 1)

            open_blocks()
            pe.wait_ge(s_visr, 16)

            def sum0(i, k):
                pe.wait_ge(s_hot0[k], i + 1)
                pe.wait_ge(s_msg0[k], i + 1)
                for m, b in enumerate(load_blocks(pe, 16 * i + G * k)):
                    T_.matmul(acc[:, bass.ds(b * P, P)], hot0[:, k, m, :], h_wgt[:, k, m, :], start=False, stop=True, skip_group_check=True)
                    ins = T_.matmul(acc[:, bass.ds(b + STATS, 1)], hot0[:, k, m, :], ones[:, 0:1], start=False, stop=True, skip_group_check=True)
                ins.then_inc(s_acc0[k], 1)

            with pe.Fori(0, QIT) as i:
                for k in range(2):
                    pe.wait_ge(s_ain[k], 16 * i + 16)
                    pe.wait_ge(s_atc, 2 * i + k)
                    for q in range(2):
                        ins = T_.transpose(aside[:, q * P:(q + 1) * P], attr_in[:, k, q, :], ident[:, :])
                    ins.then_inc(s_atr, 1)
                    sum0(i, k)
            for i in range(QIT, NG // 2):
                for k in range(2):
                    sum0(i, k)
            pe.wait_ge(s_rin, 33)
            pe.wait_ge(s_atc, 2 * QIT)
            for n in range(RESTC):
                if n:
                    pe.wait_ge(s_rest, 2 * n)
                for m in range(min(4, REST - 4 * n)):
                    ins = T_.transpose(aside[0:A, m * P:(m + 1) * P], rest_in[:, 4 * n + m, :], ident[:, :])
                ins.then_inc(s_rest, 1)
            pe.wait_ge(s_rest, 2 * RESTC)

            pe.wait_ge(s_wload, 16 * WEIGHTS)
            at0 = [0]

            def tick(name, u, ins):
                at0[0] += 1
                assert pe0[name, u] == at0[0]
                ins.then_inc(s_n0pe, 1)

            def mix(u):
                pe.wait_ge(s_n0dve, dve0["mean", u])
                for c in range(U):
                    ins = T_.transpose(bank(u)[:, c * P:(c + 1) * P], mean_in[:, u * U + c, :], ident[:, :])
                tick("mean_t", u, ins)
                pe.wait_ge(s_n0act, act0["side", u])
                for c in range(U):
                    ins = T_.matmul(bank(u)[:, c * F:(c + 1) * F], side[:, u % 2, c * P:(c + 1) * P], w_mix_s[:, :], start=True, stop=True)
                tick("mix", u, ins)

            mix(0)
            for u in range(NU):
                if u + 1 < NU:
                    mix(u + 1)
                pe.wait_ge(s_n0dve, dve0["h2", u])
                for c in range(U):
                    ins = T_.transpose(bank(u)[:, c * P:(c + 1) * P], h2_u[:, u % 2, c * P:(c + 1) * P], ident[:, :])
                tick("h2_t", u, ins)
                pe.wait_ge(s_n0act, act0["h2_side", u])
                for c in range(U):
                    b = u * U + c
                    if b >= 2:
                        pe.wait_ge(s_n0act, act0[f"skip{(b - 2) % U}", (b - 2) // U])
                    dest = bank(7) if c % 2 == 0 else bank(u)
                    T_.matmul(dest, ones[0:1, :], b_kvqs[0:1, :], start=True, stop=False)
                    tick(f"proj{c}", u, T_.matmul(dest, h2t_u[:, u % 2, c * P:(c + 1) * P], w_kvqs[:, :], start=False, stop=True))

            pe.wait_ge(s_n0act, LAST(act0))
            pe.wait_ge(s_n0dve, LAST(dve0))
            with pe.Fori(0, NG // 2) as i:
                for k in range(2):
                    g_ = 2 * i + k
                    blocks = load_blocks(pe, 16 * i + G * k)
                    pe.wait_ge(s_hot1[k], i + 1)
                    for j in range(2):
                        for m in range(HALF):
                            ins = T_.transpose(bank(j).bitcast(bf16)[:, m * P:(m + 1) * P], hot_b[:, k, HALF * j + m, :], identb[:, :])
                        ins.then_inc(s_hott[j], 1)
                        if j == 0:
                            pe.wait_ge(s_attr1[k], 16 * G * i + 16 * G)
                        pe.wait_ge(s_kve[j], g_)
                        for m in range(HALF):
                            ins = T_.matmul(bank(4 + j)[:, m * F:(m + 1) * F], attr_g[:, k, HALF * j + m, :], we_s[:, :], start=True, stop=True)
                        ins.then_inc(s_edge[j], 1)
                        pe.wait_ge(s_hotc[j], g_ + 1)
                        pe.wait_ge(s_prod[j], g_)
                        for m in range(HALF):
                            b = blocks[HALF * j + m]
                            for t in range(3):
                                ins = T_.matmul(bank(2 + j)[:, m * F:(m + 1) * F], hot_t[:, k, HALF * j + m, :],
                                                qs[:, bass.ds(b, 1), t, :].rearrange("p b f -> p (b f)"), start=t == 0, stop=t == 2)
                        ins.then_inc(s_q[j], 1)

            for k in range(2):
                pe.wait_ge(s_score[k], NG // 2)
            for n in range(NCH):
                T_.transpose(bank(n // U)[:, (n % U) * P:(n % U + 1) * P], score[:, CHUNK * n:CHUNK * (n + 1), :].rearrange("p v h -> p (v h)"), ident[:, :]).then_inc(s_lt, 1)
            pe.wait_ge(s_ends, 1)
            for n in range(4):
                ins = T_.transpose(bank(7)[0:H, n * P:(n + 1) * P], ends[:, n, 0:H], ident[:, :])
            ins.then_inc(s_endt, 1)
            pe.wait_ge(s_ends, 2)
            T_.transpose(bank(7)[:, 0:H], ends_t[0:H, 4, 0:P], ident[0:H, 0:H])
            T_.transpose(bank(7)[:, H:2 * H], ends_t[0:H, 5, 1:P + 1], ident[0:H, 0:H]).then_inc(s_endt, 1)
            pe.wait_ge(s_expr, 16 * H)
            pe.wait_ge(s_lc, -(-NCH // U))
            for n in range(NCH):
                if n >= 7:
                    pe.wait_ge(s_ec, n - 6)
                T_.transpose(bank(n % 7)[:, 0:P], line_rows[:, n, :], ident[:, :]).then_inc(s_et, 1)
            pe.wait_ge(s_ec, NCH)

            open_blocks()
            with pe.Fori(0, NG // 4) as i:
                for k in range(4):
                    pe.wait_ge(s_hotp[k], i + 1)
                    pe.wait_ge(s_msg1[k], i + 1)
                    for m, b in enumerate(load_blocks(pe, 32 * i + G * k)):
                        T_.matmul(acc[:, bass.ds(b * P, P)], hot1[:, k, m, :], msg[:, k, m, :], start=False, stop=True, skip_group_check=True)
                        ins = T_.matmul(acc[:, bass.ds(b * H + STATS, H)], hot1[:, k, m, :], exp_ring[:, k, m, :], start=False, stop=True, skip_group_check=True)
                    ins.then_inc(s_acc1[k], 1)

            at1 = [0]

            def tock(name, u, ins):
                at1[0] += 1
                assert pe1[name, u] == at1[0]
                ins.then_inc(s_n1pe, 1)

            def o_t(u):
                pe.wait_ge(s_n1dve, dve1["skip", u])
                for c in range(U):
                    ins = T_.transpose(bank(u)[:, c * P:(c + 1) * P], o_u[:, u * U + c, :], ident[:, :])
                tock("o_t", u, ins)

            o_t(0)
            for u in range(NU):
                k = u % 2
                if u + 1 < NU:
                    o_t(u + 1)
                pe.wait_ge(s_n1act, act1["ot", u])
                tock("w1", u, T_.matmul(bank(u), w1_s[:, :], ot_u[:, k, :], start=True, stop=True))
                pe.wait_ge(s_n1act, act1["gelu1", u])
                for c in range(U):
                    T_.matmul(bank(u)[:, c * F:(c + 1) * F], ones[0:1, :], b2_s[:, :], start=True, stop=False)
                    ins = T_.matmul(bank(u)[:, c * F:(c + 1) * F], ht_u[:, k, c * P:(c + 1) * P], w2_s[:, :], start=False, stop=True)
                tock("w2", u, ins)


_INS = ['x', 'src', 'dst', 'edge_attr_32', 'edge_weight', 'L0_gnn_W_mix', 'L0_gnn_log_scale', 'L0_gnn_filter_w',
        'L0_gnn_filter_b', 'L1_gnn_Wq', 'L1_gnn_bq', 'L1_gnn_Wk', 'L1_gnn_bk', 'L1_gnn_Wv', 'L1_gnn_bv', 'L1_gnn_We',
        'L1_gnn_Wskip', 'L1_gnn_bskip', 'L1_gnn_W1', 'L1_gnn_b1', 'L1_gnn_W2', 'L1_gnn_b2']


def kernel(**inputs):
    import numpy as np
    import concourse.bacc as bacc
    from concourse.bass_utils import run_bass_kernel_spmd

    nc = bacc.Bacc("TRN2", target_bir_lowering=False, num_devices=1)
    arrays, args = {}, []
    for name in _INS:
        a = np.ascontiguousarray(inputs[name])
        a = a.reshape(1) if a.ndim == 0 else a
        arrays[f"in_{name}"] = a
        args.append(nc.dram_tensor(f"in_{name}", a.shape, mybir.dt.from_np(a.dtype), kind="ExternalInput").ap())
    shape = tuple(inputs['x'].shape)
    out = nc.dram_tensor("out", shape, mybir.dt.float32, kind="ExternalOutput").ap()
    gnn_kernel(nc, *args, out)
    r = run_bass_kernel_spmd(nc, [arrays], core_ids=[0])
    return r.results[0]["out"]
```

```python
import concourse.bass as bass
from concourse import mybir
from contextlib import ExitStack

P = 128
F = 128
H = 4
C = F // H
A = 32
G = 8
HALF = G // 2
BANK = 512
U = BANK // F
BIG = 1.0e30
FLT_MAX = 3.4028234e38
LN_EPS = 1e-5


def gnn_kernel(nc, x, src, dst, edge_attr, edge_weight, w_mix, log_scale, filter_w, filter_b,
               wq, bq, wk, bk, wv, bv, we, wskip, bskip, w1, b1, w2, b2, out):
    f32, bf16, i32 = mybir.dt.float32, mybir.dt.bfloat16, mybir.dt.int32
    ALU, ACT, AX = mybir.AluOpType, mybir.ActivationFunctionType, mybir.AxisListType

    N, E = x.shape[0], src.shape[0]
    NB = -(-N // P)
    NU = -(-NB // U)
    NBP = NU * U
    T = -(-E // P)
    TAIL = E - (T - 1) * P
    V = -(-(T + NB - 1) // 32) * 32
    VC = -(-V // P)
    NG = V // G
    PD = max(p for p in range(1, P + 1) if E % p == 0)
    DD = E // PD
    LINE = V * P // P
    CHUNK = 32
    NCH = V // CHUNK
    STATS = NB * P
    assert NU <= 7 and STATS + NB <= 7 * BANK and NB <= 32 and N < 1 << 24

    edges_d = nc.dram_tensor("edges_d", (T, 3 * P), i32).ap()
    h_d = nc.dram_tensor("h_d", (NBP * P, F), f32).ap()
    kv_d = nc.dram_tensor("kv_d", (NBP * P, 2 * F), f32).ap()
    attr_d = nc.dram_tensor("attr_d", (T * A, P), f32).ap()
    v_d = nc.dram_tensor("v_d", (NG, P, G, F), f32).ap()
    key_d = nc.dram_tensor("key_d", (VC * P, P), f32).ap()
    line_d = nc.dram_tensor("line_d", (H, V * P), f32).ap()
    exp_d = nc.dram_tensor("exp_d", (H, V * P), f32).ap()
    visit_d = nc.dram_tensor("visit_d", (2, VC * P), i32).ap()

    ctx = ExitStack()
    with ctx:
        ctx.enter_context(nc.allow_non_contiguous_dma(reason="a few hundred single words"))

        def sb(name, shape, dt=f32):
            return ctx.enter_context(nc.sbuf_tensor(name, shape, dt))

        def sem(name):
            return ctx.enter_context(nc.semaphore(name))

        def sems(name, n):
            return [sem(f"{name}{k}") for k in range(n)]

        ident = sb("ident", [P, P])
        identb = sb("identb", [P, P], bf16)
        iota = sb("iota", [P, P])
        ones = sb("ones", [P, P])
        zeros = sb("zeros", [P, BANK], bf16)
        w_kvqs = sb("w_kvqs", [P, 4 * F])
        b_rows = sb("b_rows", [1, 5 * F])
        b_part = sb("b_part", [1, 3, 5 * F], bf16)
        b_left = sb("b_left", [1, 2, 5 * F])
        b_3 = sb("b_3", [3, 5 * F], bf16)
        ones3 = sb("ones3", [3, P], bf16)
        w_mix_s = sb("w_mix_s", [P, F])
        w1_s = sb("w1_s", [P, F])
        w2_s = sb("w2_s", [P, F])
        b1_s = sb("b1_s", [P, 1])
        we_s = sb("we_s", [A, F])
        gate = sb("gate", [P, 8])
        xs = sb("xs", [P, NBP, F])
        hs = sb("hs", [P, NBP, F])
        qs = sb("qs", [P, NBP, 3, F], bf16)
        slot_e = sb("slot_e", [P, VC * P])
        src_e = sb("src_e", [P, VC * P + G], i32)
        wgt_e = sb("wgt_e", [P, VC * P])
        visit_row = sb("visit_row", [1, 2, VC * P], i32)
        score = sb("score", [P, V, H])
        stat = sb("stat", [P, 4, NBP])
        degree = sb("degree", [P, NB])

        ARENA = 17600
        arena = sb("arena", [P, ARENA])
        used = [0]

        def carve(words, dt=f32, fresh=False):
            if fresh:
                used[0] = 0
            view = arena[:, used[0]:used[0] + words]
            used[0] += words
            assert used[0] <= ARENA, used[0]
            return view if dt is f32 else view.bitcast(dt)

        edge_rows = carve(VC * 3 * P, fresh=True).rearrange("p (c n) -> p c n", c=VC)
        edge_int = edge_rows.bitcast(i32)
        dst_all = carve(DD, i32)
        below = carve(DD)
        rel = carve(VC * P).rearrange("p (c e) -> p c e", c=VC)
        fits = carve(VC * P).rearrange("p (c e) -> p c e", c=VC)
        key = carve(VC * P).rearrange("p (c e) -> p c e", c=VC)
        srcf = carve(VC * P).rearrange("p (c e) -> p c e", c=VC)
        past = carve(VC * (NB - 1)).rearrange("p (c b) -> p c b", c=VC)
        small = carve(24 * 32).rearrange("p (k b) -> p k b", b=32)
        small_i = small.bitcast(i32)
        vis = carve(8 * VC).rearrange("p (k c) -> p k c", k=8)
        vis_i = vis.bitcast(i32)
        pad_row = carve(3 * P, i32)
        centred = carve(NBP * F).rearrange("p (b f) -> p b f", b=NBP)
        squares = qs[:, :, :, :].rearrange("p b t f -> p (b t f)").bitcast(f32)[:, 0:NBP * F].rearrange("p (b f) -> p b f", b=NBP)
        decay, sig, ok = (score[:, :, :].rearrange("p v h -> p (v h)")[:, n * V:(n + 1) * V] for n in range(3))
        src_ring = carve(2 * G, i32, fresh=True).rearrange("p (k s) -> p k s", k=2)
        wgt_ring = carve(2 * G).rearrange("p (k s) -> p k s", k=2)
        h_src = carve(2 * G * F).rearrange("p (k s f) -> p k s f", k=2, s=G)
        h_wgt = carve(2 * G * F).rearrange("p (k s f) -> p k s f", k=2, s=G)
        hot0 = carve(2 * G * P).rearrange("p (k s n) -> p k s n", k=2, s=G)
        attr_in = carve(2 * 2 * P).rearrange("p (k q n) -> p k q n", k=2, q=2)
        attr_t = carve(2 * G * P).rearrange("p (k n) -> p k n", k=2)[0:A]
        rest_in = carve(16 * A).rearrange("p (t c) -> p t c", t=16)
        rest_t = carve(16 * P)[0:A]
        mean_in = carve(NBP * F, fresh=True).rearrange("p (b f) -> p b f", b=NBP)
        side = carve(2 * BANK).rearrange("p (k n) -> p k n", k=2)
        c_u = carve(2 * BANK).rearrange("p (k n) -> p k n", k=2)
        sq_u = carve(2 * BANK).rearrange("p (k n) -> p k n", k=2)
        h2_u = carve(2 * BANK).rearrange("p (k n) -> p k n", k=2)
        h2t_u = carve(2 * BANK).rearrange("p (k n) -> p k n", k=2)
        kv_u = carve(2 * U * 2 * F).rearrange("p (k c f) -> p k c f", k=2, c=U)
        q_f = carve(3 * 2 * U * F).rearrange("p (t k c f) -> p t k c f", t=3, k=2, c=U)
        src_ring1 = carve(2 * G, i32, fresh=True).rearrange("p (k s) -> p k s", k=2)
        kv_src = carve(2 * G * 2 * F).rearrange("p (k s t f) -> p k s t f", k=2, s=G, t=2)
        kv_edge = carve(2 * G * 2 * F).rearrange("p (k s t f) -> p k s t f", k=2, s=G, t=2)
        prod = carve(2 * HALF * F).rearrange("p (j n) -> p j n", j=2)
        hot_b = carve(2 * G * P // 2, bf16).rearrange("p (k s n) -> p k s n", k=2, s=G)
        hot_t = carve(2 * G * P // 2, bf16).rearrange("p (k s n) -> p k s n", k=2, s=G)
        attr_g = carve(2 * G * P).rearrange("p (k s e) -> p k s e", k=2, s=G)[0:A]
        line_rows = carve(NCH * P, fresh=True).rearrange("p (c e) -> p c e", c=NCH)
        line = carve(H * LINE).rearrange("p (h n) -> p h n", h=H)
        peak = carve(H * LINE).rearrange("p (h n) -> p h n", h=H)
        keys = carve(LINE + 2)
        same = carve(LINE + 1)
        apart = carve(LINE + 1)
        lead = carve(LINE)
        trail = carve(LINE)
        in_lead = carve(LINE)
        in_trail = carve(LINE)
        ends = carve(6 * 2 * H).rearrange("p (k n) -> p k n", k=6)
        ends_t = carve(8 * (P + 1)).rearrange("p (k n) -> p k n", k=8)
        v_ring = carve(4 * G * F, fresh=True).rearrange("p (k s f) -> p k s f", k=4, s=G)
        msg = carve(4 * G * F).rearrange("p (k s f) -> p k s f", k=4, s=G)
        hot1 = carve(4 * G * P).rearrange("p (k s n) -> p k s n", k=4, s=G)
        exp_ring = carve(4 * G * H).rearrange("p (k s h) -> p k s h", k=4, s=G)
        o_u = carve(NBP * F, fresh=True).rearrange("p (b f) -> p b f", b=NBP)
        ot_u = carve(2 * BANK).rearrange("p (k n) -> p k n", k=2)
        ht_u = carve(2 * BANK).rearrange("p (k n) -> p k n", k=2)
        g_u = carve(2 * BANK).rearrange("p (k n) -> p k n", k=2)

        acc = ctx.enter_context(nc.psum_tensor("acc", [P, 7 * BANK], f32))
        aside = ctx.enter_context(nc.psum_tensor("aside", [P, BANK], f32))

        def bank(b):
            return aside[:, :] if b == 7 else acc[:, b * BANK:(b + 1) * BANK]

        s_const = sem("s_const")
        s_pad = sem("s_pad")
        s_dst = sem("s_dst")
        s_x = sem("s_x")
        s_wload = sem("s_wload")
        s_gate = sem("s_gate")
        s_edges = sem("s_edges")
        s_cnt = sem("s_cnt")
        s_bound = sem("s_bound")
        s_vis = sem("s_vis")
        s_visd = sem("s_visd")
        s_visr = sem("s_visr")
        s_rows = sem("s_rows")
        s_key = sem("s_key")
        s_keyd = sem("s_keyd")
        s_tr = sem("s_tr")
        s_trc = sem("s_trc")
        s_dve = sem("s_dve")
        s_act = sem("s_act")
        s_mean = sem("s_mean")
        s_sq = sem("s_sq")
        s_var = sem("s_var")
        s_std = sem("s_std")
        s_h = sem("s_h")
        s_hd = sem("s_hd")
        s_dec = sem("s_dec")
        s_decv = sem("s_decv")
        s_wgt = sem("s_wgt")
        s_zero = sem("s_zero")
        s_bpart = sem("s_bpart")
        s_b3 = sem("s_b3")
        s_src0 = sems("s_src0_", 2)
        s_wr0 = sems("s_wr0_", 2)
        s_hot0 = sems("s_hot0_", 2)
        s_gath0 = sems("s_gath0_", 2)
        s_msg0 = sems("s_msg0_", 2)
        s_acc0 = sems("s_acc0_", 2)
        s_hop_pool = sem("s_hop_pool")
        s_hop_act = sem("s_hop_act")
        s_hop_sp = sem("s_hop_sp")
        s_hop_dve = sem("s_hop_dve")
        s_hop_pe = sem("s_hop_pe")
        s_ain = sems("s_ain", 2)
        s_atr = sem("s_atr")
        s_atc = sem("s_atc")
        s_aout = sems("s_aout", 2)
        s_rin = sem("s_rin")
        s_rest = sem("s_rest")
        s_mix_in = sem("s_mix_in")
        s_n0pe = sem("s_n0pe")
        s_n0act = sem("s_n0act")
        s_n0dve = sem("s_n0dve")
        s_n0pool = sem("s_n0pool")
        s_kvd = sems("s_kvd", 2)
        s_src1 = sems("s_src1_", 2)
        s_gath1 = sems("s_gath1_", 2)
        s_attr1 = sems("s_attr1_", 2)
        s_hot1 = sems("s_hot1_", 2)
        s_hott = sems("s_hott", 2)
        s_hotc = sems("s_hotc", 2)
        s_edge = sems("s_edge", 2)
        s_kve = sems("s_kve", 2)
        s_q = sems("s_q", 2)
        s_prod = sems("s_prod", 2)
        s_score = sems("s_score", 2)
        s_vout = sems("s_vout", 2)
        s_lt = sem("s_lt")
        s_lc = sem("s_lc")
        s_lined = sem("s_lined")
        s_line = sem("s_line")
        s_keys = sem("s_keys")
        s_ends = sem("s_ends")
        s_endt = sem("s_endt")
        s_diff = sem("s_diff")
        s_exp = sem("s_exp")
        s_share = sem("s_share")
        s_expd = sem("s_expd")
        s_expr = sem("s_expr")
        s_et = sem("s_et")
        s_ec = sem("s_ec")
        s_v = sems("s_v", 4)
        s_expc = sems("s_expc", 4)
        s_msg1 = sems("s_msg1_", 4)
        s_acc1 = sems("s_acc1_", 4)
        s_n1pe = sem("s_n1pe")
        s_n1act = sem("s_n1act")
        s_n1dve = sem("s_n1dve")
        s_out = sem("s_out")

        WEIGHTS = 14
        FULL = T - 1
        QIT = (T - 1) // 16
        REST = T - 16 * QIT
        assert QIT <= NG // 2
        RESTC = -(-REST // 4)

        def numbered(steps):
            return {s: n + 1 for n, s in enumerate(steps)}

        def ahead(first, rest):
            for u in range(-1, NU):
                if u + 1 < NU:
                    yield from ((f, u + 1) for f in first)
                if u >= 0:
                    yield from ((f, u) for f in rest)

        pe0 = numbered(ahead(["mean_t", "mix"], ["h2_t"] + [f"proj{c}" for c in range(U)]))
        act0 = numbered(ahead(["side", "std"], ["h2_side"] + [f"{f}{c}" for c in range(U) for f in ("kv", "q", "skip")]))
        dve0 = numbered([("degree", 0), ("one", 0), ("rdeg", 0)] + [("mean", u) for u in range(NU)] + [("xh", 0)]
                        + [(f, u) for u in range(NU) for f in ("x1", "sum", "mu", "centre", "square", "sum2", "var", "relu", "rstd", "h2")])
        pool0 = numbered((f, u) for u in range(NU) for f in ("part0", "left1", "part1", "left2", "part2"))
        pe1 = numbered(ahead(["o_t"], ["w1", "w2"]))
        act1 = numbered(ahead(["ot"], ["gelu1", "gelu2"]))
        dve1 = numbered([("o", u) for u in range(NU)] + [(f, u) for u in range(NU) for f in ("xo", "y")])
        LAST = len

        def table_done(eng):
            for k in range(2):
                eng.wait_ge(s_kvd[k], 16 * ((NU + 1 - k) // 2))

        def load_blocks(pe, first):
            blocks = []
            for m in (0, 4):
                blocks += nc.values_load_multi_w_load_instructions(
                    visit_row[0:1, 0, bass.ds(first + m, 4)], engines=[mybir.EngineType.PE], min_val=0, max_val=NB - 1,
                    skip_runtime_bounds_check_because="the values are clamped on the chip")[1]
            return blocks

        block = ctx.enter_context(nc.Block())


        @block.sync
        def _(sp):
            for k in range(2):
                sp.sem_inc(s_aout[k], 16)
            sp.dma_start(dst_all[0:PD, :], dst.rearrange("(p n) -> p n", p=PD)).then_inc(s_dst, 16)
            nfull = N // P
            sp.wait_ge(s_pad, 2)
            sp.dma_start(xs[:, 0:nfull, :], x[0:nfull * P, :].rearrange("(b p) f -> p b f", p=P)).then_inc(s_x, 16)
            if N % P:
                sp.dma_start(xs[0:N % P, nfull, :], x[nfull * P:N, :]).then_inc(s_x, 16)
            else:
                sp.sem_inc(s_x, 16)
            for n, a in enumerate((src, dst, edge_weight.bitcast(i32))):
                cols = slice(n * P, n * P + P)
                sp.dma_start(edges_d[0:FULL, cols], a[0:FULL * P].rearrange("(t e) -> t e", e=P)).then_inc(s_edges, 16)
                sp.dma_start(edges_d[FULL:T, n * P:n * P + TAIL], a[FULL * P:E].rearrange("(t e) -> t e", t=1)).then_inc(s_edges, 16)
                if TAIL < P:
                    sp.dma_start(edges_d[FULL:T, n * P + TAIL:n * P + P], pad_row[0:1, n * P + TAIL:n * P + P]).then_inc(s_edges, 16)
                else:
                    sp.sem_inc(s_edges, 16)
            sp.wait_ge(s_vis, 1)
            for n in range(2):
                sp.dma_start(visit_d[n, :].rearrange("(c p) -> p c", p=P), vis_i[:, 6 + n, :]).then_inc(s_visd, 16)
            sp.wait_ge(s_visd, 32)
            sp.dma_start(visit_row[:, :, :], visit_d.rearrange("(a k) n -> a k n", a=1)).then_inc(s_visr, 16)
            sp.wait_ge(s_h, 1)
            sp.dma_start(h_d.rearrange("(b p) f -> p b f", p=P), hs[:, :, :]).then_inc(s_hd, 16)
            sp.wait_ge(s_key, 1)
            sp.dma_start(key_d.rearrange("(c p) e -> p c e", p=P), key).then_inc(s_keyd, 16)
            sp.wait_ge(s_keyd, 16)

            sp.wait_ge(s_bpart, 1)
            for n in range(3):
                sp.dma_start(b_3[n:n + 1, :], b_part[0:1, n, :]).then_inc(s_b3, 16)

            sp.wait_ge(s_trc, 3 * -(-VC // U))
            sp.wait_ge(s_rows, 16 * VC)
            sp.wait_ge(s_wgt, 1)
            sp.wait_ge(s_hd, 16)
            sp.wait_ge(s_visr, 16)
            attr_q = edge_attr.rearrange("e c -> (e c)")[0:16 * QIT * P * A].rearrange("(i k q p n) -> i k q p n", i=QIT, k=2, q=2, p=P)
            attr_o = attr_d[0:16 * QIT * A, :].rearrange("(g t c) e -> g c t e", t=G, c=A)
            with sp.Fori(0, QIT) as i:
                for k in range(2):
                    sp.wait_ge(s_atr, 1 + 2 * i + k)
                    sp.sem_inc(s_hop_sp, 1)
                    sp.dma_start(attr_in[:, k, :, :], attr_q[bass.ds(i, 1), k].rearrange("i q p n -> p (i q) n")).then_inc(s_ain[k], 16)
                for k in range(2):
                    sp.wait_ge(s_atc, 1 + 2 * i + k + 1)
                    sp.sem_inc(s_hop_sp, 1)
                    sp.dma_start(attr_o[bass.ds(2 * i + k, 1)].rearrange("g c t e -> c (g t) e"),
                                 attr_t[:, k, :].rearrange("c (t e) -> c t e", t=G)).then_inc(s_aout[k], 16)
            sp.wait_ge(s_rin, 1)
            nrest = REST - 1
            if nrest:
                sp.dma_start(rest_in[:, 0:nrest, :], edge_attr[16 * QIT * P:FULL * P, :].rearrange("(t e) c -> e t c", e=P)).then_inc(s_rin, 16)
            else:
                sp.sem_inc(s_rin, 16)
            sp.dma_start(rest_in[0:TAIL, nrest, :], edge_attr[FULL * P:E, :]).then_inc(s_rin, 16)
            sp.wait_ge(s_rest, 2 * RESTC)
            sp.dma_start(attr_d[16 * QIT * A:T * A, :].rearrange("(t c) e -> c t e", c=A),
                         rest_t[:, 0:REST * P].rearrange("c (t e) -> c t e", t=REST)).then_inc(s_aout[0], 16)

            for u in range(NU):
                sp.wait_ge(s_n0act, act0[f"skip{U - 1}", u])
                sp.dma_start(kv_d[u * U * P:(u + 1) * U * P, :].rearrange("(c p) f -> p c f", p=P), kv_u[:, u % 2, :, :]).then_inc(s_kvd[u % 2], 16)
            table_done(sp)
            sp.wait_ge(s_aout[0], 16 + 16 * (QIT + 1))
            sp.wait_ge(s_aout[1], 16 + 16 * QIT)
            sp.wait_ge(s_n0dve, LAST(dve0))
            sp.wait_ge(s_n0act, LAST(act0))
            sp.wait_ge(s_n0pool, LAST(pool0))

            attr_rows = attr_d.rearrange("(t c) e -> c t e", c=A)
            with sp.Fori(0, NG // 2) as i:
                for k in range(2):
                    sp.wait_ge(s_score[k], 1 + i)
                    sp.sem_inc(s_hop_sp, 1)
                    tiles = []
                    for m in (0, 4):
                        tiles += nc.values_load_multi_w_load_instructions(
                            visit_row[0:1, 1, bass.ds(16 * i + G * k + m, 4)], engines=[mybir.EngineType.SP], min_val=0, max_val=T - 1,
                            skip_runtime_bounds_check_because="the values are clamped on the chip")[1]
                    for m, t in enumerate(tiles):
                        sp.dma_start(attr_g[:, k, m, :], attr_rows[:, bass.ds(t, 1), :].rearrange("c t e -> c (t e)")).then_inc(s_attr1[k], 16)

            for h in range(H):
                sp.wait_ge(s_lc, -(-NCH // U))
                sp.dma_start(line_d[h, :].rearrange("(c v e) -> v c e", v=CHUNK, e=P),
                             line_rows[h::H, :, :]).then_inc(s_lined, 16)
            flat = key_d.rearrange("v e -> (v e)")[0:V * P]
            sp.wait_ge(s_pad, 3)
            sp.dma_start(keys[:, 1:LINE + 1], flat.rearrange("(p n) -> p n", p=P)).then_inc(s_keys, 16)
            sp.dma_start(keys[1:P, 0:1], flat[LINE - 1:LINE - 1 + (P - 1) * LINE].rearrange("(p n) -> p n", n=LINE)[:, 0:1]).then_inc(s_keys, 16)
            sp.dma_start(keys[0:P - 1, LINE + 1:LINE + 2], flat[LINE:V * P].rearrange("(p n) -> p n", n=LINE)[:, 0:1]).then_inc(s_keys, 16)
            sp.wait_ge(s_lined, 16 * H)
            for h in range(H):
                sp.dma_start(line[:, h, :], line_d[h, :].rearrange("(p n) -> p n", p=P)).then_inc(s_line, 16)
            for h in range(H):
                sp.wait_ge(s_share, h + 1)
                sp.dma_start(exp_d[h, :].rearrange("(p n) -> p n", p=P), line[:, h, :]).then_inc(s_expd, 16)
            for h in range(H):
                sp.wait_ge(s_expd, 16 * H)
                sp.dma_start(line_rows[h::H, :, :],
                             exp_d[h, :].rearrange("(c v e) -> v c e", v=CHUNK, e=P)).then_inc(s_expr, 16)

            sp.wait_ge(s_vout[0], 16 + 16 * (NG // 2))
            sp.wait_ge(s_vout[1], 16 + 16 * (NG // 2))
            sp.wait_ge(s_et, NCH)
            with sp.Fori(0, NG // 4) as i:
                for k in range(4):
                    sp.wait_ge(s_msg1[k], 1 + i)
                    sp.sem_inc(s_hop_sp, 1)
                    sp.dma_start(v_ring[:, k, :, :], v_d[bass.ds(4 * i + k, 1)].rearrange("g p s f -> p (g s) f")).then_inc(s_v[k], 16)

            for u in range(NU):
                sp.wait_ge(s_n1dve, dve1["y", u])
                b0, b1_ = u * U, min((u + 1) * U, N // P)
                if b1_ > b0:
                    sp.dma_start(out[b0 * P:b1_ * P, :].rearrange("(b p) f -> p b f", p=P), xs[:, b0:b1_, :]).then_inc(s_out, 16)
                else:
                    sp.sem_inc(s_out, 16)
            if N % P:
                sp.dma_start(out[(N // P) * P:N, :], xs[0:N % P, N // P, :]).then_inc(s_out, 16)
                sp.wait_ge(s_out, 16 * (NU + 1))
            else:
                sp.wait_ge(s_out, 16 * NU)

        @block.gpsimd
        def _(pool):
            pool.memset(xs[:, N // P:NBP, :], 0.0).then_inc(s_pad, 1)
            pool.memset(pad_row[:, :], 0).then_inc(s_const, 1)
            pool.wait_ge(s_const, 1)
            pool.memset(pad_row[:, P:2 * P], -1).then_inc(s_pad, 1)
            pool.memset(ones[:, :], 1.0).then_inc(s_const, 1)
            pool.memset(ident[:, :], 0.0).then_inc(s_const, 1)
            pool.memset(identb[:, :], 0.0).then_inc(s_const, 1)
            pool.wait_ge(s_const, 4)
            for m in (ident, identb):
                pool.affine_select(out=m[:, :], in_=m[:, :], compare_op=ALU.not_equal, fill=1.0, base=0,
                                   pattern=[[-1, P]], channel_multiplier=1).then_inc(s_const, 1)
            pool.iota(iota[:, :], pattern=[[1, P]], base=0, channel_multiplier=0,
                      allow_small_or_imprecise_dtypes=True).then_inc(s_const, 1)
            pool.iota(vis[:, 0, :], pattern=[[P, VC]], base=0, channel_multiplier=1,
                      allow_small_or_imprecise_dtypes=True).then_inc(s_const, 1)
            pool.memset(zeros[:, :], 0.0).then_inc(s_const, 1)
            pool.memset(ones3[:, :], 1.0).then_inc(s_const, 1)
            for n, w in enumerate((wk, wv, wq, wskip)):
                pool.dma_start(w_kvqs[:, n * F:(n + 1) * F], w).then_inc(s_wload, 16)
            for n, b in enumerate((bk, bv, bq, bskip, b2)):
                pool.dma_start(b_rows[0:1, n * F:(n + 1) * F], b.rearrange("(a n) -> a n", a=1)).then_inc(s_wload, 16)
            for s, w in ((w_mix_s, w_mix), (w1_s, w1), (w2_s, w2), (we_s, we)):
                pool.dma_start(s[:, :], w).then_inc(s_wload, 16)
            pool.dma_start(b1_s[:, :], b1.rearrange("(n a) -> n a", a=1)).then_inc(s_wload, 16)
            pool.wait_ge(s_vis, 1)
            pool.wait_ge(s_edges, 16 * 9)
            for c in range(VC):
                pool.indirect_dma_start(out=edge_int[:, c, :], out_offset=None, in_=edges_d,
                                        in_offset=bass.IndirectOffsetOnAxis(ap=vis_i[:, 7, c:c + 1], axis=0)).then_inc(s_rows, 16)
            pool.wait_ge(s_hd, 16)
            pool.wait_ge(s_trc, 3 * -(-VC // U))
            pool.wait_ge(s_keyd, 16)
            with pool.Fori(0, NG // 2) as i:
                for k in range(2):
                    pool.wait_ge(s_src0[k], i + 1)
                    pool.wait_ge(s_msg0[k], 1 + i)
                    pool.sem_inc(s_hop_pool, 1)
                    for m in range(G):
                        pool.indirect_dma_start(out=h_src[:, k, m, :], out_offset=None, in_=h_d,
                                                in_offset=bass.IndirectOffsetOnAxis(ap=src_ring[:, k, m:m + 1], axis=0)).then_inc(s_gath0[k], 16)
            at0 = [0]

            def tick(name, u, ins):
                at0[0] += 1
                assert pool0[name, u] == at0[0]
                ins.then_inc(s_n0pool, 1)
                pool.wait_ge(s_n0pool, at0[0])

            for u in range(NU):
                sl, k = slice(u * U, (u + 1) * U), u % 2
                pool.wait_ge(s_n0act, act0[f"q{U - 1}", u])
                tick("part0", u, pool.tensor_copy(qs[:, sl, 0, :], q_f[:, 0, k, :, :]))
                tick("left1", u, pool.tensor_tensor(q_f[:, 1, k, :, :], q_f[:, 0, k, :, :], qs[:, sl, 0, :], ALU.subtract))
                tick("part1", u, pool.tensor_copy(qs[:, sl, 1, :], q_f[:, 1, k, :, :]))
                tick("left2", u, pool.tensor_tensor(q_f[:, 2, k, :, :], q_f[:, 1, k, :, :], qs[:, sl, 1, :], ALU.subtract))
                tick("part2", u, pool.tensor_copy(qs[:, sl, 2, :], q_f[:, 2, k, :, :]))

            table_done(pool)
            pool.wait_ge(s_n0dve, LAST(dve0))
            pool.wait_ge(s_n0act, LAST(act0))
            with pool.Fori(0, NG // 2) as i:
                for k in range(2):
                    pool.wait_ge(s_src1[k], i + 1)
                    pool.wait_ge(s_score[k], 1 + i)
                    pool.sem_inc(s_hop_pool, 1)
                    for m in range(G):
                        pool.indirect_dma_start(out=kv_src[:, k, m, :, :].rearrange("p t f -> p (t f)"), out_offset=None, in_=kv_d,
                                                in_offset=bass.IndirectOffsetOnAxis(ap=src_ring1[:, k, m:m + 1], axis=0)).then_inc(s_gath1[k], 16)
            pool.wait_ge(s_score[0], 1 + NG // 2)
            pool.wait_ge(s_score[1], 1 + NG // 2)
            pool.wait_ge(s_vout[0], 16 + 16 * (NG // 2))
            pool.wait_ge(s_vout[1], 16 + 16 * (NG // 2))
            pool.memset(keys[:, :], -2.0).then_inc(s_pad, 1)

        @block.vector
        def _(dve):
            for k in range(2):
                dve.sem_inc(s_score[k], 1)
            for k in range(2):
                dve.sem_inc(s_kve[k], 1)
            for k in range(2):
                dve.sem_inc(s_prod[k], 1)
            for k in range(4):
                dve.sem_inc(s_msg1[k], 1)
            order = [0]

            def step(ins):
                order[0] += 1
                ins.then_inc(s_dve, 1)
                dve.wait_ge(s_dve, order[0])

            V_ = nc.vector
            start, cnt = small[:, 0, :], small[:, 1, :]
            step(V_.memset(small[:, :, :], 0.0))
            dve.wait_ge(s_dst, 16)
            for b in range(1, NB):
                step(V_.tensor_scalar(below[0:PD, :], dst_all[0:PD, :], float(P * b), 0.0, ALU.is_lt, ALU.add,
                                      accum_out=cnt[0:PD, b:b + 1]))
            V_.memset(cnt[0:PD, NB:NB + 1], float(DD)).then_inc(s_cnt, 1)
            dve.wait_ge(s_x, 32)
            mean, var, rstd = stat[:, 0, :], stat[:, 1, :], stat[:, 2, :]

            def wide(a, n=F):
                return a.unsqueeze(2).to_broadcast([P, a.shape[1], n])

            step(V_.tensor_reduce(mean, xs[:, :, :], AX.X, ALU.add))
            step(V_.tensor_scalar(mean, mean, 1.0 / F, None, ALU.mult))
            V_.tensor_tensor(centred, xs[:, :, :], wide(mean), ALU.subtract).then_inc(s_mean, 1)
            dve.wait_ge(s_bound, 1)
            B = slice(0, NB)
            step(V_.tensor_copy(start[:, 0:NB + 1], bank(7)[:, 0:NB + 1]))
            end = start[:, 1:NB + 1]
            s_int, e_int, ft, cl, full, cntv, last, first, gap, dif = (small[:, n, B] for n in range(2, 12))
            si_i, ei_i = small_i[:, 12, B], small_i[:, 13, B]
            step(V_.tensor_copy(si_i, start[:, B]))
            step(V_.tensor_scalar(e_int, end, float(P - 1), None, ALU.add))
            step(V_.tensor_copy(ei_i, e_int))
            step(V_.tensor_scalar(small_i[:, 14, B], si_i, 7, None, ALU.arith_shift_right))
            step(V_.tensor_scalar(small_i[:, 15, B], ei_i, 7, None, ALU.arith_shift_right))
            step(V_.tensor_copy(ft, small_i[:, 14, B]))
            step(V_.tensor_copy(cl, small_i[:, 15, B]))
            step(V_.tensor_tensor(full, end, start[:, B], ALU.is_gt))
            step(V_.tensor_tensor(cntv, cl, ft, ALU.subtract))
            step(V_.tensor_tensor(cntv, cntv, full, ALU.mult))
            step(V_.tensor_tensor_scan(last, ones[:, B], cntv, 0.0, ALU.mult, ALU.add))
            step(V_.tensor_tensor(first, last, cntv, ALU.subtract))
            step(V_.tensor_tensor(gap, ft, first, ALU.subtract))
            dve.wait_ge(s_const, 9)
            visit, blk, tile, live, base, tmp = (vis[:, n, :] for n in range(6))
            if NB > 1:
                step(V_.tensor_tensor(dif[:, 1:NB], gap[:, 1:NB], gap[:, 0:NB - 1], ALU.subtract))
                step(V_.tensor_tensor(past, wide(visit, NB - 1), first[:, 1:NB].unsqueeze(1).to_broadcast([P, VC, NB - 1]), ALU.is_ge))
                step(V_.tensor_reduce(blk, past, AX.X, ALU.add))
                step(V_.tensor_tensor(past, past, dif[:, 1:NB].unsqueeze(1).to_broadcast([P, VC, NB - 1]), ALU.mult))
                step(V_.tensor_reduce(tile, past, AX.X, ALU.add))
            else:
                step(V_.memset(vis[:, 1:3, :], 0.0))
            step(V_.tensor_tensor(tile, tile, visit, ALU.add))
            step(V_.tensor_scalar(tile, tile, float(T - 1), 0.0, ALU.min, ALU.max))
            step(V_.tensor_scalar(live, visit, last[:, NB - 1:NB], None, ALU.is_ge))
            step(V_.tensor_scalar(tmp, live, float(1 << 22), None, ALU.mult))
            step(V_.tensor_scalar(base, blk, float(P), None, ALU.mult))
            step(V_.tensor_tensor(base, base, tmp, ALU.add))
            step(V_.tensor_copy(vis_i[:, 6, :], blk))
            V_.tensor_copy(vis_i[:, 7, :], tile).then_inc(s_vis, 1)
            dve.wait_ge(s_sq, 1)
            step(V_.tensor_reduce(var, squares, AX.X, ALU.add))
            V_.tensor_scalar(var, var, 1.0 / F, LN_EPS, ALU.mult, ALU.add).then_inc(s_var, 1)
            dve.wait_ge(s_std, 1)
            step(V_.reciprocal(rstd, stat[:, 3, :]))
            step(V_.tensor_scalar(hs[:, :, :], centred, 0.0, None, ALU.max))
            V_.tensor_tensor(hs[:, :, :], hs[:, :, :], wide(rstd), ALU.mult).then_inc(s_h, 1)
            dve.wait_ge(s_rows, 16 * VC)
            step(V_.tensor_tensor(rel, edge_int[:, :, P:2 * P], wide(base, P), ALU.subtract))
            step(V_.tensor_scalar(fits, rel, 0.0, None, ALU.is_ge))
            step(V_.scalar_tensor_tensor(fits, rel, float(P), fits, ALU.is_lt, ALU.mult))
            step(V_.scalar_tensor_tensor(key, edge_int[:, :, P:2 * P], 1.0, fits, ALU.add, ALU.mult))
            step(V_.tensor_scalar(key, key, 1.0, None, ALU.subtract))
            V_.tensor_copy(srcf, edge_int[:, :, 0:P]).then_inc(s_key, 1)
            dve.wait_ge(s_dec, 1)
            g = gate
            step(V_.tensor_scalar(g[:, 4:5], g[:, 3:4], 1e-6, None, ALU.add))
            step(V_.reciprocal(g[:, 5:6], g[:, 4:5]))
            dve.wait_ge(s_trc, 3 * -(-VC // U))
            wv_ = wgt_e[:, 0:V]
            step(V_.tensor_scalar(decay, wv_, g[:, 5:6], 0.0, ALU.mult, ALU.max))
            step(V_.tensor_tensor(decay, decay, decay, ALU.mult))
            step(V_.tensor_scalar(sig, wv_, g[:, 1:2], g[:, 2:3], ALU.mult, ALU.add))
            V_.memset(ok, 0.0).then_inc(s_decv, 1)
            dve.wait_ge(s_dec, 2)
            step(V_.tensor_scalar(sig, sig, 1.0, None, ALU.add))
            step(V_.reciprocal(sig, sig))
            step(V_.tensor_tensor(decay, decay, sig, ALU.mult))
            step(V_.tensor_scalar(ok, decay, FLT_MAX, None, ALU.is_le))
            step(V_.tensor_scalar(sig, decay, -FLT_MAX, None, ALU.is_ge))
            step(V_.tensor_tensor(ok, ok, sig, ALU.mult))
            step(V_.memset(wv_, 0.0))
            V_.copy_predicated(wv_, ok.bitcast(i32), decay).then_inc(s_wgt, 1)
            dve.wait_ge(s_wgt, 1)

            dve.wait_ge(s_wload, 16 * WEIGHTS)
            step(V_.tensor_copy(b_part[:, 0, :], b_rows[:, :]))
            step(V_.tensor_tensor(b_left[:, 0, :], b_rows[:, :], b_part[:, 0, :], ALU.subtract))
            step(V_.tensor_copy(b_part[:, 1, :], b_left[:, 0, :]))
            step(V_.tensor_tensor(b_left[:, 1, :], b_left[:, 0, :], b_part[:, 1, :], ALU.subtract))
            V_.tensor_copy(b_part[:, 2, :], b_left[:, 1, :]).then_inc(s_bpart, 1)

            dve.wait_ge(s_keyd, 16)
            dve.wait_ge(s_hd, 16)
            dve.wait_ge(s_visr, 16)
            V_.memset(rest_in, 0.0).then_inc(s_rin, 1)
            with dve.Fori(0, NG // 2) as i:
                for k in range(2):
                    at = bass.ds(16 * i + G * k, G)
                    dve.wait_ge(s_msg0[k], 1 + i)
                    V_.tensor_copy(src_ring[:, k, :], src_e[:, at]).then_inc(s_src0[k], 1)
                    V_.tensor_copy(wgt_ring[:, k, :], wgt_e[:, at]).then_inc(s_wr0[k], 1)
                    dve.wait_ge(s_acc0[k], 1 + i)
                    V_.tensor_tensor(hot0[:, k, :, :], iota[:, :].unsqueeze(1).to_broadcast([P, G, P]),
                                     slot_e[:, at].unsqueeze(2).to_broadcast([P, G, P]), ALU.is_equal).then_inc(s_hot0[k], 1)

            at0 = [0]

            def tick(name, u, ins, chained=True):
                at0[0] += 1
                assert dve0[name, u] == at0[0]
                ins.then_inc(s_n0dve, 1)
                if chained:
                    dve.wait_ge(s_n0dve, at0[0])

            for k in range(2):
                dve.wait_ge(s_acc0[k], 1 + NG // 2)
            dve.wait_ge(s_rest, 2 * RESTC)
            dve.wait_ge(s_aout[0], 16 + 16 * (QIT + 1))
            dve.wait_ge(s_aout[1], 16 + 16 * QIT)
            tick("degree", 0, V_.tensor_scalar(degree[:, :], acc[:, STATS:STATS + NB], 1.0, None, ALU.max))
            tick("one", 0, V_.memset(stat[:, 0, :], 1.0))
            tick("rdeg", 0, V_.reciprocal(stat[:, 0, 0:NB], degree[:, :]))
            for u in range(NU):
                tick("mean", u, V_.tensor_tensor(mean_in[:, u * U:(u + 1) * U, :], bank(u).rearrange("p (b f) -> p b f", b=U),
                                                 wide(stat[:, 0, u * U:(u + 1) * U]), ALU.mult), chained=False)
            tick("xh", 0, V_.tensor_tensor(xs[:, :, :], xs[:, :, :], hs[:, :, :], ALU.add))

            def second_norm(u):
                sl, k = slice(u * U, (u + 1) * U), u % 2
                c3, q3, h3 = (a[:, k, :].rearrange("p (b f) -> p b f", b=U) for a in (c_u, sq_u, h2_u))
                m4, v4, d4, r4 = (stat[:, n, sl] for n in range(4))
                dve.wait_ge(s_n0pe, pe0["mix", u])
                tick("x1", u, V_.tensor_tensor(xs[:, sl, :], bank(u).rearrange("p (b f) -> p b f", b=U), xs[:, sl, :], ALU.add))
                tick("sum", u, V_.tensor_reduce(m4, xs[:, sl, :], AX.X, ALU.add))
                tick("mu", u, V_.tensor_scalar(m4, m4, 1.0 / F, None, ALU.mult))
                tick("centre", u, V_.tensor_tensor(c3, xs[:, sl, :], wide(m4), ALU.subtract))
                tick("square", u, V_.tensor_tensor(q3, c3, c3, ALU.mult))
                tick("sum2", u, V_.tensor_reduce(v4, q3, AX.X, ALU.add))
                tick("var", u, V_.tensor_scalar(v4, v4, 1.0 / F, LN_EPS, ALU.mult, ALU.add))
                tick("relu", u, V_.tensor_scalar(c3, c3, 0.0, None, ALU.max))
                dve.wait_ge(s_n0act, act0["std", u])
                tick("rstd", u, V_.reciprocal(r4, d4))
                if u >= 2:
                    dve.wait_ge(s_n0pe, pe0["h2_t", u - 2])
                tick("h2", u, V_.tensor_tensor(h3, c3, wide(r4), ALU.mult), chained=False)

            for u in range(NU):
                second_norm(u)

            table_done(dve)
            dve.wait_ge(s_n0act, LAST(act0))
            dve.wait_ge(s_n0pool, LAST(pool0))
            V_.memset(src_e[:, VC * P:VC * P + G], 0)
            V_.tensor_copy(src_ring1[:, 0, :], src_e[:, 0:G]).then_inc(s_src1[0], 1)
            with dve.Fori(0, NG // 2) as i:
                for k in range(2):
                    g_ = 2 * i + k
                    V_.tensor_copy(src_ring1[:, 1 - k, :], src_e[:, bass.ds(16 * i + G * k + G, G)]).then_inc(s_src1[1 - k], 1)
                    V_.tensor_tensor(hot_b[:, k, :, :], iota[:, :].unsqueeze(1).to_broadcast([P, G, P]),
                                     slot_e[:, bass.ds(16 * i + G * k, G)].unsqueeze(2).to_broadcast([P, G, P]),
                                     ALU.is_equal).then_inc(s_hot1[k], 1)
                    dve.wait_ge(s_vout[k], 16 + 16 * i)
                    dve.wait_ge(s_gath1[k], 16 * G * i + 16 * G)
                    for j in range(2):
                        part = slice(HALF * j, HALF * (j + 1))
                        dve.wait_ge(s_edge[j], g_ + 1)
                        V_.tensor_tensor(kv_edge[:, k, part, :, :], kv_src[:, k, part, :, :],
                                         bank(4 + j).rearrange("p (s f) -> p s f", s=HALF).unsqueeze(2).to_broadcast([P, HALF, 2, F]),
                                         ALU.add).then_inc(s_kve[j], 1)
                        dve.wait_ge(s_kve[j], 1 + g_ + 1)
                        dve.wait_ge(s_q[j], g_ + 1)
                        V_.tensor_tensor(prod[:, j, :].rearrange("p (s f) -> p s f", s=HALF), kv_edge[:, k, part, 0, :],
                                         bank(2 + j).rearrange("p (s f) -> p s f", s=HALF), ALU.mult).then_inc(s_prod[j], 1)
                        dve.wait_ge(s_prod[j], 1 + g_ + 1)
                        red = V_.tensor_reduce(score[:, bass.ds(16 * i + G * k + HALF * j, HALF), :],
                                               prod[:, j, :].rearrange("p (s h c) -> p s h c", s=HALF, h=H), AX.X, ALU.add)
                    red.then_inc(s_score[k], 1)

            R = slice(None, None, -1)
            dve.wait_ge(s_keys, 48)
            step(V_.tensor_tensor(same, keys[:, 0:LINE + 1], keys[:, 1:LINE + 2], ALU.is_equal))
            step(V_.tensor_scalar(apart, same, BIG, BIG, ALU.mult, ALU.subtract))
            step(V_.tensor_tensor_scan(lead, apart[:, 0:LINE], apart[:, 0:LINE], 0.0, ALU.min, ALU.min))
            step(V_.tensor_tensor_scan(trail[:, R], apart[:, LINE:0:-1], apart[:, LINE:0:-1], 0.0, ALU.min, ALU.min))
            step(V_.tensor_scalar(in_lead, lead, 0.0, None, ALU.is_equal))
            step(V_.tensor_scalar(in_trail, trail, 0.0, None, ALU.is_equal))
            step(V_.memset(ends, 0.0))

            def carried_back(h):
                step(V_.tensor_tensor_scan(peak[:, h, R], apart[:, LINE:0:-1], peak[:, h, R], -BIG, ALU.add, ALU.max))
                step(V_.tensor_copy(ends[:, 0, h:h + 1], peak[:, h, LINE - 1:LINE]))
                V_.tensor_copy(ends[:, 1, h:h + 1], peak[:, h, 0:1])

            def across(turn, from_before, from_behind, op, nothing):
                step(V_.memset(ends_t[0:H, :, :], nothing))
                for h in range(H):
                    step(V_.tensor_copy(ends[:, 2, h:h + 1], from_before[:, LINE - 1:LINE]))
                    step(V_.tensor_copy(ends[:, 3, h:h + 1], from_behind[:, 0:1]))
                V_.memset(ends[:, 5, :], 0.0).then_inc(s_ends, 1)
                dve.wait_ge(s_endt, 2 * turn + 1)
                step(V_.tensor_copy(ends_t[0:H, 0:4, 0:P], bank(7)[0:H, :].rearrange("h (n p) -> h n p", n=4)))
                step(V_.tensor_tensor_scan(ends_t[0:H, 4, 1:P + 1], ends_t[0:H, 2, 0:P], ends_t[0:H, 0, 0:P], nothing, *op))
                step(V_.tensor_tensor_scan(ends_t[0:H, 5, P - 1::-1], ends_t[0:H, 3, P - 1::-1], ends_t[0:H, 1, P - 1::-1], nothing, *op))
                V_.memset(ends[:, 5, :], 0.0).then_inc(s_ends, 1)
                dve.wait_ge(s_endt, 2 * turn + 2)
                step(V_.tensor_copy(ends[:, 4, 0:2 * H], bank(7)[:, 0:2 * H]))

            for h in range(H):
                dve.wait_ge(s_line, 16 * H)
                step(V_.tensor_tensor_scan(peak[:, h, :], apart[:, 0:LINE], line[:, h, :], -BIG, ALU.add, ALU.max))
                carried_back(h)
            across(0, lead, trail, (ALU.add, ALU.max), -BIG)
            for h in range(H):
                step(V_.scalar_tensor_tensor(peak[:, h, :], lead, ends[:, 4, h:h + 1], peak[:, h, :], ALU.add, ALU.max))
                step(V_.scalar_tensor_tensor(peak[:, h, :], trail, ends[:, 4, H + h:H + h + 1], peak[:, h, :], ALU.add, ALU.max))
                V_.tensor_tensor(line[:, h, :], line[:, h, :], peak[:, h, :], ALU.subtract).then_inc(s_diff, 1)
            for h in range(H):
                dve.wait_ge(s_exp, h + 1)
                step(V_.tensor_tensor_scan(peak[:, h, :], same[:, 0:LINE], line[:, h, :], 0.0, ALU.mult, ALU.add))
                carried_back(h)
            across(1, in_lead, in_trail, (ALU.mult, ALU.add), 0.0)
            for h in range(H):
                total = peak[:, h, :]
                step(V_.scalar_tensor_tensor(total, in_lead, ends[:, 4, h:h + 1], total, ALU.mult, ALU.add))
                step(V_.scalar_tensor_tensor(total, in_trail, ends[:, 4, H + h:H + h + 1], total, ALU.mult, ALU.add))
                step(V_.tensor_scalar(total, total, 1e-16, None, ALU.add))
                step(V_.reciprocal(total, total))
                V_.tensor_tensor(line[:, h, :], line[:, h, :], total, ALU.mult).then_inc(s_share, 1)

            dve.wait_ge(s_et, NCH)
            with dve.Fori(0, NG // 4) as i:
                for k in range(4):
                    dve.wait_ge(s_acc1[k], 1 + i)
                    V_.tensor_tensor(hot1[:, k, :, :], iota[:, :].unsqueeze(1).to_broadcast([P, G, P]),
                                     slot_e[:, bass.ds(32 * i + G * k, G)].unsqueeze(2).to_broadcast([P, G, P]), ALU.is_equal)
                    dve.wait_ge(s_v[k], 16 * i + 16)
                    dve.wait_ge(s_expc[k], i + 1)
                    V_.tensor_tensor(msg[:, k, :, :].rearrange("p s (h c) -> p (s h) c", h=H),
                                     v_ring[:, k, :, :].rearrange("p s (h c) -> p (s h) c", h=H),
                                     exp_ring[:, k, :, :].rearrange("p s h -> p (s h)").unsqueeze(2).to_broadcast([P, G * H, C]),
                                     ALU.mult).then_inc(s_msg1[k], 1)

            at1 = [0]

            def tock(name, u, ins, chained=True):
                at1[0] += 1
                assert dve1[name, u] == at1[0]
                ins.then_inc(s_n1dve, 1)
                if chained:
                    dve.wait_ge(s_n1dve, at1[0])

            for k in range(4):
                dve.wait_ge(s_acc1[k], 1 + NG // 4)
            for u in range(NU):
                sl = slice(u * U, (u + 1) * U)
                tock("o", u, V_.tensor_tensor(o_u[:, sl, :], bank(u).rearrange("p (b f) -> p b f", b=U), hs[:, sl, :], ALU.add))
            for u in range(NU):
                sl, k = slice(u * U, (u + 1) * U), u % 2
                tock("xo", u, V_.tensor_tensor(xs[:, sl, :], xs[:, sl, :], o_u[:, sl, :], ALU.add))
                dve.wait_ge(s_n1act, act1["gelu2", u])
                tock("y", u, V_.tensor_tensor(xs[:, sl, :], xs[:, sl, :], g_u[:, k, :].rearrange("p (b f) -> p b f", b=U), ALU.add), chained=False)

        @block.scalar
        def _(act):
            for k in range(2):
                act.sem_inc(s_msg0[k], 1)
            act.sem_inc(s_atc, 1)
            for k in range(2):
                act.sem_inc(s_vout[k], 16)
            S_ = nc.scalar
            for n, a in enumerate((log_scale, filter_w, filter_b)):
                act.dma_start(gate[:, n:n + 1], a.rearrange("(a n) -> a n", a=1).to_broadcast([P, 1])).then_inc(s_gate, 16)
            act.wait_ge(s_gate, 48)
            S_.activation(gate[:, 3:4], gate[:, 0:1], ACT.Exp).then_inc(s_dec, 1)
            act.wait_ge(s_mean, 1)
            S_.activation(squares, centred, ACT.Square).then_inc(s_sq, 1)
            act.wait_ge(s_var, 1)
            S_.activation(stat[:, 3, :], stat[:, 1, :], ACT.Sqrt).then_inc(s_std, 1)
            n = 0
            for dest in (slot_e, src_e, wgt_e):
                for c in range(0, VC, U):
                    w = min(U, VC - c) * P
                    act.wait_ge(s_tr, n + 1)
                    S_.activation(dest[:, c * P:c * P + w], bank(n % 7)[:, 0:w], ACT.Copy).then_inc(s_trc, 1)
                    n += 1
            act.wait_ge(s_decv, 1)
            S_.activation(decay, decay, ACT.Exp, scale=-1.0).then_inc(s_act, 1)
            S_.activation(sig, sig, ACT.Exp, scale=-1.0).then_inc(s_dec, 1)
            act.wait_ge(s_act, 1)

            act.wait_ge(s_keyd, 16)

            def messages(i, k):
                act.wait_ge(s_gath0[k], 16 * G * i + 16 * G)
                act.wait_ge(s_wr0[k], i + 1)
                act.wait_ge(s_acc0[k], 1 + i)
                act.sem_inc(s_hop_act, 1)
                for m in range(G):
                    ins = S_.activation(h_wgt[:, k, m, :], h_src[:, k, m, :], ACT.Copy, scale=wgt_ring[:, k, m:m + 1])
                ins.then_inc(s_msg0[k], 1)

            with act.Fori(0, QIT) as i:
                for k in range(2):
                    messages(i, k)
                    act.wait_ge(s_atr, 1 + 2 * i + k + 1)
                    act.wait_ge(s_aout[k], 16 + 16 * i)
                    act.sem_inc(s_hop_act, 1)
                    for j in range(4):
                        ins = S_.activation(attr_t[:, k, :].rearrange("c (t r j) -> c t r j", t=G, j=4)[:, :, :, j],
                                            aside[32 * j:32 * j + A, 0:2 * P].rearrange("c (t r) -> c t r", t=G), ACT.Copy)
                    ins.then_inc(s_atc, 1)
            for i in range(QIT, NG // 2):
                for k in range(2):
                    messages(i, k)
            for n in range(RESTC):
                w = min(4, REST - 4 * n) * P
                act.wait_ge(s_rest, 2 * n + 1)
                S_.activation(rest_t[:, 4 * n * P:4 * n * P + w], aside[0:A, 0:w], ACT.Copy).then_inc(s_rest, 1)

            act.wait_ge(s_n0dve, dve0["xh", 0])
            at0 = [0]

            def tick(name, u, ins):
                at0[0] += 1
                assert act0[name, u] == at0[0]
                ins.then_inc(s_n0act, 1)

            def side_std(u):
                act.wait_ge(s_n0pe, pe0["mean_t", u])
                tick("side", u, S_.activation(side[:, u % 2, :], bank(u), ACT.Copy))
                act.wait_ge(s_n0dve, dve0["var", u])
                tick("std", u, S_.activation(stat[:, 2, u * U:(u + 1) * U], stat[:, 1, u * U:(u + 1) * U], ACT.Sqrt))

            side_std(0)
            for u in range(NU):
                k = u % 2
                if u + 1 < NU:
                    side_std(u + 1)
                act.wait_ge(s_n0pe, pe0["h2_t", u])
                tick("h2_side", u, S_.activation(h2t_u[:, k, :], bank(u), ACT.Copy))
                if u >= 2:
                    act.wait_ge(s_kvd[k], 16 * (u // 2))
                for c in range(U):
                    b = u * U + c
                    dest = bank(7) if c % 2 == 0 else bank(u)
                    act.wait_ge(s_n0pe, pe0[f"proj{c}", u])
                    tick(f"kv{c}", u, S_.activation(kv_u[:, k, c, :], dest[:, 0:2 * F], ACT.Copy))
                    if u >= 2:
                        act.wait_ge(s_n0pool, pool0["part2", u - 2])
                    tick(f"q{c}", u, S_.activation(q_f[:, 0, k, c, :], dest[:, 2 * F:3 * F], ACT.Copy))
                    tick(f"skip{c}", u, S_.activation(hs[:, b, :], dest[:, 3 * F:4 * F], ACT.Copy))

            act.wait_ge(s_n0act, LAST(act0))
            table_done(act)
            act.wait_ge(s_n0pool, LAST(pool0))
            with act.Fori(0, NG // 2) as i:
                for k in range(2):
                    for j in range(2):
                        act.wait_ge(s_hott[j], 2 * i + k + 1)
                        act.sem_inc(s_hop_act, 1)
                        S_.activation(hot_t[:, k, HALF * j:HALF * (j + 1), :],
                                      bank(j).bitcast(bf16)[:, 0:HALF * P].rearrange("p (s e) -> p s e", s=HALF), ACT.Copy).then_inc(s_hotc[j], 1)
                    act.wait_ge(s_kve[1], 1 + 2 * i + k + 1)
                    act.sem_inc(s_hop_act, 1)
                    act.dma_start(v_d[bass.ds(2 * i + k, 1)].rearrange("g p s f -> p (g s) f"), kv_edge[:, k, :, 1, :]).then_inc(s_vout[k], 16)

            for k in range(2):
                act.wait_ge(s_score[k], 1 + NG // 2)
                act.wait_ge(s_vout[k], 16 + 16 * (NG // 2))
            for n in range(0, NCH, U):
                w = min(U, NCH - n)
                act.wait_ge(s_lt, min(n + U, NCH))
                S_.activation(line_rows[:, n:n + w, :], bank(n // U)[:, 0:w * P].rearrange("p (c e) -> p c e", c=w), ACT.Copy).then_inc(s_lc, 1)
            for h in range(H):
                act.wait_ge(s_diff, h + 1)
                S_.activation(line[:, h, :], line[:, h, :], ACT.Exp, scale=float(C) ** -0.5).then_inc(s_exp, 1)
            for n in range(NCH):
                act.wait_ge(s_et, n + 1)
                S_.activation(score[:, CHUNK * n:CHUNK * (n + 1), :].rearrange("p v h -> p (v h)"), bank(n % 7)[:, 0:P], ACT.Copy).then_inc(s_ec, 1)

            act.wait_ge(s_ec, NCH)
            with act.Fori(0, NG // 4) as i:
                for k in range(4):
                    act.wait_ge(s_acc1[k], 1 + i)
                    act.sem_inc(s_hop_act, 1)
                    S_.activation(exp_ring[:, k, :, :], score[:, bass.ds(32 * i + G * k, G), :], ACT.Copy).then_inc(s_expc[k], 1)

            at1 = [0]

            def tock(name, u, ins):
                at1[0] += 1
                assert act1[name, u] == at1[0]
                ins.then_inc(s_n1act, 1)

            def o_side(u):
                act.wait_ge(s_n1pe, pe1["o_t", u])
                tock("ot", u, S_.activation(ot_u[:, u % 2, :], bank(u), ACT.Copy))

            o_side(0)
            for u in range(NU):
                k = u % 2
                if u + 1 < NU:
                    o_side(u + 1)
                act.wait_ge(s_n1pe, pe1["w1", u])
                tock("gelu1", u, S_.activation(ht_u[:, k, :], bank(u), ACT.Gelu_apprx_tanh, bias=b1_s[:, 0:1]))
                act.wait_ge(s_n1pe, pe1["w2", u])
                if u >= 2:
                    act.wait_ge(s_n1dve, dve1["y", u - 2])
                tock("gelu2", u, S_.activation(g_u[:, k, :], bank(u), ACT.Gelu_apprx_tanh))

        @block.tensor
        def _(pe):
            for k in range(2):
                pe.sem_inc(s_acc0[k], 1)
            pe.sem_inc(s_atr, 1)
            for k in range(4):
                pe.sem_inc(s_acc1[k], 1)
            T_ = nc.tensor
            pe.wait_ge(s_const, 10)
            pe.wait_ge(s_cnt, 1)
            T_.matmul(bank(7)[:, 0:NB + 1], ones[0:PD, :], small[0:PD, 1, 0:NB + 1], start=True, stop=True).then_inc(s_bound, 1)
            pe.wait_ge(s_key, 1)
            n = 0
            for rows in (rel, srcf, edge_rows[:, :, 2 * P:3 * P]):
                for c in range(0, VC, U):
                    w = min(U, VC - c)
                    if n >= 7:
                        pe.wait_ge(s_trc, n - 6)
                    for m in range(w):
                        ins = T_.transpose(bank(n % 7)[:, m * P:(m + 1) * P], rows[:, c + m, :], ident[:, :])
                    ins.then_inc(s_tr, 1)
                    n += 1
            pe.wait_ge(s_trc, n)

            def open_blocks():
                for u in range(-(-(STATS + NB) // BANK)):
                    ins = T_.matmul(bank(u), zeros[:, 0:P], zeros[:, :], start=True, stop=True)
                ins.then_inc(s_zero, 1)

            open_blocks()
            pe.wait_ge(s_visr, 16)

            def sum0(i, k):
                pe.wait_ge(s_hot0[k], i + 1)
                pe.wait_ge(s_msg0[k], 1 + i + 1)
                for m, b in enumerate(load_blocks(pe, 16 * i + G * k)):
                    T_.matmul(acc[:, bass.ds(b * P, P)], hot0[:, k, m, :], h_wgt[:, k, m, :], start=False, stop=True, skip_group_check=True)
                    ins = T_.matmul(acc[:, bass.ds(b + STATS, 1)], hot0[:, k, m, :], ones[:, 0:1], start=False, stop=True, skip_group_check=True)
                ins.then_inc(s_acc0[k], 1)

            with pe.Fori(0, QIT) as i:
                for k in range(2):
                    pe.wait_ge(s_ain[k], 16 * i + 16)
                    pe.wait_ge(s_atc, 1 + 2 * i + k)
                    for q in range(2):
                        ins = T_.transpose(aside[:, q * P:(q + 1) * P], attr_in[:, k, q, :], ident[:, :])
                    ins.then_inc(s_atr, 1)
                    sum0(i, k)
            for i in range(QIT, NG // 2):
                for k in range(2):
                    sum0(i, k)
            pe.wait_ge(s_rin, 33)
            pe.wait_ge(s_atc, 1 + 2 * QIT)
            for n in range(RESTC):
                if n:
                    pe.wait_ge(s_rest, 2 * n)
                for m in range(min(4, REST - 4 * n)):
                    ins = T_.transpose(aside[0:A, m * P:(m + 1) * P], rest_in[:, 4 * n + m, :], ident[:, :])
                ins.then_inc(s_rest, 1)
            pe.wait_ge(s_rest, 2 * RESTC)

            pe.wait_ge(s_wload, 16 * WEIGHTS)
            pe.wait_ge(s_b3, 48)
            at0 = [0]

            def tick(name, u, ins):
                at0[0] += 1
                assert pe0[name, u] == at0[0]
                ins.then_inc(s_n0pe, 1)

            def mix(u):
                pe.wait_ge(s_n0dve, dve0["mean", u])
                for c in range(U):
                    ins = T_.transpose(bank(u)[:, c * P:(c + 1) * P], mean_in[:, u * U + c, :], ident[:, :])
                tick("mean_t", u, ins)
                pe.wait_ge(s_n0act, act0["side", u])
                for c in range(U):
                    ins = T_.matmul(bank(u)[:, c * F:(c + 1) * F], side[:, u % 2, c * P:(c + 1) * P], w_mix_s[:, :], start=True, stop=True)
                tick("mix", u, ins)

            mix(0)
            for u in range(NU):
                if u + 1 < NU:
                    mix(u + 1)
                pe.wait_ge(s_n0dve, dve0["h2", u])
                for c in range(U):
                    ins = T_.transpose(bank(u)[:, c * P:(c + 1) * P], h2_u[:, u % 2, c * P:(c + 1) * P], ident[:, :])
                tick("h2_t", u, ins)
                pe.wait_ge(s_n0act, act0["h2_side", u])
                for c in range(U):
                    b = u * U + c
                    if b >= 2:
                        pe.wait_ge(s_n0act, act0[f"skip{(b - 2) % U}", (b - 2) // U])
                    dest = bank(7) if c % 2 == 0 else bank(u)
                    T_.matmul(dest, ones3[:, :], b_3[:, 0:4 * F], start=True, stop=False)
                    tick(f"proj{c}", u, T_.matmul(dest, h2t_u[:, u % 2, c * P:(c + 1) * P], w_kvqs[:, :], start=False, stop=True))

            pe.wait_ge(s_n0act, LAST(act0))
            pe.wait_ge(s_n0pool, LAST(pool0))
            pe.wait_ge(s_n0dve, LAST(dve0))
            with pe.Fori(0, NG // 2) as i:
                for k in range(2):
                    g_ = 2 * i + k
                    blocks = load_blocks(pe, 16 * i + G * k)
                    pe.wait_ge(s_hot1[k], i + 1)
                    for j in range(2):
                        for m in range(HALF):
                            ins = T_.transpose(bank(j).bitcast(bf16)[:, m * P:(m + 1) * P], hot_b[:, k, HALF * j + m, :], identb[:, :])
                        ins.then_inc(s_hott[j], 1)
                        if j == 0:
                            pe.wait_ge(s_attr1[k], 16 * G * i + 16 * G)
                        pe.wait_ge(s_kve[j], 1 + g_)
                        for m in range(HALF):
                            ins = T_.matmul(bank(4 + j)[:, m * F:(m + 1) * F], attr_g[:, k, HALF * j + m, :], we_s[:, :], start=True, stop=True)
                        ins.then_inc(s_edge[j], 1)
                        pe.wait_ge(s_hotc[j], g_ + 1)
                        pe.wait_ge(s_prod[j], 1 + g_)
                        for m in range(HALF):
                            b = blocks[HALF * j + m]
                            for t in range(3):
                                ins = T_.matmul(bank(2 + j)[:, m * F:(m + 1) * F], hot_t[:, k, HALF * j + m, :],
                                                qs[:, bass.ds(b, 1), t, :].rearrange("p b f -> p (b f)"), start=t == 0, stop=t == 2)
                        ins.then_inc(s_q[j], 1)

            for k in range(2):
                pe.wait_ge(s_score[k], 1 + NG // 2)
            for n in range(NCH):
                T_.transpose(bank(n // U)[:, (n % U) * P:(n % U + 1) * P], score[:, CHUNK * n:CHUNK * (n + 1), :].rearrange("p v h -> p (v h)"), ident[:, :]).then_inc(s_lt, 1)
            for turn in range(2):
                pe.wait_ge(s_ends, 2 * turn + 1)
                for n in range(4):
                    ins = T_.transpose(bank(7)[0:H, n * P:(n + 1) * P], ends[:, n, 0:H], ident[:, :])
                ins.then_inc(s_endt, 1)
                pe.wait_ge(s_ends, 2 * turn + 2)
                T_.transpose(bank(7)[:, 0:H], ends_t[0:H, 4, 0:P], ident[0:H, 0:H])
                T_.transpose(bank(7)[:, H:2 * H], ends_t[0:H, 5, 1:P + 1], ident[0:H, 0:H]).then_inc(s_endt, 1)
            pe.wait_ge(s_expr, 16 * H)
            pe.wait_ge(s_lc, -(-NCH // U))
            for n in range(NCH):
                if n >= 7:
                    pe.wait_ge(s_ec, n - 6)
                T_.transpose(bank(n % 7)[:, 0:P], line_rows[:, n, :], ident[:, :]).then_inc(s_et, 1)
            pe.wait_ge(s_ec, NCH)

            open_blocks()
            with pe.Fori(0, NG // 4) as i:
                for k in range(4):
                    pe.wait_ge(s_msg1[k], 1 + i + 1)
                    for m, b in enumerate(load_blocks(pe, 32 * i + G * k)):
                        ins = T_.matmul(acc[:, bass.ds(b * P, P)], hot1[:, k, m, :], msg[:, k, m, :], start=False, stop=True, skip_group_check=True)
                    ins.then_inc(s_acc1[k], 1)

            at1 = [0]

            def tock(name, u, ins):
                at1[0] += 1
                assert pe1[name, u] == at1[0]
                ins.then_inc(s_n1pe, 1)

            def o_t(u):
                pe.wait_ge(s_n1dve, dve1["o", u])
                for c in range(U):
                    ins = T_.transpose(bank(u)[:, c * P:(c + 1) * P], o_u[:, u * U + c, :], ident[:, :])
                tock("o_t", u, ins)

            o_t(0)
            for u in range(NU):
                k = u % 2
                if u + 1 < NU:
                    o_t(u + 1)
                pe.wait_ge(s_n1act, act1["ot", u])
                tock("w1", u, T_.matmul(bank(u), w1_s[:, :], ot_u[:, k, :], start=True, stop=True))
                pe.wait_ge(s_n1act, act1["gelu1", u])
                for c in range(U):
                    T_.matmul(bank(u)[:, c * F:(c + 1) * F], ones3[:, :], b_3[:, 4 * F:5 * F], start=True, stop=False)
                    ins = T_.matmul(bank(u)[:, c * F:(c + 1) * F], ht_u[:, k, c * P:(c + 1) * P], w2_s[:, :], start=False, stop=True)
                tock("w2", u, ins)


_INS = ['x', 'src', 'dst', 'edge_attr_32', 'edge_weight', 'L0_gnn_W_mix', 'L0_gnn_log_scale', 'L0_gnn_filter_w',
        'L0_gnn_filter_b', 'L1_gnn_Wq', 'L1_gnn_bq', 'L1_gnn_Wk', 'L1_gnn_bk', 'L1_gnn_Wv', 'L1_gnn_bv', 'L1_gnn_We',
        'L1_gnn_Wskip', 'L1_gnn_bskip', 'L1_gnn_W1', 'L1_gnn_b1', 'L1_gnn_W2', 'L1_gnn_b2']


def kernel(**inputs):
    import numpy as np
    import concourse.bacc as bacc
    from concourse.bass_utils import run_bass_kernel_spmd

    nc = bacc.Bacc("TRN2", target_bir_lowering=False, num_devices=1)
    arrays, args = {}, []
    for name in _INS:
        a = np.ascontiguousarray(inputs[name])
        a = a.reshape(1) if a.ndim == 0 else a
        arrays[f"in_{name}"] = a
        args.append(nc.dram_tensor(f"in_{name}", a.shape, mybir.dt.from_np(a.dtype), kind="ExternalInput").ap())
    shape = tuple(inputs['x'].shape)
    out = nc.dram_tensor("out", shape, mybir.dt.float32, kind="ExternalOutput").ap()
    gnn_kernel(nc, *args, out)
    r = run_bass_kernel_spmd(nc, [arrays], core_ids=[0])
    return r.results[0]["out"]
```

```python
import concourse.bass as bass
from concourse import mybir
from contextlib import ExitStack

P = 128
F = 128
H = 4
C = F // H
A = 32
G = 8
HALF = G // 2
BANK = 512
U = BANK // F
BIG = 1.0e30
FLT_MAX = 3.4028234e38
LN_EPS = 1e-5


def gnn_kernel(nc, x, src, dst, edge_attr, edge_weight, w_mix, log_scale, filter_w, filter_b,
               wq, bq, wk, bk, wv, bv, we, wskip, bskip, w1, b1, w2, b2, out):
    f32, bf16, i32 = mybir.dt.float32, mybir.dt.bfloat16, mybir.dt.int32
    ALU, ACT, AX = mybir.AluOpType, mybir.ActivationFunctionType, mybir.AxisListType

    N, E = x.shape[0], src.shape[0]
    NB = -(-N // P)
    NU = -(-NB // U)
    NBP = NU * U
    T = -(-E // P)
    TAIL = E - (T - 1) * P
    V = -(-(T + NB - 1) // 32) * 32
    VC = -(-V // P)
    NG = V // G
    PD = max(p for p in range(1, P + 1) if E % p == 0)
    DD = E // PD
    LINE = V * P // P
    CHUNK = P // H
    NCH = V // CHUNK
    STATS = NB * P
    assert CHUNK == 4 * G and NG * G == NCH * CHUNK
    assert NU <= 7 and STATS + NB <= 7 * BANK and NB <= 32 and N < 1 << 24

    edges_d = nc.dram_tensor("edges_d", (T, 3 * P), i32).ap()
    h_d = nc.dram_tensor("h_d", (NB * P, F), f32).ap()
    kv_d = nc.dram_tensor("kv_d", (NB * P, 2 * F), f32).ap()
    attr_d = nc.dram_tensor("attr_d", (T * A, P), f32).ap()
    v_d = nc.dram_tensor("v_d", (NG, P, G, F), f32).ap()
    key_d = nc.dram_tensor("key_d", (VC * P, P), f32).ap()
    line_d = nc.dram_tensor("line_d", (H, V * P), f32).ap()
    share_d = nc.dram_tensor("share_d", (H, V * P), f32).ap()
    visit_d = nc.dram_tensor("visit_d", (2, VC * P), i32).ap()
    spare_d = nc.dram_tensor("spare_d", (4, 32), f32).ap()

    ctx = ExitStack()
    with ctx:
        ctx.enter_context(nc.allow_non_contiguous_dma(reason="a few hundred single words"))

        def sb(name, shape, dt=f32):
            return ctx.enter_context(nc.sbuf_tensor(name, shape, dt))

        def sem(name):
            return ctx.enter_context(nc.semaphore(name))

        def sems(name, n):
            return [sem(f"{name}{k}") for k in range(n)]

        ACTB = NB * 3 // 4
        ACTS = 3

        ident = sb("ident", [P, P])
        identb = sb("identb", [P, P], bf16)
        iota = sb("iota", [P, P])
        ones = sb("ones", [P, P])
        zeros = sb("zeros", [P, BANK], bf16)
        w_kvqs = sb("w_kvqs", [P, 4 * F])
        b_rows = sb("b_rows", [1, 5 * F])
        b_part = sb("b_part", [1, 3, 5 * F], bf16)
        b_left = sb("b_left", [1, 2, 5 * F])
        b_3 = sb("b_3", [3, 5 * F], bf16)
        ones3 = sb("ones3", [3, P], bf16)
        w_mix_s = sb("w_mix_s", [P, F])
        w1_s = sb("w1_s", [P, F])
        w2_s = sb("w2_s", [P, F])
        b1_s = sb("b1_s", [P, 1])
        we_s = sb("we_s", [A, F])
        gate = sb("gate", [P, 8])
        xs = sb("xs", [P, NBP, F])
        hs = sb("hs", [P, NBP, F])
        qs = sb("qs", [P, NBP, 3, F], bf16)
        slot_e = sb("slot_e", [P, VC * P + G])
        src_e = sb("src_e", [P, VC * P + 4 * G], i32)
        wgt_e = sb("wgt_e", [P, VC * P])
        visit_row = sb("visit_row", [1, 2, VC * P], i32)
        score = sb("score", [P, V, H])
        stat = sb("stat", [P, 4, NBP])
        spare_row = sb("spare_row", [1, 32])
        small_stat = sb("small_stat", [P, 2, 4, U])
        degree = sb("degree", [P, NB])

        keys = sb("keys", [P, LINE + 2])[:, :]
        same = sb("same", [P, LINE + 1])[:, :]
        apart = sb("apart", [P, LINE + 1])[:, :]
        lead = sb("lead", [P, LINE])[:, :]
        trail = sb("trail", [P, LINE])[:, :]
        in_lead = sb("in_lead", [P, LINE])[:, :]
        in_trail = sb("in_trail", [P, LINE])[:, :]

        ARENA = 17600
        arena = sb("arena", [P, ARENA])
        used = [0]

        def carve(words, dt=f32, fresh=False):
            if fresh:
                used[0] = 0
            view = arena[:, used[0]:used[0] + words]
            used[0] += words
            assert used[0] <= ARENA, used[0]
            return view if dt is f32 else view.bitcast(dt)

        edge_rows = carve(VC * 3 * P, fresh=True).rearrange("p (c n) -> p c n", c=VC)
        edge_int = edge_rows.bitcast(i32)
        dst_all = carve(DD, i32)
        dst_blk = carve(DD // 2 + 1, bf16)[:, 0:DD]
        below = carve(DD // 2 + 1, bf16)[:, 0:DD]
        rel = carve(VC * P).rearrange("p (c e) -> p c e", c=VC)
        fits = carve(VC * P).rearrange("p (c e) -> p c e", c=VC)
        key = carve(VC * P).rearrange("p (c e) -> p c e", c=VC)
        srcf = carve(VC * P).rearrange("p (c e) -> p c e", c=VC)
        past = carve(VC * (NB - 1)).rearrange("p (c b) -> p c b", c=VC)
        small = carve(24 * 32).rearrange("p (k b) -> p k b", b=32)
        small_i = small.bitcast(i32)
        vis = carve(8 * VC).rearrange("p (k c) -> p k c", k=8)
        vis_i = vis.bitcast(i32)
        pad_row = carve(3 * P, i32)
        centred = carve(NBP * F).rearrange("p (b f) -> p b f", b=NBP)
        qs_words = qs[:, :, :, :].rearrange("p b t f -> p (b t f)").bitcast(f32)
        squares = qs_words[:, 0:NBP * F].rearrange("p (b f) -> p b f", b=NBP)
        rest_in = qs_words[:, NBP * F:NBP * F + 16 * A].rearrange("p (t c) -> p t c", t=16)
        assert 3 * VC * P <= V * H
        decay, sig, ok = (score[:, :, :].rearrange("p v h -> p (v h)")[:, n * VC * P:(n + 1) * VC * P] for n in range(3))
        wgt_rows = wgt_e[:, :].rearrange("p (c e) -> p c e", c=VC)
        src_ring = carve(2 * G, i32, fresh=True).rearrange("p (k s) -> p k s", k=2)
        wgt_ring = carve(2 * G).rearrange("p (k s) -> p k s", k=2)
        h_src = carve(2 * G * F).rearrange("p (k s f) -> p k s f", k=2, s=G)
        h_wgt = carve(2 * G * F).rearrange("p (k s f) -> p k s f", k=2, s=G)
        hot0 = carve(2 * G * P).rearrange("p (k s n) -> p k s n", k=2, s=G)
        attr_in = carve(2 * 2 * P).rearrange("p (k q n) -> p k q n", k=2, q=2)
        attr_t = carve(2 * G * P).rearrange("p (k n) -> p k n", k=2)[0:A]
        rest_t = carve(16 * P)[0:A]
        mean_in = carve(NBP * F, fresh=True).rearrange("p (b f) -> p b f", b=NBP)
        side = carve(2 * BANK).rearrange("p (k n) -> p k n", k=2)
        c_u = carve(2 * BANK).rearrange("p (k n) -> p k n", k=2)
        sq_u = carve(2 * BANK).rearrange("p (k n) -> p k n", k=2)
        h2_u = carve(2 * BANK).rearrange("p (k n) -> p k n", k=2)
        KV_RING = 4 * G + 4 * G * 2 * F
        carve(max(0, KV_RING - used[0]))
        h2t = carve(NBP * F).rearrange("p (u n) -> p u n", u=NU)
        q_left = carve(2 * 2 * U * F).rearrange("p (t k c f) -> p t k c f", t=2, k=2, c=U)
        kv_u = carve(2 * U * 2 * F).rearrange("p (k c f) -> p k c f", k=2, c=U)
        src_ring1 = carve(4 * G, i32, fresh=True).rearrange("p (k s) -> p k s", k=4)
        kv_src = carve(4 * G * 2 * F).rearrange("p (k s t f) -> p k s t f", k=4, s=G, t=2)
        kv_edge = carve(2 * G * 2 * F).rearrange("p (k s t f) -> p k s t f", k=2, s=G, t=2)
        prod = carve(2 * HALF * F).rearrange("p (j n) -> p j n", j=2)
        hot_b = carve(2 * G * P // 2, bf16).rearrange("p (k s n) -> p k s n", k=2, s=G)
        hot_t = carve(2 * G * P // 2, bf16).rearrange("p (k s n) -> p k s n", k=2, s=G)
        attr_g = carve(2 * G * P).rearrange("p (k s e) -> p k s e", k=2, s=G)[0:A]
        line_rows = carve((NCH + 1) * P, fresh=True).rearrange("p (c e) -> p c e", c=NCH + 1)
        line = carve(H * LINE).rearrange("p (h n) -> p h n", h=H)
        peak = carve(H * LINE).rearrange("p (h n) -> p h n", h=H)
        ends = carve(6 * 2 * H).rearrange("p (k n) -> p k n", k=6)
        ends_t = carve(8 * (P + 1)).rearrange("p (k n) -> p k n", k=8)
        carve((NCH + 1) * P, fresh=True)
        v_ring = carve(4 * G * F).rearrange("p (k s f) -> p k s f", k=4, s=G)
        msg = carve(4 * G * F).rearrange("p (k s f) -> p k s f", k=4, s=G)
        hot1 = carve(4 * G * P).rearrange("p (k s n) -> p k s n", k=4, s=G)
        chunk_rows = carve(P)
        share = carve(4 * G * H).rearrange("p (k s h) -> p k s h", k=4, s=G)
        neg_slot = carve(4 * G).rearrange("p (k s) -> p k s", k=4)
        o_u = carve(NBP * F, fresh=True).rearrange("p (b f) -> p b f", b=NBP)
        ot_u = carve(2 * BANK).rearrange("p (k n) -> p k n", k=2)
        ht_u = carve(2 * BANK).rearrange("p (k n) -> p k n", k=2)
        g_u = carve(2 * BANK).rearrange("p (k n) -> p k n", k=2)

        acc = ctx.enter_context(nc.psum_tensor("acc", [P, 7 * BANK], f32))
        aside = ctx.enter_context(nc.psum_tensor("aside", [P, BANK], f32))

        def bank(b):
            return aside[:, :] if b == 7 else acc[:, b * BANK:(b + 1) * BANK]

        def q_bank(u):
            return acc[:, (u % 3) * 2 * BANK:(u % 3 + 1) * 2 * BANK].rearrange("p (c f) -> p c f", c=U)

        s_const = sem("s_const")
        s_pad = sem("s_pad")
        s_spare = sem("s_spare")
        s_dst = sem("s_dst")
        s_x = sem("s_x")
        s_wload = sem("s_wload")
        s_gate = sem("s_gate")
        s_edges = sem("s_edges")
        s_cnt = sem("s_cnt")
        s_bound = sem("s_bound")
        s_vis = sem("s_vis")
        s_visd = sem("s_visd")
        s_visr = sem("s_visr")
        s_rows = sem("s_rows")
        s_key = sem("s_key")
        s_keyd = sem("s_keyd")
        s_tr = sem("s_tr")
        s_trc = sem("s_trc")
        s_dve = sem("s_dve")
        s_act = sem("s_act")
        s_sq = sem("s_sq")
        s_var = sem("s_var")
        s_std = sem("s_std")
        s_h = sem("s_h")
        s_hv = sem("s_hv")
        s_hd = sem("s_hd")
        s_dec = sem("s_dec")
        s_decv = sem("s_decv")
        s_wgt = sem("s_wgt")
        s_bpart = sem("s_bpart")
        s_b3 = sem("s_b3")
        s_src0 = sems("s_src0_", 2)
        s_wr0 = sems("s_wr0_", 2)
        s_hot0 = sems("s_hot0_", 2)
        s_gath0 = sems("s_gath0_", 2)
        s_msg0 = sems("s_msg0_", 2)
        s_acc0 = sems("s_acc0_", 2)
        s_hop_pool = sem("s_hop_pool")
        s_hop_act = sem("s_hop_act")
        s_hop_sp = sem("s_hop_sp")
        s_ain = sems("s_ain", 2)
        s_atr = sem("s_atr")
        s_atc = sem("s_atc")
        s_aout = sems("s_aout", 2)
        s_rin = sem("s_rin")
        s_rout = sem("s_rout")
        s_mean = sem("s_mean")
        s_rstd = sem("s_rstd")
        s_rest = sem("s_rest")
        s_n0pe = sem("s_n0pe")
        s_n0act = sem("s_n0act")
        s_n0dve = sem("s_n0dve")
        s_kvd = sems("s_kvd", 2)
        s_src1 = sems("s_src1_", 4)
        s_gath1 = sems("s_gath1_", 4)
        s_attr1 = sems("s_attr1_", 2)
        s_hot1 = sems("s_hot1_", 2)
        s_hott = sems("s_hott", 2)
        s_hotc = sems("s_hotc", 2)
        s_edge = sems("s_edge", 2)
        s_kve = sems("s_kve", 2)
        s_q = sems("s_q", 2)
        s_prod = sems("s_prod", 2)
        s_score = sem("s_score")
        s_vout = sems("s_vout", 2)
        s_lt = sem("s_lt")
        s_lc = sem("s_lc")
        s_lined = sems("s_lined", H)
        s_line = sems("s_line", H)
        s_keys = sem("s_keys")
        s_ends = sem("s_ends")
        s_endt = sem("s_endt")
        s_diff = sem("s_diff")
        s_exp = sem("s_exp")
        s_share = sem("s_share")
        s_shared = sems("s_shared", H)
        s_shareb = sem("s_shareb")
        s_shart = sem("s_shart")
        s_v = sems("s_v", 4)
        s_chunk = sem("s_chunk")
        s_sharec = sems("s_sharec", 4)
        s_neg = sems("s_neg", 4)
        s_sqr = sems("s_sqr", 4)
        s_hota = sems("s_hota", 4)
        s_msg1 = sems("s_msg1_", 4)
        s_acc1 = sems("s_acc1_", 4)
        s_n1pe = sem("s_n1pe")
        s_n1act = sem("s_n1act")
        s_n1dve = sem("s_n1dve")
        s_out = sem("s_out")

        TRC = -(-VC // U)
        WEIGHTS = 14
        FULL = T - 1
        QIT = (T - 1) // 16
        REST = T - 16 * QIT
        assert QIT <= NG // 2
        RESTC = -(-REST // 4)

        def numbered(steps):
            return {s: n + 1 for n, s in enumerate(steps)}

        def ahead(first, rest):
            for u in range(-1, NU):
                if u + 1 < NU:
                    yield from ((f, u + 1) for f in first)
                if u >= 0:
                    yield from ((f, u) for f in rest)

        no_kv1 = ("kv1", NU - 1) if NB - (NU - 1) * U <= 2 else None

        def kv_end(u):
            return ("kv0", u) if ("kv1", u) == no_kv1 else ("kv1", u)

        pe0 = numbered([(f, u) for f in ("mean_t", "mix") for u in range(min(2, NU))]
                       + [(f, n) for u in range(NU)
                          for f, n in (("h2_t", u), ("mean_t", u + 2), ("kv0", u), ("kv1", u), ("mix", u + 2)) if n < NU and (f, n) != no_kv1]
                       + [("q", u) for u in range(NU)])
        act0 = numbered([("mean", u) for u in range(min(2, NU))] + [("side", u) for u in range(min(2, NU))]
                        + [("mean", u) for u in range(2, min(3, NU))] + [("square", 0), ("std", 0)]
                        + [(f, n) for u in range(NU)
                           for f, n in (("h2_side", u), ("side", u + 2), ("square", u + 1), ("std", u + 1), ("kv0", u), ("kv1", u),
                                        ("mean", u + 3)) if n < NU and (f, n) != no_kv1]
                        + [(f, n) for u in range(NU + 2)
                           for f, n in (("skip", u), ("part0", u), ("part1", u - 1), ("part2", u - 2)) if 0 <= n < NU])
        dve0 = numbered([("degree", 0), ("one", 0), ("rdeg", 0)]
                        + [(f, u) for u in range(NU) for f in ("x1", "sum", "mu", "centre", "relu", "var", "rstd", "h2")]
                        + [(f, n) for u in range(NU + 1) for f, n in (("left1", u), ("left2", u - 1)) if 0 <= n < NU])
        pe1 = numbered(ahead(["o_t"], ["w1", "w2"]))
        act1 = numbered(ahead(["ot"], ["gelu1", "gelu2"]))
        dve1 = numbered([("o", u) for u in range(NU)] + [(f, u) for u in range(NU) for f in ("xo", "y")])

        def blocks_of(u):
            n = min(U, NB - u * U)
            return n, slice(u * U, u * U + n)

        LAST = len

        def table_done(eng):
            for k in range(2):
                eng.wait_ge(s_kvd[k], 16 * ((NU + 1 - k) // 2))

        def line_in(eng, first):
            eng.wait_ge(s_lc, -(-NCH // U))
            for h in range(first, H, 2):
                eng.dma_start(line_d[h, :].rearrange("(c v e) -> v c e", v=CHUNK, e=P), line_rows[h::H, 0:NCH, :]).then_inc(s_lined[h], 16)
            for h in range(first, H, 2):
                eng.wait_ge(s_lined[h], 16)
                eng.dma_start(line[:, h, :], line_d[h, :].rearrange("(p n) -> p n", p=P)).then_inc(s_line[h], 16)

        def load_blocks(pe, first):
            return nc.values_load_multi_w_load_instructions(
                visit_row[0:1, 0, bass.ds(first, G)], engines=[mybir.EngineType.PE], min_val=0, max_val=NB - 1,
                skip_runtime_bounds_check_because="a count of NB - 1 comparisons")[1]

        block = ctx.enter_context(nc.Block())


        @block.sync
        def _(sp):
            sp.dma_start(dst_all[0:PD, :], dst.rearrange("(p n) -> p n", p=PD)).then_inc(s_dst, 16)
            nfull = N // P
            sp.wait_ge(s_pad, 2)
            sp.dma_start(xs[:, 0:nfull, :], x[0:nfull * P, :].rearrange("(b p) f -> p b f", p=P)).then_inc(s_x, 16)
            if N % P:
                sp.dma_start(xs[0:N % P, nfull, :], x[nfull * P:N, :]).then_inc(s_x, 16)
            else:
                sp.sem_inc(s_x, 16)
            sp.wait_ge(s_rin, 1)
            nrest = REST - 1
            if nrest:
                sp.dma_start(rest_in[:, 0:nrest, :], edge_attr[16 * QIT * P:FULL * P, :].rearrange("(t e) c -> e t c", e=P)).then_inc(s_rin, 16)
            else:
                sp.sem_inc(s_rin, 16)
            sp.dma_start(rest_in[0:TAIL, nrest, :], edge_attr[FULL * P:E, :]).then_inc(s_rin, 16)
            for n, a in enumerate((src, dst, edge_weight.bitcast(i32))):
                cols = slice(n * P, n * P + P)
                sp.dma_start(edges_d[0:FULL, cols], a[0:FULL * P].rearrange("(t e) -> t e", e=P)).then_inc(s_edges, 16)
                sp.dma_start(edges_d[FULL:T, n * P:n * P + TAIL], a[FULL * P:E].rearrange("(t e) -> t e", t=1)).then_inc(s_edges, 16)
                if TAIL < P:
                    sp.dma_start(edges_d[FULL:T, n * P + TAIL:n * P + P], pad_row[0:1, n * P + TAIL:n * P + P]).then_inc(s_edges, 16)
                else:
                    sp.sem_inc(s_edges, 16)
            sp.wait_ge(s_spare, 1)
            for k in range(2):
                sp.dma_start(spare_d[k:k + 1, :], spare_row[0:1, :]).then_inc(s_aout[k], 16)
                sp.dma_start(spare_d[2 + k:3 + k, :], spare_row[0:1, :]).then_inc(s_vout[k], 16)
            sp.wait_ge(s_vis, 1)
            for n in range(2):
                sp.dma_start(visit_d[n, :].rearrange("(c p) -> p c", p=P), vis_i[:, 6 + n, :]).then_inc(s_visd, 16)
            sp.wait_ge(s_visd, 32)
            sp.dma_start(visit_row[:, :, :], visit_d.rearrange("(a k) n -> a k n", a=1)).then_inc(s_visr, 16)
            def store_h(b0, b1_):
                sp.dma_start(h_d[b0 * P:b1_ * P, :].rearrange("(b p) f -> p b f", p=P), hs[:, b0:b1_, :]).then_inc(s_hd, 16)

            sp.wait_ge(s_h, 1)
            store_h(0, ACTB // 2)
            sp.wait_ge(s_key, 1)
            sp.dma_start(key_d.rearrange("(c p) e -> p c e", p=P), key).then_inc(s_keyd, 16)
            sp.wait_ge(s_h, 2)
            store_h(ACTB // 2, ACTB)
            sp.wait_ge(s_hv, 1)
            store_h(ACTB, NB)
            sp.wait_ge(s_keyd, 16)
            flat = key_d.rearrange("v e -> (v e)")[0:V * P]
            sp.wait_ge(s_pad, 3)
            sp.dma_start(keys[:, 1:LINE + 1], flat.rearrange("(p n) -> p n", p=P)).then_inc(s_keys, 16)
            sp.dma_start(keys[1:P, 0:1], flat[LINE - 1:LINE - 1 + (P - 1) * LINE].rearrange("(p n) -> p n", n=LINE)[:, 0:1]).then_inc(s_keys, 16)
            sp.dma_start(keys[0:P - 1, LINE + 1:LINE + 2], flat[LINE:V * P].rearrange("(p n) -> p n", n=LINE)[:, 0:1]).then_inc(s_keys, 16)

            sp.wait_ge(s_trc, 2 * TRC)
            sp.wait_ge(s_hd, 48)
            sp.wait_ge(s_visr, 16)
            sp.wait_ge(s_rest, 2 * RESTC)
            sp.dma_start(attr_d[16 * QIT * A:T * A, :].rearrange("(t c) e -> c t e", c=A),
                         rest_t[:, 0:REST * P].rearrange("c (t e) -> c t e", t=REST)).then_inc(s_rout, 16)
            attr_q = edge_attr.rearrange("e c -> (e c)")[0:16 * QIT * P * A].rearrange("(i k q p n) -> i k q p n", i=QIT, k=2, q=2, p=P)
            attr_o = attr_d[0:16 * QIT * A, :].rearrange("(g t c) e -> g c t e", t=G, c=A)
            with sp.Fori(0, QIT) as i:
                for k in range(2):
                    sp.wait_ge(s_atr, 1 + 2 * i + k)
                    sp.sem_inc(s_hop_sp, 1)
                    sp.dma_start(attr_in[:, k, :, :], attr_q[bass.ds(i, 1), k].rearrange("i q p n -> p (i q) n")).then_inc(s_ain[k], 16)
                for k in range(2):
                    sp.wait_ge(s_atc, 1 + 2 * i + k + 1)
                    sp.sem_inc(s_hop_sp, 1)
                    sp.dma_start(attr_o[bass.ds(2 * i + k, 1)].rearrange("g c t e -> c (g t) e"),
                                 attr_t[:, k, :].rearrange("c (t e) -> c t e", t=G)).then_inc(s_aout[k], 16)
            sp.wait_ge(s_bpart, 1)
            for n in range(3):
                sp.dma_start(b_3[n:n + 1, :], b_part[0:1, n, :]).then_inc(s_b3, 16)

            for u in range(NU):
                sp.wait_ge(s_n0act, act0[kv_end(u)])
                n, _ = blocks_of(u)
                sp.dma_start(kv_d[u * U * P:(u * U + n) * P, :].rearrange("(c p) f -> p c f", p=P), kv_u[:, u % 2, 0:n, :]).then_inc(s_kvd[u % 2], 16)
            table_done(sp)
            sp.wait_ge(s_rout, 16)
            sp.wait_ge(s_aout[0], 16 + 16 * QIT)
            sp.wait_ge(s_aout[1], 16 + 16 * QIT)
            sp.wait_ge(s_n0dve, dve0["h2", NU - 1])
            sp.wait_ge(s_n0pe, pe0[kv_end(NU - 1)])

            attr_rows = attr_d.rearrange("(t c) e -> c t e", c=A)
            with sp.Fori(0, NG // 2) as i:
                for k in range(2):
                    sp.wait_ge(s_kve[1], 1 + 2 * i + k)
                    sp.sem_inc(s_hop_sp, 1)
                    tiles = nc.values_load_multi_w_load_instructions(
                        visit_row[0:1, 1, bass.ds(16 * i + G * k, G)], engines=[mybir.EngineType.SP], min_val=0, max_val=T - 1,
                        skip_runtime_bounds_check_because="the values are clamped on the chip")[1]
                    for m, t in enumerate(tiles):
                        sp.dma_start(attr_g[:, k, m, :], attr_rows[:, bass.ds(t, 1), :].rearrange("c t e -> c (t e)")).then_inc(s_attr1[k], 16)

            line_in(sp, 0)
            for h in range(H):
                sp.wait_ge(s_share, h + 1)
                sp.dma_start(share_d[h, :].rearrange("(p n) -> p n", p=P), line[:, h, :]).then_inc(s_shared[h], 16)
                sp.wait_ge(s_shared[h], 16)
                sp.dma_start(line_rows[h::H, 0:NCH, :],
                             share_d[h, :].rearrange("(c v e) -> v c e", v=CHUNK, e=P)).then_inc(s_shareb, 16)

            sp.wait_ge(s_vout[0], 16 + 16 * (NG // 2))
            sp.wait_ge(s_vout[1], 16 + 16 * (NG // 2))
            with sp.Fori(0, NG // 4) as i:
                for k in range(4):
                    sp.wait_ge(s_msg1[k], 1 + i)
                    sp.sem_inc(s_hop_sp, 1)
                    sp.dma_start(v_ring[:, k, :, :], v_d[bass.ds(4 * i + k, 1)].rearrange("g p s f -> p (g s) f")).then_inc(s_v[k], 16)

            for u in range(NU):
                sp.wait_ge(s_n1dve, dve1["y", u])
                b0, b1_ = u * U, min((u + 1) * U, N // P)
                if b1_ > b0:
                    sp.dma_start(out[b0 * P:b1_ * P, :].rearrange("(b p) f -> p b f", p=P), xs[:, b0:b1_, :]).then_inc(s_out, 16)
                else:
                    sp.sem_inc(s_out, 16)
            if N % P:
                sp.dma_start(out[(N // P) * P:N, :], xs[0:N % P, N // P, :]).then_inc(s_out, 16)
                sp.wait_ge(s_out, 16 * (NU + 1))
            else:
                sp.wait_ge(s_out, 16 * NU)

        @block.gpsimd
        def _(pool):
            pool.memset(spare_row[:, :], 0.0).then_inc(s_spare, 1)
            pool.memset(xs[:, N // P:NBP, :], 0.0).then_inc(s_pad, 1)
            pool.memset(pad_row[:, :], 0).then_inc(s_const, 1)
            pool.wait_ge(s_const, 1)
            pool.memset(pad_row[:, P:2 * P], -1).then_inc(s_pad, 1)
            pool.memset(ones[:, :], 1.0).then_inc(s_const, 1)
            pool.memset(ident[:, :], 0.0).then_inc(s_const, 1)
            pool.memset(identb[:, :], 0.0).then_inc(s_const, 1)
            pool.wait_ge(s_const, 4)
            for m in (ident, identb):
                pool.affine_select(out=m[:, :], in_=m[:, :], compare_op=ALU.not_equal, fill=1.0, base=0,
                                   pattern=[[-1, P]], channel_multiplier=1).then_inc(s_const, 1)
            pool.iota(iota[:, :], pattern=[[1, P]], base=0, channel_multiplier=0,
                      allow_small_or_imprecise_dtypes=True).then_inc(s_const, 1)
            pool.iota(vis[:, 0, :], pattern=[[P, VC]], base=0, channel_multiplier=1,
                      allow_small_or_imprecise_dtypes=True).then_inc(s_const, 1)
            pool.memset(zeros[:, :], 0.0).then_inc(s_const, 1)
            pool.memset(ones3[:, :], 1.0).then_inc(s_const, 1)
            pool.memset(keys[:, :], -2.0).then_inc(s_pad, 1)
            for n, w in enumerate((wk, wv, wq, wskip)):
                pool.dma_start(w_kvqs[:, n * F:(n + 1) * F], w).then_inc(s_wload, 16)
            for n, b in enumerate((bk, bv, bq, bskip, b2)):
                pool.dma_start(b_rows[0:1, n * F:(n + 1) * F], b.rearrange("(a n) -> a n", a=1)).then_inc(s_wload, 16)
            for s, w in ((w_mix_s, w_mix), (w1_s, w1), (w2_s, w2), (we_s, we)):
                pool.dma_start(s[:, :], w).then_inc(s_wload, 16)
            pool.dma_start(b1_s[:, :], b1.rearrange("(n a) -> n a", a=1)).then_inc(s_wload, 16)
            pool.wait_ge(s_vis, 1)
            pool.wait_ge(s_edges, 16 * 9)
            for c in range(VC):
                pool.indirect_dma_start(out=edge_int[:, c, :], out_offset=None, in_=edges_d,
                                        in_offset=bass.IndirectOffsetOnAxis(ap=vis_i[:, 7, c:c + 1], axis=0)).then_inc(s_rows, 16)
            pool.wait_ge(s_hd, 48)
            pool.wait_ge(s_trc, 2 * TRC)
            pool.wait_ge(s_keyd, 16)
            with pool.Fori(0, NG // 2) as i:
                for k in range(2):
                    pool.wait_ge(s_src0[k], i + 1)
                    pool.sem_inc(s_hop_pool, 1)
                    for m in range(G):
                        pool.indirect_dma_start(out=h_src[:, k, m, :], out_offset=None, in_=h_d,
                                                in_offset=bass.IndirectOffsetOnAxis(ap=src_ring[:, k, m:m + 1], axis=0)).then_inc(s_gath0[k], 16)
            table_done(pool)
            pool.wait_ge(s_n0dve, dve0["h2", NU - 1])
            pool.wait_ge(s_n0pe, pe0[kv_end(NU - 1)])
            with pool.Fori(0, NG // 4) as i:
                for k in range(4):
                    pool.wait_ge(s_src1[k], i + 1)
                    pool.sem_inc(s_hop_pool, 1)
                    for m in range(G):
                        pool.indirect_dma_start(out=kv_src[:, k, m, :, :].rearrange("p t f -> p (t f)"), out_offset=None, in_=kv_d,
                                                in_offset=bass.IndirectOffsetOnAxis(ap=src_ring1[:, k, m:m + 1], axis=0)).then_inc(s_gath1[k], 16)
            pool.wait_ge(s_score, NG)
            for k in range(2):
                pool.wait_ge(s_vout[k], 16 + 16 * (NG // 2))
            pool.memset(line_rows[:, NCH, :], 0.0).then_inc(s_pad, 1)

            pool.wait_ge(s_shareb, 16 * H)
            pool.wait_ge(s_pad, 4)
            with pool.Fori(0, NCH) as i:
                pool.wait_ge(s_shart, i + 1)
                pool.sem_inc(s_hop_pool, 1)
                pool.tensor_copy(chunk_rows, line_rows[:, bass.ds(i + 1, 1), :].rearrange("p c e -> p (c e)")).then_inc(s_chunk, 1)

        @block.vector
        def _(dve):
            for k in range(2):
                dve.sem_inc(s_kve[k], 2)
            for k in range(2):
                dve.sem_inc(s_prod[k], 1)
            for k in range(4):
                dve.sem_inc(s_msg1[k], 1)
            order = [0]

            def step(ins):
                order[0] += 1
                ins.then_inc(s_dve, 1)
                dve.wait_ge(s_dve, order[0])

            V_ = nc.vector
            start, cnt = small[:, 0, :], small[:, 1, :]
            step(V_.memset(small[:, :, :], 0.0))
            V_.memset(rest_in, 0.0).then_inc(s_rin, 1)
            V_.memset(src_e[:, VC * P:], 0)
            V_.memset(slot_e[:, VC * P:], 0.0)
            dve.wait_ge(s_dst, 16)
            step(V_.tensor_scalar(dst_all[0:PD, :], dst_all[0:PD, :], 7, None, ALU.arith_shift_right))
            step(V_.tensor_copy(dst_blk[0:PD, :], dst_all[0:PD, :]))
            for b in range(1, NB):
                step(V_.tensor_scalar(below[0:PD, :], dst_blk[0:PD, :], float(b), 0.0, ALU.is_lt, ALU.add,
                                      accum_out=cnt[0:PD, b:b + 1]))
            V_.memset(cnt[0:PD, NB:NB + 1], float(DD)).then_inc(s_cnt, 1)
            dve.wait_ge(s_x, 32)
            mean, var, rstd = stat[:, 0, :], stat[:, 1, :], stat[:, 2, :]

            def wide(a, n=F):
                return a.unsqueeze(2).to_broadcast([P, a.shape[1], n])

            step(V_.tensor_reduce(mean, xs[:, :, :], AX.X, ALU.add))
            step(V_.tensor_scalar(mean, mean, 1.0 / F, None, ALU.mult))
            dve.wait_ge(s_bound, 1)
            B = slice(0, NB)
            step(V_.tensor_copy(start[:, 0:NB + 1], bank(7)[:, 0:NB + 1]))
            end = start[:, 1:NB + 1]
            s_int, e_int, ft, cl, full, cntv, last, first, gap, dif = (small[:, n, B] for n in range(2, 12))
            si_i, ei_i = small_i[:, 12, B], small_i[:, 13, B]
            step(V_.tensor_copy(si_i, start[:, B]))
            step(V_.tensor_scalar(e_int, end, float(P - 1), None, ALU.add))
            step(V_.tensor_copy(ei_i, e_int))
            step(V_.tensor_scalar(small_i[:, 14, B], si_i, 7, None, ALU.arith_shift_right))
            step(V_.tensor_scalar(small_i[:, 15, B], ei_i, 7, None, ALU.arith_shift_right))
            step(V_.tensor_copy(ft, small_i[:, 14, B]))
            step(V_.tensor_copy(cl, small_i[:, 15, B]))
            step(V_.tensor_tensor(full, end, start[:, B], ALU.is_gt))
            step(V_.tensor_tensor(cntv, cl, ft, ALU.subtract))
            step(V_.tensor_tensor(cntv, cntv, full, ALU.mult))
            step(V_.tensor_tensor_scan(last, ones[:, B], cntv, 0.0, ALU.mult, ALU.add))
            step(V_.tensor_tensor(first, last, cntv, ALU.subtract))
            step(V_.tensor_tensor(gap, ft, first, ALU.subtract))
            dve.wait_ge(s_const, 9)
            visit, blk, tile, live, base, tmp = (vis[:, n, :] for n in range(6))
            if NB > 1:
                step(V_.tensor_tensor(dif[:, 1:NB], gap[:, 1:NB], gap[:, 0:NB - 1], ALU.subtract))
                step(V_.tensor_tensor(past, wide(visit, NB - 1), first[:, 1:NB].unsqueeze(1).to_broadcast([P, VC, NB - 1]), ALU.is_ge))
                step(V_.tensor_reduce(blk, past, AX.X, ALU.add))
                step(V_.tensor_tensor(past, past, dif[:, 1:NB].unsqueeze(1).to_broadcast([P, VC, NB - 1]), ALU.mult))
                step(V_.tensor_reduce(tile, past, AX.X, ALU.add))
            else:
                step(V_.memset(vis[:, 1:3, :], 0.0))
            step(V_.tensor_tensor(tile, tile, visit, ALU.add))
            step(V_.tensor_scalar(tile, tile, float(T - 1), 0.0, ALU.min, ALU.max))
            step(V_.tensor_scalar(live, visit, last[:, NB - 1:NB], None, ALU.is_ge))
            step(V_.tensor_scalar(tmp, live, float(1 << 22), None, ALU.mult))
            step(V_.tensor_scalar(base, blk, float(P), None, ALU.mult))
            step(V_.tensor_tensor(base, base, tmp, ALU.add))
            step(V_.tensor_copy(vis_i[:, 6, :], blk))
            V_.tensor_copy(vis_i[:, 7, :], tile).then_inc(s_vis, 1)
            V_.tensor_tensor(centred, xs[:, :, :], wide(mean), ALU.subtract).then_inc(s_mean, 1)
            dve.wait_ge(s_rows, 16 * VC)
            step(V_.tensor_tensor(rel, edge_int[:, :, P:2 * P], wide(base, P), ALU.subtract))
            step(V_.tensor_scalar(fits, rel, 0.0, None, ALU.is_ge))
            step(V_.scalar_tensor_tensor(fits, rel, float(P), fits, ALU.is_lt, ALU.mult))
            dve.wait_ge(s_sq, 1)
            V_.tensor_scalar(var, var, 1.0 / F, LN_EPS, ALU.mult, ALU.add).then_inc(s_var, 1)
            step(V_.scalar_tensor_tensor(key, edge_int[:, :, P:2 * P], 1.0, fits, ALU.add, ALU.mult))
            dve.wait_ge(s_std, 1)
            V_.reciprocal(rstd, stat[:, 3, :]).then_inc(s_rstd, 1)
            step(V_.tensor_scalar(key, key, 1.0, None, ALU.subtract))
            V_.tensor_copy(srcf, edge_int[:, :, 0:P]).then_inc(s_key, 1)
            dve.wait_ge(s_rstd, 1)
            step(V_.tensor_scalar(hs[:, ACTB:NBP, :], centred[:, ACTB:NBP, :], 0.0, None, ALU.max))
            V_.tensor_tensor(hs[:, ACTB:NBP, :], hs[:, ACTB:NBP, :], wide(rstd[:, ACTB:NBP]), ALU.mult).then_inc(s_hv, 1)
            dve.wait_ge(s_dec, 1)
            g = gate
            step(V_.tensor_scalar(g[:, 4:5], g[:, 3:4], 1e-6, None, ALU.add))
            step(V_.reciprocal(g[:, 5:6], g[:, 4:5]))
            raw = edge_rows[:, :, 2 * P:3 * P]
            as_rows = [a.rearrange("p (c e) -> p c e", c=VC) for a in (decay, sig)]
            step(V_.tensor_scalar(as_rows[0], raw, g[:, 5:6], 0.0, ALU.mult, ALU.max))
            step(V_.tensor_scalar(as_rows[1], raw, g[:, 1:2], g[:, 2:3], ALU.mult, ALU.add))
            V_.tensor_tensor(decay, decay, decay, ALU.mult).then_inc(s_decv, 1)
            dve.wait_ge(s_trc, 2 * TRC)
            dve.wait_ge(s_keyd, 16)
            dve.wait_ge(s_hd, 48)
            for k in range(2):
                V_.tensor_copy(src_ring[:, k, :], src_e[:, G * k:G * k + G]).then_inc(s_src0[k], 1)
            dve.wait_ge(s_dec, 2)
            step(V_.tensor_scalar(sig, sig, 1.0, None, ALU.add))
            step(V_.reciprocal(sig, sig))
            step(V_.tensor_tensor(decay, decay, sig, ALU.mult))
            step(V_.tensor_scalar(ok, decay, FLT_MAX, None, ALU.is_le))
            step(V_.tensor_scalar(sig, decay, -FLT_MAX, None, ALU.is_ge))
            step(V_.tensor_tensor(ok, ok, sig, ALU.mult))
            step(V_.memset(wgt_e[:, :], 0.0))
            V_.copy_predicated(wgt_e[:, :], ok.bitcast(i32), decay).then_inc(s_wgt, 1)
            dve.wait_ge(s_trc, 3 * TRC)

            dve.wait_ge(s_visr, 16)

            def turn0(i):
                for k in range(2):
                    at = bass.ds(16 * i + G * k, G)
                    dve.wait_ge(s_acc0[k], 1 + i)
                    V_.tensor_copy(wgt_ring[:, k, :], wgt_e[:, at]).then_inc(s_wr0[k], 1)
                    V_.tensor_tensor(hot0[:, k, :, :], iota[:, :].unsqueeze(1).to_broadcast([P, G, P]),
                                     slot_e[:, at].unsqueeze(2).to_broadcast([P, G, P]), ALU.is_equal).then_inc(s_hot0[k], 1)
                    dve.wait_ge(s_msg0[k], 1 + i + 1)
                    V_.tensor_copy(src_ring[:, k, :], src_e[:, bass.ds(16 * i + G * k + 2 * G, G)]).then_inc(s_src0[k], 1)

            turn0(0)
            R = slice(None, None, -1)
            dve.wait_ge(s_keys, 48)
            step(V_.tensor_tensor(same, keys[:, 0:LINE + 1], keys[:, 1:LINE + 2], ALU.is_equal))
            step(V_.tensor_scalar(apart, same, BIG, BIG, ALU.mult, ALU.subtract))
            step(V_.tensor_tensor_scan(lead, apart[:, 0:LINE], apart[:, 0:LINE], 0.0, ALU.min, ALU.min))
            step(V_.tensor_tensor_scan(trail[:, R], apart[:, LINE:0:-1], apart[:, LINE:0:-1], 0.0, ALU.min, ALU.min))
            step(V_.tensor_scalar(in_lead, lead, 0.0, None, ALU.is_equal))
            step(V_.tensor_scalar(in_trail, trail, 0.0, None, ALU.is_equal))
            turn0(1)
            dve.wait_ge(s_wload, 16 * WEIGHTS)
            step(V_.tensor_copy(b_part[:, 0, :], b_rows[:, :]))
            step(V_.tensor_tensor(b_left[:, 0, :], b_rows[:, :], b_part[:, 0, :], ALU.subtract))
            step(V_.tensor_copy(b_part[:, 1, :], b_left[:, 0, :]))
            step(V_.tensor_tensor(b_left[:, 1, :], b_left[:, 0, :], b_part[:, 1, :], ALU.subtract))
            V_.tensor_copy(b_part[:, 2, :], b_left[:, 1, :]).then_inc(s_bpart, 1)
            step(V_.tensor_tensor(xs[:, :, :], xs[:, :, :], hs[:, :, :], ALU.add))
            with dve.Fori(2, NG // 2) as i:
                turn0(i)

            at0 = [0]

            def tick(name, u, ins, chained=True):
                at0[0] += 1
                assert dve0[name, u] == at0[0]
                ins.then_inc(s_n0dve, 1)
                if chained:
                    dve.wait_ge(s_n0dve, at0[0])

            for k in range(2):
                dve.wait_ge(s_acc0[k], 1 + NG // 2)
            dve.wait_ge(s_rest, 2 * RESTC)
            dve.wait_ge(s_rout, 16)
            dve.wait_ge(s_aout[0], 16 + 16 * QIT)
            dve.wait_ge(s_aout[1], 16 + 16 * QIT)
            tick("degree", 0, V_.tensor_scalar(degree[:, :], acc[:, STATS:STATS + NB], 1.0, None, ALU.max))
            tick("one", 0, V_.memset(stat[:, 0, :], 1.0))
            tick("rdeg", 0, V_.reciprocal(stat[:, 0, 0:NB], degree[:, :]))

            for u in range(NU):
                (n, sl), k = blocks_of(u), u % 2
                c3, h3 = (a[:, k, 0:n * F].rearrange("p (b f) -> p b f", b=n) for a in (c_u, h2_u))
                m4, v4, d4, r4 = (small_stat[:, k, t, 0:n] for t in range(4))
                dve.wait_ge(s_n0pe, pe0["mix", u])
                tick("x1", u, V_.tensor_tensor(xs[:, sl, :], bank(u)[:, 0:n * F].rearrange("p (b f) -> p b f", b=n), xs[:, sl, :], ALU.add))
                tick("sum", u, V_.tensor_reduce(m4, xs[:, sl, :], AX.X, ALU.add))
                tick("mu", u, V_.tensor_scalar(m4, m4, 1.0 / F, None, ALU.mult))
                tick("centre", u, V_.tensor_tensor(c3, xs[:, sl, :], wide(m4), ALU.subtract))
                if u >= 2:
                    dve.wait_ge(s_n0pe, pe0["h2_t", u - 2])
                tick("relu", u, V_.tensor_scalar(h3, c3, 0.0, None, ALU.max))
                dve.wait_ge(s_n0act, act0["square", u])
                tick("var", u, V_.tensor_scalar(v4, v4, 1.0 / F, LN_EPS, ALU.mult, ALU.add))
                dve.wait_ge(s_n0act, act0["std", u])
                tick("rstd", u, V_.reciprocal(r4, d4))
                tick("h2", u, V_.tensor_tensor(h3, h3, wide(r4), ALU.mult), chained=False)

            dve.wait_ge(s_n0pe, pe0[kv_end(NU - 1)])

            def src_of(g, k):
                V_.tensor_copy(src_ring1[:, k % 4, :], src_e[:, bass.ds(G * g, G)]).then_inc(s_src1[k % 4], 1)

            for k in range(4):
                src_of(k, k)
            for u in range(NU + 1):
                if u < NU:
                    (n, sl), k = blocks_of(u), u % 2
                    if u >= 2:
                        dve.wait_ge(s_n0act, act0["part1", u - 2])
                    dve.wait_ge(s_n0act, act0["part0", u])
                    tick("left1", u, V_.tensor_tensor(q_left[:, 0, k, 0:n, :], q_bank(u)[:, 0:n, 0:F], qs[:, sl, 0, :], ALU.subtract))
                if u >= 1:
                    (n, sl), k = blocks_of(u - 1), (u - 1) % 2
                    if u >= 3:
                        dve.wait_ge(s_n0act, act0["part2", u - 3])
                    dve.wait_ge(s_n0act, act0["part1", u - 1])
                    tick("left2", u - 1, V_.tensor_tensor(q_left[:, 1, k, 0:n, :], q_left[:, 0, k, 0:n, :], qs[:, sl, 1, :], ALU.subtract))

            table_done(dve)
            dve.wait_ge(s_n0act, LAST(act0))

            def hot_of(g, k):
                V_.tensor_tensor(hot_b[:, k % 2, :, :], iota[:, :].unsqueeze(1).to_broadcast([P, G, P]),
                                 slot_e[:, bass.ds(G * g, G)].unsqueeze(2).to_broadcast([P, G, P]),
                                 ALU.is_equal).then_inc(s_hot1[k % 2], 1)

            hot_of(0, 0)
            with dve.Fori(0, NG // 4) as i:
                for k in range(4):
                    g_, p = 4 * i + k, k % 2
                    hot_of(g_ + 1, k + 1)
                    dve.wait_ge(s_vout[p], 16 + 16 * (2 * i + k // 2))
                    dve.wait_ge(s_gath1[k], 16 * G * i + 16 * G)
                    parts = [slice(HALF * j, HALF * (j + 1)) for j in range(2)]
                    for j in range(2):
                        dve.wait_ge(s_edge[j], g_ + 1)
                        V_.tensor_tensor(kv_edge[:, p, parts[j], :, :], kv_src[:, k, parts[j], :, :],
                                         bank(4 + j).rearrange("p (s f) -> p s f", s=HALF).unsqueeze(2).to_broadcast([P, HALF, 2, F]),
                                         ALU.add).then_inc(s_kve[j], 1)
                    for j in range(2):
                        dve.wait_ge(s_kve[j], 2 + g_ + 1)
                        dve.wait_ge(s_q[j], g_ + 1)
                        V_.tensor_tensor(prod[:, j, :].rearrange("p (s f) -> p s f", s=HALF), kv_edge[:, p, parts[j], 0, :],
                                         bank(2 + j).rearrange("p (s f) -> p s f", s=HALF), ALU.mult).then_inc(s_prod[j], 1)
                    src_of(g_ + 4, k)
                    for j in range(2):
                        dve.wait_ge(s_prod[j], 1 + g_ + 1)
                        red = V_.tensor_reduce(score[:, bass.ds(G * g_ + HALF * j, HALF), :],
                                               prod[:, j, :].rearrange("p (s h c) -> p s h c", s=HALF, h=H), AX.X, ALU.add)
                    red.then_inc(s_score, 1)

            def carried_back(h):
                step(V_.tensor_tensor_scan(peak[:, h, R], apart[:, LINE:0:-1], peak[:, h, R], -BIG, ALU.add, ALU.max))

            def across(turn, from_before, from_behind, op, nothing):
                step(V_.memset(ends_t[0:H, 4:6, :], nothing))
                V_.tensor_copy(ends[:, 0, 0:H], peak[:, :, LINE - 1])
                V_.tensor_copy(ends[:, 1, 0:H], peak[:, :, 0])
                V_.tensor_copy(ends[:, 2, 0:H], from_before[:, LINE - 1:LINE].to_broadcast([P, H]))
                V_.tensor_copy(ends[:, 3, 0:H], from_behind[:, 0:1].to_broadcast([P, H])).then_inc(s_ends, 1)
                dve.wait_ge(s_endt, 2 * turn + 1)
                step(V_.tensor_copy(ends_t[0:H, 0:4, 0:P], bank(7)[0:H, :].rearrange("h (n p) -> h n p", n=4)))
                step(V_.tensor_tensor_scan(ends_t[0:H, 4, 1:P + 1], ends_t[0:H, 2, 0:P], ends_t[0:H, 0, 0:P], nothing, *op))
                step(V_.tensor_tensor_scan(ends_t[0:H, 5, P - 1::-1], ends_t[0:H, 3, P - 1::-1], ends_t[0:H, 1, P - 1::-1], nothing, *op))
                V_.memset(ends[:, 5, :], 0.0).then_inc(s_ends, 1)
                dve.wait_ge(s_endt, 2 * turn + 2)
                step(V_.tensor_copy(ends[:, 4, 0:2 * H], bank(7)[:, 0:2 * H]))

            for h in range(H):
                dve.wait_ge(s_line[h], 16)
                if h == 0:
                    step(V_.memset(ends, 0.0))
                step(V_.tensor_tensor_scan(peak[:, h, :], apart[:, 0:LINE], line[:, h, :], -BIG, ALU.add, ALU.max))
                carried_back(h)
            across(0, lead, trail, (ALU.add, ALU.max), -BIG)
            for h in range(H):
                step(V_.scalar_tensor_tensor(peak[:, h, :], lead, ends[:, 4, h:h + 1], peak[:, h, :], ALU.add, ALU.max))
                step(V_.scalar_tensor_tensor(peak[:, h, :], trail, ends[:, 4, H + h:H + h + 1], peak[:, h, :], ALU.add, ALU.max))
                V_.tensor_tensor(line[:, h, :], line[:, h, :], peak[:, h, :], ALU.subtract).then_inc(s_diff, 1)
            for h in range(H):
                dve.wait_ge(s_exp, h + 1)
                step(V_.tensor_tensor_scan(peak[:, h, :], same[:, 0:LINE], line[:, h, :], 0.0, ALU.mult, ALU.add))
                carried_back(h)
            across(1, in_lead, in_trail, (ALU.mult, ALU.add), 0.0)
            for h in range(H):
                total = peak[:, h, :]
                step(V_.scalar_tensor_tensor(total, in_lead, ends[:, 4, h:h + 1], total, ALU.mult, ALU.add))
                step(V_.scalar_tensor_tensor(total, in_trail, ends[:, 4, H + h:H + h + 1], total, ALU.mult, ALU.add))
                step(V_.tensor_scalar(total, total, 1e-16, None, ALU.add))
                step(V_.reciprocal(total, total))
                V_.tensor_tensor(line[:, h, :], line[:, h, :], total, ALU.mult).then_inc(s_share, 1)

            with dve.Fori(0, NG // 4) as i:
                for k in range(4):
                    dve.wait_ge(s_acc1[k], 1 + i)
                    V_.tensor_tensor(hot1[:, k, ACTS:G, :], iota[:, :].unsqueeze(1).to_broadcast([P, G - ACTS, P]),
                                     slot_e[:, bass.ds(32 * i + G * k + ACTS, G - ACTS)].unsqueeze(2).to_broadcast([P, G - ACTS, P]),
                                     ALU.is_equal)
                    dve.wait_ge(s_v[k], 16 * i + 16)
                    dve.wait_ge(s_sharec[k], i + 1)
                    V_.tensor_tensor(msg[:, k, :, :].rearrange("p s (h c) -> p (s h) c", h=H),
                                     v_ring[:, k, :, :].rearrange("p s (h c) -> p (s h) c", h=H),
                                     share[:, k, :, :].rearrange("p s h -> p (s h)").unsqueeze(2).to_broadcast([P, G * H, C]),
                                     ALU.mult).then_inc(s_msg1[k], 1)

            at1 = [0]

            def tock(name, u, ins, chained=True):
                at1[0] += 1
                assert dve1[name, u] == at1[0]
                ins.then_inc(s_n1dve, 1)
                if chained:
                    dve.wait_ge(s_n1dve, at1[0])

            for k in range(4):
                dve.wait_ge(s_acc1[k], 1 + NG // 4)
            for u in range(NU):
                sl = slice(u * U, (u + 1) * U)
                tock("o", u, V_.tensor_tensor(o_u[:, sl, :], bank(u).rearrange("p (b f) -> p b f", b=U), hs[:, sl, :], ALU.add))
            for u in range(NU):
                sl, k = slice(u * U, (u + 1) * U), u % 2
                tock("xo", u, V_.tensor_tensor(xs[:, sl, :], xs[:, sl, :], o_u[:, sl, :], ALU.add))
                dve.wait_ge(s_n1act, act1["gelu2", u])
                tock("y", u, V_.tensor_tensor(xs[:, sl, :], xs[:, sl, :], g_u[:, k, :].rearrange("p (b f) -> p b f", b=U), ALU.add), chained=False)

        @block.scalar
        def _(act):
            for k in range(2):
                act.sem_inc(s_msg0[k], 1)
            act.sem_inc(s_atc, 1)
            S_ = nc.scalar
            for n, a in enumerate((log_scale, filter_w, filter_b)):
                act.dma_start(gate[:, n:n + 1], a.rearrange("(a n) -> a n", a=1).to_broadcast([P, 1])).then_inc(s_gate, 16)
            act.wait_ge(s_gate, 48)
            S_.activation(gate[:, 3:4], gate[:, 0:1], ACT.Exp).then_inc(s_dec, 1)
            S_.activation(gate[:, 6:7], gate[:, 0:1], ACT.Square).then_inc(s_act, 1)
            act.wait_ge(s_mean, 1)
            for b in range(NBP):
                ins = S_.activation(squares[:, b, :], centred[:, b, :], ACT.Square, accum_out=stat[:, 1, b:b + 1])
            ins.then_inc(s_sq, 1)
            act.wait_ge(s_var, 1)
            S_.activation(stat[:, 3, :], stat[:, 1, :], ACT.Sqrt).then_inc(s_std, 1)
            act.wait_ge(s_rstd, 1)
            for b in range(ACTB):
                ins = S_.activation(hs[:, b, :], centred[:, b, :], ACT.Relu, scale=stat[:, 2, b:b + 1])
                if b + 1 in (ACTB // 2, ACTB):
                    ins.then_inc(s_h, 1)
            def edges_out(dest, n):
                for c in range(0, VC, U):
                    w = min(U, VC - c) * P
                    act.wait_ge(s_tr, n + 1)
                    S_.activation(dest[:, c * P:c * P + w], bank(n % 7)[:, 0:w], ACT.Copy).then_inc(s_trc, 1)
                    n += 1

            edges_out(slot_e, 0)
            edges_out(src_e, TRC)
            act.wait_ge(s_decv, 1)
            S_.activation(decay, decay, ACT.Exp, scale=-1.0).then_inc(s_act, 1)
            S_.activation(sig, sig, ACT.Exp, scale=-1.0).then_inc(s_dec, 1)
            act.wait_ge(s_act, 2)
            act.wait_ge(s_visr, 16)
            for n in range(RESTC):
                w = min(4, REST - 4 * n) * P
                act.wait_ge(s_rest, 2 * n + 1)
                S_.activation(rest_t[:, 4 * n * P:4 * n * P + w], aside[0:A, 0:w], ACT.Copy).then_inc(s_rest, 1)
            edges_out(wgt_e, 2 * TRC)

            act.wait_ge(s_keyd, 16)

            def messages(i, k):
                act.wait_ge(s_gath0[k], 16 * G * i + 16 * G)
                act.wait_ge(s_wr0[k], i + 1)
                act.wait_ge(s_acc0[k], 1 + i)
                act.sem_inc(s_hop_act, 1)
                for m in range(G):
                    ins = S_.activation(h_wgt[:, k, m, :], h_src[:, k, m, :], ACT.Copy, scale=wgt_ring[:, k, m:m + 1])
                ins.then_inc(s_msg0[k], 1)

            with act.Fori(0, QIT) as i:
                for k in range(2):
                    messages(i, k)
                    act.wait_ge(s_atr, 1 + 2 * i + k + 1)
                    act.wait_ge(s_aout[k], 16 + 16 * i)
                    act.sem_inc(s_hop_act, 1)
                    for j in range(4):
                        ins = S_.activation(attr_t[:, k, :].rearrange("c (t r j) -> c t r j", t=G, j=4)[:, :, :, j],
                                            aside[32 * j:32 * j + A, 0:2 * P].rearrange("c (t r) -> c t r", t=G), ACT.Copy)
                    ins.then_inc(s_atc, 1)
            for i in range(QIT, NG // 2):
                for k in range(2):
                    messages(i, k)

            at0 = [0]

            def tick(name, u, ins):
                at0[0] += 1
                assert act0[name, u] == at0[0]
                ins.then_inc(s_n0act, 1)

            def mean_of(u):
                n, _ = blocks_of(u)
                for c in range(n):
                    ins = S_.activation(mean_in[:, u * U + c, :], bank(u)[:, c * P:(c + 1) * P], ACT.Copy, scale=stat[:, 0, u * U + c:u * U + c + 1])
                tick("mean", u, ins)

            def side_of(u):
                n, _ = blocks_of(u)
                act.wait_ge(s_n0pe, pe0["mean_t", u])
                tick("side", u, S_.activation(side[:, u % 2, 0:n * P], bank(u)[:, 0:n * P], ACT.Copy))

            def square_std(u):
                (n, _), k = blocks_of(u), u % 2
                act.wait_ge(s_n0dve, dve0["centre", u])
                for c in range(n):
                    ins = S_.activation(sq_u[:, k, c * F:(c + 1) * F], c_u[:, k, c * F:(c + 1) * F], ACT.Square, accum_out=small_stat[:, k, 1, c:c + 1])
                tick("square", u, ins)
                act.wait_ge(s_n0dve, dve0["var", u])
                tick("std", u, S_.activation(small_stat[:, k, 2, 0:n], small_stat[:, k, 1, 0:n], ACT.Sqrt))

            S_.activation(gate[:, 7:8], gate[:, 6:7], ACT.Sqrt)
            act.wait_ge(s_n0dve, dve0["rdeg", 0])
            for u in range(min(2, NU)):
                mean_of(u)
            for u in range(min(2, NU)):
                side_of(u)
            if NU > 2:
                mean_of(2)
            square_std(0)
            for u in range(NU):
                (n, sl), k = blocks_of(u), u % 2
                act.wait_ge(s_n0pe, pe0["h2_t", u])
                tick("h2_side", u, S_.activation(h2t[:, u, 0:n * P], bank(u)[:, 0:n * P], ACT.Copy))
                if u + 2 < NU:
                    side_of(u + 2)
                if u + 1 < NU:
                    square_std(u + 1)
                if u >= 2:
                    act.wait_ge(s_kvd[k], 16 * (u // 2))
                for j in range(2):
                    m = max(0, min(2, n - 2 * j))
                    if m:
                        act.wait_ge(s_n0pe, pe0[f"kv{j}", u])
                        tick(f"kv{j}", u, S_.activation(kv_u[:, k, 2 * j:2 * j + m, :].rearrange("p c f -> p (c f)"),
                                                        (bank(7), bank(u))[j][:, 0:m * 2 * F], ACT.Copy))
                if u + 3 < NU:
                    mean_of(u + 3)
            for u in range(NU + 2):
                if u < NU:
                    n, sl = blocks_of(u)
                    act.wait_ge(s_n0pe, pe0["q", u])
                    tick("skip", u, S_.activation(hs[:, sl, :], q_bank(u)[:, 0:n, F:2 * F], ACT.Copy))
                    tick("part0", u, S_.activation(qs[:, sl, 0, :], q_bank(u)[:, 0:n, 0:F], ACT.Copy))
                for t in (1, 2):
                    if 0 <= u - t < NU:
                        n, sl = blocks_of(u - t)
                        act.wait_ge(s_n0dve, dve0[f"left{t}", u - t])
                        tick(f"part{t}", u - t, S_.activation(qs[:, sl, t, :], q_left[:, t - 1, (u - t) % 2, 0:n, :], ACT.Copy))

            act.wait_ge(s_n0act, LAST(act0))
            table_done(act)
            with act.Fori(0, NG // 2) as i:
                for k in range(2):
                    for j in range(2):
                        act.wait_ge(s_hott[j], 2 * i + k + 1)
                        act.sem_inc(s_hop_act, 1)
                        S_.activation(hot_t[:, k, HALF * j:HALF * (j + 1), :],
                                      bank(j).bitcast(bf16)[:, 0:HALF * P].rearrange("p (s e) -> p s e", s=HALF), ACT.Copy).then_inc(s_hotc[j], 1)
                    act.wait_ge(s_kve[1], 2 + 2 * i + k + 1)
                    act.sem_inc(s_hop_act, 1)
                    act.dma_start(v_d[bass.ds(2 * i + k, 1)].rearrange("g p s f -> p (g s) f"), kv_edge[:, k, :, 1, :]).then_inc(s_vout[k], 16)

            act.wait_ge(s_score, NG)
            for k in range(2):
                act.wait_ge(s_vout[k], 16 + 16 * (NG // 2))
            for n in range(0, NCH, U):
                w = min(U, NCH - n)
                act.wait_ge(s_lt, min(n + U, NCH))
                S_.activation(line_rows[:, n:n + w, :], bank(n // U)[:, 0:w * P].rearrange("p (c e) -> p c e", c=w), ACT.Copy).then_inc(s_lc, 1)
            line_in(act, 1)
            for h in range(H):
                act.wait_ge(s_diff, h + 1)
                S_.activation(line[:, h, :], line[:, h, :], ACT.Exp, scale=float(C) ** -0.5).then_inc(s_exp, 1)

            with act.Fori(0, NG // 4) as i:
                for k in range(4):
                    act.wait_ge(s_acc1[k], 1 + i)
                    act.sem_inc(s_hop_act, 1)
                    S_.activation(neg_slot[:, k, 0:ACTS], slot_e[:, bass.ds(32 * i + G * k, ACTS)], ACT.Copy, scale=-1.0).then_inc(s_neg[k], 1)
                    act.wait_ge(s_neg[k], i + 1)
                    for m in range(ACTS):
                        ins = S_.activation(hot1[:, k, m, :], iota[:, :], ACT.Square, bias=neg_slot[:, k, m:m + 1])
                    ins.then_inc(s_sqr[k], 1)
                    act.wait_ge(s_sqr[k], i + 1)
                    S_.activation(hot1[:, k, 0:ACTS, :], hot1[:, k, 0:ACTS, :], ACT.Relu, scale=-2.0, bias=1.0).then_inc(s_hota[k], 1)
                    act.wait_ge(s_shart, i + 1)
                    act.sem_inc(s_hop_act, 1)
                    S_.activation(share[:, k, :, :], bank(7)[:, G * H * k:G * H * (k + 1)].rearrange("p (s h) -> p s h", s=G),
                                  ACT.Copy).then_inc(s_sharec[k], 1)

            at1 = [0]

            def tock(name, u, ins):
                at1[0] += 1
                assert act1[name, u] == at1[0]
                ins.then_inc(s_n1act, 1)

            def o_side(u):
                act.wait_ge(s_n1pe, pe1["o_t", u])
                tock("ot", u, S_.activation(ot_u[:, u % 2, :], bank(u), ACT.Copy))

            o_side(0)
            for u in range(NU):
                k = u % 2
                if u + 1 < NU:
                    o_side(u + 1)
                act.wait_ge(s_n1pe, pe1["w1", u])
                tock("gelu1", u, S_.activation(ht_u[:, k, :], bank(u), ACT.Gelu_apprx_tanh, bias=b1_s[:, 0:1]))
                act.wait_ge(s_n1pe, pe1["w2", u])
                if u >= 2:
                    act.wait_ge(s_n1dve, dve1["y", u - 2])
                tock("gelu2", u, S_.activation(g_u[:, k, :], bank(u), ACT.Gelu_apprx_tanh))

        @block.tensor
        def _(pe):
            for k in range(2):
                pe.sem_inc(s_acc0[k], 1)
            pe.sem_inc(s_atr, 1)
            for k in range(4):
                pe.sem_inc(s_acc1[k], 1)
            T_ = nc.tensor
            pe.wait_ge(s_const, 10)
            pe.wait_ge(s_cnt, 1)
            T_.matmul(bank(7)[:, 0:NB + 1], ones[0:PD, :], small[0:PD, 1, 0:NB + 1], start=True, stop=True).then_inc(s_bound, 1)
            pe.wait_ge(s_key, 1)
            n = 0

            def rows_to_edges(rows, n):
                for c in range(0, VC, U):
                    if n >= 7:
                        pe.wait_ge(s_trc, n - 6)
                    for m in range(min(U, VC - c)):
                        ins = T_.transpose(bank(n % 7)[:, m * P:(m + 1) * P], rows[:, c + m, :], ident[:, :])
                    ins.then_inc(s_tr, 1)
                    n += 1

            rows_to_edges(rel, 0)
            rows_to_edges(srcf, TRC)

            pe.wait_ge(s_rin, 33)
            for n in range(RESTC):
                if n:
                    pe.wait_ge(s_rest, 2 * n)
                for m in range(min(4, REST - 4 * n)):
                    ins = T_.transpose(aside[0:A, m * P:(m + 1) * P], rest_in[:, 4 * n + m, :], ident[:, :])
                ins.then_inc(s_rest, 1)
            pe.wait_ge(s_rest, 2 * RESTC)
            pe.wait_ge(s_wgt, 1)
            rows_to_edges(wgt_rows, 2 * TRC)
            pe.wait_ge(s_trc, 3 * TRC)

            def open_blocks():
                for u in range(-(-(STATS + NB) // BANK)):
                    T_.matmul(bank(u), zeros[:, 0:P], zeros[:, :], start=True, stop=True)

            open_blocks()
            pe.wait_ge(s_visr, 16)

            def sum0(i, k):
                blocks = load_blocks(pe, 16 * i + G * k)
                pe.wait_ge(s_hot0[k], i + 1)
                for m, b in enumerate(blocks):
                    T_.matmul(acc[:, bass.ds(b + STATS, 1)], hot0[:, k, m, :], ones[:, 0:1], start=False, stop=True, skip_group_check=True)
                pe.wait_ge(s_msg0[k], 1 + i + 1)
                for m, b in enumerate(blocks):
                    ins = T_.matmul(acc[:, bass.ds(b * P, P)], hot0[:, k, m, :], h_wgt[:, k, m, :], start=False, stop=True, skip_group_check=True)
                ins.then_inc(s_acc0[k], 1)

            with pe.Fori(0, QIT) as i:
                for k in range(2):
                    pe.wait_ge(s_ain[k], 16 * i + 16)
                    pe.wait_ge(s_atc, 1 + 2 * i + k)
                    for q in range(2):
                        ins = T_.transpose(aside[:, q * P:(q + 1) * P], attr_in[:, k, q, :], ident[:, :])
                    ins.then_inc(s_atr, 1)
                    sum0(i, k)
            for i in range(QIT, NG // 2):
                for k in range(2):
                    sum0(i, k)

            pe.wait_ge(s_wload, 16 * WEIGHTS)
            pe.wait_ge(s_b3, 48)
            at0 = [0]

            def tick(name, u, ins):
                at0[0] += 1
                assert pe0[name, u] == at0[0]
                ins.then_inc(s_n0pe, 1)

            def mean_t(u):
                pe.wait_ge(s_n0act, act0["mean", u])
                for c in range(blocks_of(u)[0]):
                    ins = T_.transpose(bank(u)[:, c * P:(c + 1) * P], mean_in[:, u * U + c, :], ident[:, :])
                tick("mean_t", u, ins)

            def mix(u):
                pe.wait_ge(s_n0act, act0["side", u])
                for c in range(blocks_of(u)[0]):
                    ins = T_.matmul(bank(u)[:, c * F:(c + 1) * F], side[:, u % 2, c * P:(c + 1) * P], w_mix_s[:, :], start=True, stop=True)
                tick("mix", u, ins)

            def project(dest, u, c, cols):
                T_.matmul(dest, ones3[:, :], b_3[:, cols], start=True, stop=False)
                return T_.matmul(dest, h2t[:, u, c * P:(c + 1) * P], w_kvqs[:, cols], start=False, stop=True)

            for u in range(min(2, NU)):
                mean_t(u)
            for u in range(min(2, NU)):
                mix(u)
            for u in range(NU):
                n, _ = blocks_of(u)
                pe.wait_ge(s_n0dve, dve0["h2", u])
                for c in range(n):
                    ins = T_.transpose(bank(u)[:, c * P:(c + 1) * P], h2_u[:, u % 2, c * P:(c + 1) * P], ident[:, :])
                tick("h2_t", u, ins)
                if u + 2 < NU:
                    mean_t(u + 2)
                pe.wait_ge(s_n0act, act0["h2_side", u])
                if u:
                    pe.wait_ge(s_n0act, act0["kv0", u - 1])
                for j in range(2):
                    for c in range(max(0, min(2, n - 2 * j))):
                        ins = project((bank(7), bank(u))[j][:, c * 2 * F:(c + 1) * 2 * F], u, 2 * j + c, slice(0, 2 * F))
                    if n > 2 * j:
                        tick(f"kv{j}", u, ins)
                if u + 2 < NU:
                    mix(u + 2)
            for u in range(NU):
                if u < 3:
                    pe.wait_ge(s_n0act, act0[kv_end(min(2 * u + 1, NU - 1))])
                else:
                    pe.wait_ge(s_n0act, act0["part0", u - 3])
                    pe.wait_ge(s_n0dve, dve0["left1", u - 3])
                for c in range(blocks_of(u)[0]):
                    ins = project(q_bank(u)[:, c, :], u, c, slice(2 * F, 4 * F))
                tick("q", u, ins)

            pe.wait_ge(s_n0act, LAST(act0))
            pe.wait_ge(s_n0dve, LAST(dve0))
            with pe.Fori(0, NG // 2) as i:
                for k in range(2):
                    g_ = 2 * i + k
                    blocks = load_blocks(pe, 16 * i + G * k)
                    pe.wait_ge(s_hot1[k], i + 1)
                    for j in range(2):
                        for m in range(HALF):
                            ins = T_.transpose(bank(j).bitcast(bf16)[:, m * P:(m + 1) * P], hot_b[:, k, HALF * j + m, :], identb[:, :])
                        ins.then_inc(s_hott[j], 1)
                    pe.wait_ge(s_attr1[k], 16 * G * i + 16 * G)
                    for j in range(2):
                        pe.wait_ge(s_kve[j], 2 + g_)
                        for m in range(HALF):
                            ins = T_.matmul(bank(4 + j)[:, m * F:(m + 1) * F], attr_g[:, k, HALF * j + m, :], we_s[:, :], start=True, stop=True)
                        ins.then_inc(s_edge[j], 1)
                    for j in range(2):
                        pe.wait_ge(s_hotc[j], g_ + 1)
                        pe.wait_ge(s_prod[j], 1 + g_)
                        for m in range(HALF):
                            b = blocks[HALF * j + m]
                            for t in range(3):
                                ins = T_.matmul(bank(2 + j)[:, m * F:(m + 1) * F], hot_t[:, k, HALF * j + m, :],
                                                qs[:, bass.ds(b, 1), t, :].rearrange("p b f -> p (b f)"), start=t == 0, stop=t == 2)
                        ins.then_inc(s_q[j], 1)

            for n in range(NCH):
                if n < 2 * U:
                    pe.wait_ge(s_score, 4 * (n + 1))
                elif n == 2 * U:
                    pe.wait_ge(s_score, NG)
                T_.transpose(bank(n // U)[:, (n % U) * P:(n % U + 1) * P], score[:, CHUNK * n:CHUNK * (n + 1), :].rearrange("p v h -> p (v h)"), ident[:, :]).then_inc(s_lt, 1)
            for turn in range(2):
                pe.wait_ge(s_ends, 2 * turn + 1)
                for n in range(4):
                    ins = T_.transpose(bank(7)[0:H, n * P:(n + 1) * P], ends[:, n, 0:H], ident[:, :])
                ins.then_inc(s_endt, 1)
                pe.wait_ge(s_ends, 2 * turn + 2)
                T_.transpose(bank(7)[:, 0:H], ends_t[0:H, 4, 0:P], ident[0:H, 0:H])
                T_.transpose(bank(7)[:, H:2 * H], ends_t[0:H, 5, 1:P + 1], ident[0:H, 0:H]).then_inc(s_endt, 1)
            pe.wait_ge(s_lc, -(-NCH // U))
            open_blocks()
            pe.wait_ge(s_shareb, 16 * H)
            T_.transpose(bank(7)[:, 0:P], line_rows[:, 0, :], ident[:, :]).then_inc(s_shart, 1)

            with pe.Fori(0, NG // 4) as i:
                for k in range(4):
                    if k == 2:
                        pe.wait_ge(s_sharec[3], i + 1)
                        pe.wait_ge(s_chunk, i + 1)
                        T_.transpose(bank(7)[:, 0:P], chunk_rows, ident[:, :]).then_inc(s_shart, 1)
                    pe.wait_ge(s_hota[k], i + 1)
                    pe.wait_ge(s_msg1[k], 1 + i + 1)
                    for m, b in enumerate(load_blocks(pe, 32 * i + G * k)):
                        ins = T_.matmul(acc[:, bass.ds(b * P, P)], hot1[:, k, m, :], msg[:, k, m, :], start=False, stop=True, skip_group_check=True)
                    ins.then_inc(s_acc1[k], 1)

            at1 = [0]

            def tock(name, u, ins):
                at1[0] += 1
                assert pe1[name, u] == at1[0]
                ins.then_inc(s_n1pe, 1)

            def o_t(u):
                pe.wait_ge(s_n1dve, dve1["o", u])
                for c in range(U):
                    ins = T_.transpose(bank(u)[:, c * P:(c + 1) * P], o_u[:, u * U + c, :], ident[:, :])
                tock("o_t", u, ins)

            o_t(0)
            for u in range(NU):
                k = u % 2
                if u + 1 < NU:
                    o_t(u + 1)
                pe.wait_ge(s_n1act, act1["ot", u])
                tock("w1", u, T_.matmul(bank(u), w1_s[:, :], ot_u[:, k, :], start=True, stop=True))
                pe.wait_ge(s_n1act, act1["gelu1", u])
                for c in range(U):
                    T_.matmul(bank(u)[:, c * F:(c + 1) * F], ones3[:, :], b_3[:, 4 * F:5 * F], start=True, stop=False)
                    ins = T_.matmul(bank(u)[:, c * F:(c + 1) * F], ht_u[:, k, c * P:(c + 1) * P], w2_s[:, :], start=False, stop=True)
                tock("w2", u, ins)


_INS = ['x', 'src', 'dst', 'edge_attr_32', 'edge_weight', 'L0_gnn_W_mix', 'L0_gnn_log_scale', 'L0_gnn_filter_w',
        'L0_gnn_filter_b', 'L1_gnn_Wq', 'L1_gnn_bq', 'L1_gnn_Wk', 'L1_gnn_bk', 'L1_gnn_Wv', 'L1_gnn_bv', 'L1_gnn_We',
        'L1_gnn_Wskip', 'L1_gnn_bskip', 'L1_gnn_W1', 'L1_gnn_b1', 'L1_gnn_W2', 'L1_gnn_b2']


def kernel(**inputs):
    import numpy as np
    import concourse.bacc as bacc
    from concourse.bass_utils import run_bass_kernel_spmd

    nc = bacc.Bacc("TRN2", target_bir_lowering=False, num_devices=1)
    arrays, args = {}, []
    for name in _INS:
        a = np.ascontiguousarray(inputs[name])
        a = a.reshape(1) if a.ndim == 0 else a
        arrays[f"in_{name}"] = a
        args.append(nc.dram_tensor(f"in_{name}", a.shape, mybir.dt.from_np(a.dtype), kind="ExternalInput").ap())
    shape = tuple(inputs['x'].shape)
    out = nc.dram_tensor("out", shape, mybir.dt.float32, kind="ExternalOutput").ap()
    gnn_kernel(nc, *args, out)
    r = run_bass_kernel_spmd(nc, [arrays], core_ids=[0])
    return r.results[0]["out"]
```
